# Optimizing a Trainium2 kernel written in Bass

```python
import numpy as np
import jax
import jax.numpy as jnp

def _softmax(x, axis=-1):
    return jax.nn.softmax(x, axis=axis)

def _gelu(x):
    return jax.nn.gelu(x, approximate=True)

def _silu(x):
    return jax.nn.silu(x)

def _sigmoid(x):
    return jax.nn.sigmoid(x)

def _layernorm(x, axis=-1, eps=1e-05):
    m = jnp.mean(x, axis=axis, keepdims=True)
    v = jnp.var(x, axis=axis, keepdims=True)
    return (x - m) / jnp.sqrt(v + eps)

def _scatter_add(tgt, idx, src, axis=0):
    return tgt.at[idx].add(src)

def _segment_sum(src, seg, n):
    return jax.ops.segment_sum(src, seg, n)
kernel_name = 'mk_seq_postln_d1_jaxref_r4_720aa2'

def setup_inputs(seed: int=0):
    np.random.seed(seed)
    _w = jnp.asarray

    def _L0_attn_setup():
        import math
        import jax, jax.numpy as jnp
        import numpy as np

        def _expmap0(u):
            u0 = u[..., :1]
            us = u[..., 1:]
            mink = -u0 * u0 + jnp.sum(us * us, axis=-1, keepdims=True)
            nomin = jnp.sqrt(jnp.maximum(mink, 1e-08))
            r = jnp.sinh(nomin) * u / nomin
            space = r[..., 1:]
            time = jnp.sqrt(1.0 + jnp.sum(space * space, axis=-1, keepdims=True))
            return jnp.concatenate([time, space], axis=-1)
        key = jax.random.key(seed)
        B, T, E, H = (2, 256, 256, 16)
        ks = jax.random.split(key, 8)
        s = 0.02
        return {'x': jax.random.normal(ks[0], (B, T, E), jnp.float32), 'Wqkv': jax.random.normal(ks[1], (3 * E, E), jnp.float32) * s, 'bqkv': jnp.zeros((3 * E,), jnp.float32), 'Wout': jax.random.normal(ks[2], (E, E), jnp.float32) * s, 'bout': jnp.zeros((E,), jnp.float32), 'Wimp': jax.random.normal(ks[3], (1, E), jnp.float32) * s, 'bimp': jnp.zeros((1,), jnp.float32), 'Walpha': jax.random.normal(ks[4], (H, E), jnp.float32) * s, 'balpha': jnp.zeros((H,), jnp.float32), 'spike_threshold': jnp.asarray(0.5, jnp.float32), 'log_k': jnp.full((H,), 0.54, jnp.float32), 'qk_scale': jnp.asarray(0.1, jnp.float32)}
    _L0_attn_in = _L0_attn_setup()

    def _L0_ffn_setup():
        import jax, jax.numpy as jnp
        import numpy as np
        B, S, D, H, E, F, K = (2, 256, 256, 16, 8, 1024, 2)
        EPS = 1e-05

        def _layernorm(x, g, b):
            mu = jnp.mean(x, axis=-1, keepdims=True)
            var = jnp.mean(jnp.square(x - mu), axis=-1, keepdims=True)
            return (x - mu) * jax.lax.rsqrt(var + EPS) * g + b
        key = jax.random.key(seed)
        ks = jax.random.split(key, 12)
        w = lambda k, shape: jax.random.normal(k, shape, dtype=jnp.float32) * 0.02
        return {'x': jax.random.normal(ks[0], (B, S, D), dtype=jnp.float32), 'ln1_g': jnp.ones((D,), jnp.float32), 'ln1_b': jnp.zeros((D,), jnp.float32), 'ln2_g': jnp.ones((D,), jnp.float32), 'ln2_b': jnp.zeros((D,), jnp.float32), 'Wq': w(ks[1], (D, D)), 'Wk': w(ks[2], (D, D)), 'Wv': w(ks[3], (D, D)), 'Wo': w(ks[4], (D, D)), 'Wg': w(ks[5], (D, E)), 'W1': w(ks[6], (E, D, F)), 'b1': jnp.zeros((E, F), jnp.float32), 'W2': w(ks[7], (E, F, D)), 'b2': jnp.zeros((E, D), jnp.float32)}
    _L0_ffn_in = _L0_ffn_setup()
    _d = {'L0_attn_x': _L0_attn_in['x'], 'L0_attn_Wqkv': _L0_attn_in['Wqkv'], 'L0_attn_bqkv': _L0_attn_in['bqkv'], 'L0_attn_Wout': _L0_attn_in['Wout'], 'L0_attn_bout': _L0_attn_in['bout'], 'L0_attn_Wimp': _L0_attn_in['Wimp'], 'L0_attn_bimp': _L0_attn_in['bimp'], 'L0_attn_Walpha': _L0_attn_in['Walpha'], 'L0_attn_balpha': _L0_attn_in['balpha'], 'L0_attn_spike_threshold': _L0_attn_in['spike_threshold'], 'L0_attn_log_k': _L0_attn_in['log_k'], 'L0_attn_qk_scale': _L0_attn_in['qk_scale'], 'L0_ffn_ln1_g': _L0_ffn_in['ln1_g'], 'L0_ffn_ln1_b': _L0_ffn_in['ln1_b'], 'L0_ffn_ln2_g': _L0_ffn_in['ln2_g'], 'L0_ffn_ln2_b': _L0_ffn_in['ln2_b'], 'L0_ffn_Wq': _L0_ffn_in['Wq'], 'L0_ffn_Wk': _L0_ffn_in['Wk'], 'L0_ffn_Wv': _L0_ffn_in['Wv'], 'L0_ffn_Wo': _L0_ffn_in['Wo'], 'L0_ffn_Wg': _L0_ffn_in['Wg'], 'L0_ffn_W1': _L0_ffn_in['W1'], 'L0_ffn_b1': _L0_ffn_in['b1'], 'L0_ffn_W2': _L0_ffn_in['W2'], 'L0_ffn_b2': _L0_ffn_in['b2']}
    _x0 = _d['L0_attn_x']
    _d['L0_attn_x'] = jax.random.normal(jax.random.fold_in(jax.random.key(seed), 1), (8, 512, 256), dtype=_x0.dtype)
    del _x0
    return _d

def reference(L0_attn_x, L0_attn_Wqkv, L0_attn_bqkv, L0_attn_Wout, L0_attn_bout, L0_attn_Wimp, L0_attn_bimp, L0_attn_Walpha, L0_attn_balpha, L0_attn_spike_threshold, L0_attn_log_k, L0_attn_qk_scale, L0_ffn_ln1_g, L0_ffn_ln1_b, L0_ffn_ln2_g, L0_ffn_ln2_b, L0_ffn_Wq, L0_ffn_Wk, L0_ffn_Wv, L0_ffn_Wo, L0_ffn_Wg, L0_ffn_W1, L0_ffn_b1, L0_ffn_W2, L0_ffn_b2):

    def _L0_attn_ref(x, Wqkv, bqkv, Wout, bout, Wimp, bimp, Walpha, balpha, spike_threshold, log_k, qk_scale):
        import math
        import jax, jax.numpy as jnp
        import numpy as np

        def _expmap0(u):
            u0 = u[..., :1]
            us = u[..., 1:]
            mink = -u0 * u0 + jnp.sum(us * us, axis=-1, keepdims=True)
            nomin = jnp.sqrt(jnp.maximum(mink, 1e-08))
            r = jnp.sinh(nomin) * u / nomin
            space = r[..., 1:]
            time = jnp.sqrt(1.0 + jnp.sum(space * space, axis=-1, keepdims=True))
            return jnp.concatenate([time, space], axis=-1)
        B, T, C = x.shape
        H = log_k.shape[0]
        D = C // H
        importance = jax.nn.sigmoid(x @ Wimp.T + bimp)
        spikes = (importance > spike_threshold).astype(x.dtype)
        spike_mask = spikes.reshape(B, 1, T, 1)
        alpha = jax.nn.sigmoid(x @ Walpha.T + balpha)
        alpha = jnp.transpose(alpha, (0, 2, 1))[..., None]
        qkv = (x @ Wqkv.T + bqkv).reshape(B, T, 3, H, D)
        q = jnp.transpose(qkv[:, :, 0], (0, 2, 1, 3))
        k = jnp.transpose(qkv[:, :, 1], (0, 2, 1, 3))
        v = jnp.transpose(qkv[:, :, 2], (0, 2, 1, 3))
        scores_euclid = jnp.einsum('bhtd,bhsd->bhts', q, k) / math.sqrt(D)
        safe_scale = jax.nn.sigmoid(qk_scale) * 1.5
        qn = q / jnp.maximum(jnp.linalg.norm(q, axis=-1, keepdims=True), 1e-12) * safe_scale
        kn = k / jnp.maximum(jnp.linalg.norm(k, axis=-1, keepdims=True), 1e-12) * safe_scale
        q_hyp = _expmap0(qn)
        k_hyp = _expmap0(kn)
        inner = -jnp.einsum('bhti,bhsi->bhts', q_hyp[..., :1], k_hyp[..., :1]) + jnp.einsum('bhtd,bhsd->bhts', q_hyp[..., 1:], k_hyp[..., 1:])
        curv_k = (jax.nn.softplus(log_k) + 1e-06).reshape(1, H, 1, 1)
        mdot = jnp.maximum(-inner, 1.0 + 1e-06)
        dist = jnp.arccosh(mdot)
        scores_hyper = -(dist * dist) / curv_k
        scores = (1.0 - alpha) * scores_euclid + alpha * scores_hyper
        causal = jnp.tril(jnp.ones((T, T), bool))
        scores = jnp.where(causal[None, None], scores, -jnp.inf)
        attn = jax.nn.softmax(scores, axis=-1) * spike_mask
        y = jnp.einsum('bhts,bhsd->bhtd', attn, v)
        y = jnp.transpose(y, (0, 2, 1, 3)).reshape(B, T, C)
        return y @ Wout.T + bout

    def _L0_ffn_ref(x, ln1_g, ln1_b, ln2_g, ln2_b, Wq, Wk, Wv, Wo, Wg, W1, b1, W2, b2):
        import jax, jax.numpy as jnp
        import numpy as np
        B, S, D, H, E, F, K = (2, 256, 256, 16, 8, 1024, 2)
        EPS = 1e-05

        def _layernorm(x, g, b):
            mu = jnp.mean(x, axis=-1, keepdims=True)
            var = jnp.mean(jnp.square(x - mu), axis=-1, keepdims=True)
            return (x - mu) * jax.lax.rsqrt(var + EPS) * g + b
        Bb, Ss, Dd = x.shape
        Dh = Dd // H
        h = _layernorm(x, ln1_g, ln1_b)
        q = (h @ Wq).reshape(Bb, Ss, H, Dh)
        k = (h @ Wk).reshape(Bb, Ss, H, Dh)
        v = (h @ Wv).reshape(Bb, Ss, H, Dh)
        scores = jnp.einsum('bqhd,bkhd->bhqk', q, k) / jnp.sqrt(jnp.float32(Dh))
        attn = jax.nn.softmax(scores, axis=-1)
        ctx = jnp.einsum('bhqk,bkhd->bqhd', attn, v).reshape(Bb, Ss, Dd)
        x = x + ctx @ Wo
        m = _layernorm(x, ln2_g, ln2_b)
        xt = m.reshape(-1, Dd)
        T = xt.shape[0]
        probs = jax.nn.softmax(xt @ Wg, axis=-1)
        wts, idx = jax.lax.top_k(probs, K)
        wts = wts / jnp.sum(wts, axis=-1, keepdims=True)
        h1 = jax.nn.gelu(jnp.einsum('td,edf->etf', xt, W1) + b1[:, None, :])
        ye = jnp.einsum('etf,efd->etd', h1, W2) + b2[:, None, :]
        sel = ye[idx, jnp.arange(T)[:, None], :]
        moe_out = jnp.sum(wts[..., None] * sel, axis=1).reshape(Bb, Ss, Dd)
        return x + moe_out
    x = L0_attn_x
    x = _layernorm(x + _L0_attn_ref(x, L0_attn_Wqkv, L0_attn_bqkv, L0_attn_Wout, L0_attn_bout, L0_attn_Wimp, L0_attn_bimp, L0_attn_Walpha, L0_attn_balpha, L0_attn_spike_threshold, L0_attn_log_k, L0_attn_qk_scale), axis=-1)
    x = _layernorm(x + _L0_ffn_ref(x, L0_ffn_ln1_g, L0_ffn_ln1_b, L0_ffn_ln2_g, L0_ffn_ln2_b, L0_ffn_Wq, L0_ffn_Wk, L0_ffn_Wv, L0_ffn_Wo, L0_ffn_Wg, L0_ffn_W1, L0_ffn_b1, L0_ffn_W2, L0_ffn_b2), axis=-1)
    return x

_drawn_inputs = setup_inputs


def setup_inputs(seed=0):
    import zlib

    import numpy as np

    out = dict(_drawn_inputs(seed))
    spreads = {'L0_attn_bqkv': (0.0, 0.336),
     'L0_attn_bout': (0.0, 0.1),
     'L0_attn_balpha': (0.0, 0.8),
     'L0_attn_log_k': (0.5400000214576721, 0.6),
     'L0_ffn_ln1_g': (1.0, 0.6),
     'L0_ffn_ln1_b': (0.0, 0.8),
     'L0_ffn_ln2_g': (1.0, 0.6),
     'L0_ffn_ln2_b': (0.0, 1.568),
     'L0_ffn_b1': (0.0, 0.621),
     'L0_ffn_b2': (0.0, 0.62)}
    factors = {'L0_attn_Wqkv': 6.058,
     'L0_attn_Wimp': 3.079,
     'L0_attn_Walpha': 8.0,
     'L0_ffn_Wq': 8.0,
     'L0_ffn_Wk': 8.0,
     'L0_ffn_Wv': 5.623,
     'L0_ffn_Wo': 5.742}
    for name, (base, spread) in spreads.items():
        noise = np.random.default_rng([zlib.crc32(name.encode()), seed]).standard_normal(out[name].shape)
        drawn = base * np.exp(spread * noise) if base else spread * noise
        out[name] = jnp.asarray(drawn.astype(out[name].dtype))
    for name, factor in factors.items():
        out[name] = (out[name] * factor).astype(out[name].dtype)
    return out
```

```python
from contextlib import ExitStack
from math import factorial

import concourse.bass as bass
from concourse import mybir

ALU = mybir.AluOpType
ACT = mybir.ActivationFunctionType
AX = mybir.AxisListType
F32 = mybir.dt.float32
F16 = mybir.dt.float16
BF16 = mybir.dt.bfloat16

P = 128
EPS = 1e-5
MASKED = 1e30
SINH = [1.0 / factorial(2 * k + 1) for k in range(8)]


def build(nc, a, out):
    x_d = a["L0_attn_x"]
    B, T, C = x_d.shape
    H = a["L0_attn_log_k"].shape[0]
    D = C // H
    E, _, F = a["L0_ffn_W1"].shape
    NT = T // P
    N = B * NT
    CH = C // P
    FC = F // P
    HPC = H // CH
    G = 4
    NG = H // G
    R3 = 3 * D
    QKW = 2 * C
    VAI = C + H + 1
    WCOL = QKW + VAI
    W = [P * (i + 1) for i in range(NT)]
    OFF = {3: 0, 2: 512, 0: 896, 1: 1024}
    SW = sum(W)
    REGIONS = [[3], [2, 0], [1]]
    assert D == 16 and NT == 4 and T == 512 and H == 16 and C == 256 and SW == 1280

    x_t = x_d.rearrange("b (t p) c -> b p t c", p=P)
    out_t = out.rearrange("b (t p) c -> b p t c", p=P)

    SLOTS = 2 * N + E
    x2_d = nc.dram_tensor("x2_scratch", [B, P, NT, C], F32, kind="Internal").ap()

    xs_d = nc.dram_tensor("rows_scratch", [SLOTS, P, C], F32, kind="Internal").ap()
    ys_d = nc.dram_tensor("results_scratch", [SLOTS, P, C], F32, kind="Internal").ap()

    with ExitStack() as top:
        def sem(name):
            return top.enter_context(nc.semaphore(name))

        def sb(ctx, name, shape, dt=F32):
            return ctx.enter_context(nc.sbuf_tensor(name, shape, dt))

        X = sb(top, "X", [P, N, C])
        ident = sb(top, "ident", [P, P])
        identb = sb(top, "identb", [P, P], BF16)
        neg1 = sb(top, "neg1", [P, 1])
        epsc = sb(top, "epsc", [P, 1])
        mis = top.enter_context(nc.psum_tensor("misc", [P, 512], F32))

        setup_pool = sem("setup_pool")
        passed = sem("passed")

        with ExitStack() as ctx:
            WT = sb(ctx, "WT", [P, CH, WCOL])
            WOT = sb(ctx, "WOT", [P, CH, C])
            mask = sb(ctx, "mask", [P, P], BF16)
            bias = sb(ctx, "bias", [P, WCOL])
            bout = sb(ctx, "bout", [P, C])
            thr = sb(ctx, "thr", [P, 1])
            s2 = sb(ctx, "s2", [P, 1])
            rcurv = sb(ctx, "rcurv", [P, H])
            XI = sb(ctx, "XI", [P, NT, C])
            xT = sb(ctx, "xT", [P, 2, CH, P])
            QK = sb(ctx, "QK", [P, 2, QKW])
            AI = sb(ctx, "AI", [P, 2, H + 1])
            V = sb(ctx, "V", [P, H, D + 1])
            SQ = sb(ctx, "SQ", [P, 2 * H, D])
            st = sb(ctx, "st", [P, 10, 2 * H])
            stat = sb(ctx, "stat", [P, 5 * H])
            root = sb(ctx, "root", [P, NT, 5 * H])
            QE = sb(ctx, "QE", [P, C])
            HY = sb(ctx, "HY", [P, 2 * H, D])
            spk = sb(ctx, "spk", [P, NT])
            HI = sb(ctx, "HI", [P, 4 * CH, T], F16)
            LO = sb(ctx, "LO", [P, 4 * CH, T], F16)
            STG = sb(ctx, "STG", [P, NG, 4, 2, T], F16)
            MC = sb(ctx, "MC", [P, 2, G, SW])
            TT = sb(ctx, "TT", [P, 2, G, SW])
            PH = sb(ctx, "PH", [P, 2, SW], F16)
            PL = sb(ctx, "PL", [P, 2, SW], F16)
            VH = sb(ctx, "VH", [P, NT, H, D + 1], F16)
            VL = sb(ctx, "VL", [P, NT, H, D + 1], F16)
            mn = sb(ctx, "mn", [P, 2, G, NT])
            Y = QK[:, :, :].rearrange("p s (u c) -> p (s u) c", c=C)
            YT = SQ[:, H:2 * H, :].rearrange("p h d -> p (h d)").rearrange("p (k t) -> p k t", k=CH)
            z = SQ[:, 0:H, :].rearrange("p h d -> p (h d)")
            rin = sb(ctx, "rin", [P, NT, G])
            bst = sb(ctx, "bst", [P, 6])
            mv = sb(ctx, "mv", [P, 2])
            sd = sb(ctx, "sd", [P, 2])
            mP = [ctx.enter_context(nc.psum_tensor(f"mP{i}", [P, 512], F32)) for i in range(2)]
            SeP = [ctx.enter_context(nc.psum_tensor(f"SeP{i}", [P, 512], F32)) for i in range(2)]
            PTP = [ctx.enter_context(nc.psum_tensor(f"PTP{i}", [P, 512], F32)) for i in range(2)]
            avP = ctx.enter_context(nc.psum_tensor("avP", [P, NT, G, D + 1], F32))

            WL = TT[:, 0, :, :].rearrange("p g w -> p (g w)")
            WQR = WL[:, 0:6 * C].rearrange("p (r c) -> p r c", r=6)
            WOR = WL[:, 6 * C:8 * C].rearrange("p (r c) -> p r c", r=2)
            WAR = WL[:, 8 * C:9 * C]
            lk = st[:, 0, 0:H]

            a_w_loaded = sem("a_w_loaded")
            a_c_loaded = sem("a_c_loaded")
            wt_full = sem("wt_full")
            wt_free = sem("wt_free")
            sc_exp = sem("sc_exp")
            sc_one = sem("sc_one")
            sc_ln = sem("sc_ln")
            sc_done = sem("sc_done")
            dve_a0 = sem("dve_a0")

            with nc.Block() as block:
                @block.sync
                def _(sp):
                    sp.dma_start(WQR, a["L0_attn_Wqkv"].rearrange("(r p) c -> p r c", p=P)).then_inc(a_w_loaded, 16)
                    sp.dma_start(WOR, a["L0_attn_Wout"].rearrange("(r p) c -> p r c", p=P)).then_inc(a_w_loaded, 16)
                    sp.dma_start(WAR[0:H, :], a["L0_attn_Walpha"]).then_inc(a_w_loaded, 16)
                    sp.dma_start(WAR[H:H + 1, :], a["L0_attn_Wimp"]).then_inc(a_w_loaded, 16)

                @block.scalar
                def _(act):
                    act.dma_start(lk, a["L0_attn_log_k"].partition_broadcast(P)).then_inc(a_c_loaded, 16)
                    act.dma_start(s2[:, :], a["L0_attn_qk_scale"].partition_broadcast(P)).then_inc(a_c_loaded, 16)
                    act.dma_start(thr[:, :], a["L0_attn_spike_threshold"].partition_broadcast(P)).then_inc(a_c_loaded, 16)
                    act.dma_start(bias[:, 0:3 * C], a["L0_attn_bqkv"].partition_broadcast(P)).then_inc(a_c_loaded, 16)
                    act.dma_start(bias[:, 3 * C:3 * C + H], a["L0_attn_balpha"].partition_broadcast(P)).then_inc(a_c_loaded, 16)
                    act.dma_start(bias[:, 3 * C + H:], a["L0_attn_bimp"].partition_broadcast(P)).then_inc(a_c_loaded, 16)
                    act.dma_start(bout[:, :], a["L0_attn_bout"].partition_broadcast(P)).then_inc(a_c_loaded, 16)
                    act.wait_ge(sc_one, 1)
                    act.activation(st[:, 2, 0:H], st[:, 1, 0:H], ACT.Exp).then_inc(sc_exp, 1)
                    act.activation(sd[:, 0:1], s2[:, :], ACT.Exp, scale=-1.0).then_inc(sc_exp, 1)
                    act.wait_ge(sc_one, 2)
                    act.activation(st[:, 4, 0:H], st[:, 3, 0:H], ACT.Ln).then_inc(sc_ln, 1)

                @block.gpsimd
                def _(pool):
                    pool.memset(ident[:, :], 0.0).then_inc(setup_pool, 1)
                    pool.memset(mask[:, :], 0.0).then_inc(setup_pool, 1)
                    pool.memset(neg1[:, :], -1.0).then_inc(setup_pool, 1)
                    pool.memset(epsc[:, :], EPS).then_inc(setup_pool, 1)
                    pool.memset(V[:, :, :], 1.0).then_inc(setup_pool, 1)
                    pool.wait_ge(setup_pool, 5)
                    pool.affine_select(out=ident[:, :], in_=ident[:, :], compare_op=ALU.not_equal, fill=1.0,
                                       base=0, pattern=[[-1, P]], channel_multiplier=1).then_inc(setup_pool, 1)
                    pool.affine_select(out=mask[:, :], in_=mask[:, :], compare_op=ALU.is_ge, fill=MASKED,
                                       base=0, pattern=[[-1, P]], channel_multiplier=1).then_inc(setup_pool, 1)
                    pool.wait_ge(setup_pool, 7)
                    pool.tensor_copy(identb[:, :], ident[:, :]).then_inc(setup_pool, 1)

                @block.tensor
                def _(pe):
                    pe.wait_ge(setup_pool, 8)
                    pe.wait_ge(a_w_loaded, 64)
                    n = 0
                    for r in range(8):
                        src = WQR[:, r, :] if r < 6 else WOR[:, r - 6, :]
                        if n >= 1:
                            pe.wait_ge(wt_free, n)
                        for k in range(CH):
                            mm = pe.transpose(mis[:, k * P:(k + 1) * P], src[:, k * P:(k + 1) * P], ident[:, :])
                        mm.then_inc(wt_full, 1)
                        n += 1
                    pe.wait_ge(wt_free, n)
                    for k in range(CH):
                        mm = pe.transpose(mis[:, k * 32:k * 32 + H + 1], WAR[0:H + 1, k * P:(k + 1) * P],
                                          ident[0:H + 1, 0:H + 1])
                    mm.then_inc(wt_full, 1)

                @block.vector
                def _(dve):
                    step = [0]

                    def chain(ins):
                        step[0] += 1
                        ins.then_inc(dve_a0, 1)
                        dve.wait_ge(dve_a0, step[0])

                    dve.wait_ge(a_c_loaded, 112)
                    chain(dve.tensor_scalar(st[:, 9, 0:H], lk, -1.0, None, ALU.mult))
                    chain(dve.tensor_tensor(st[:, 8, 0:H], lk, st[:, 9, 0:H], ALU.max))
                    dve.tensor_scalar(st[:, 1, 0:H], st[:, 8, 0:H], -1.0, None, ALU.mult).then_inc(sc_one, 1)
                    dve.wait_ge(sc_exp, 2)
                    dve.tensor_scalar(st[:, 3, 0:H], st[:, 2, 0:H], 1.0, None, ALU.add).then_inc(sc_one, 1)
                    chain(dve.tensor_scalar(sd[:, 1:2], sd[:, 0:1], 1.0, None, ALU.add))
                    chain(dve.reciprocal(sd[:, 0:1], sd[:, 1:2]))
                    chain(dve.tensor_scalar(sd[:, 1:2], sd[:, 0:1], 1.5, None, ALU.mult))
                    chain(dve.tensor_tensor(s2[:, :], sd[:, 1:2], sd[:, 1:2], ALU.mult))
                    dve.wait_ge(sc_ln, 1)
                    chain(dve.tensor_scalar(st[:, 5, 0:H], lk, 0.0, None, ALU.max))
                    chain(dve.tensor_tensor(st[:, 6, 0:H], st[:, 5, 0:H], st[:, 4, 0:H], ALU.add))
                    chain(dve.tensor_scalar(st[:, 7, 0:H], st[:, 6, 0:H], 1e-6, None, ALU.add))
                    chain(dve.reciprocal(rcurv[:, :], st[:, 7, 0:H]))
                    for r in range(8):
                        dve.wait_ge(wt_full, r + 1)
                        dst = WT[:, :, r * P:(r + 1) * P] if r < 6 else WOT[:, :, (r - 6) * P:(r - 5) * P]
                        dve.tensor_copy(dst, mis[:, 0:C].rearrange("p (k c) -> p k c", k=CH)).then_inc(wt_free, 1)
                    dve.wait_ge(wt_full, 9)
                    dve.tensor_copy(WT[:, :, 3 * C:WCOL],
                                    mis[:, 0:32 * CH].rearrange("p (k c) -> p k c", k=CH)[:, :, 0:H + 1]).then_inc(wt_free, 1)

            x_loaded = sem("x_loaded")
            x_used = sem("x_used")
            misc_full = sem("misc_full")
            misc_free = sem("misc_free")
            xT_ready = sem("xT_ready")
            ai_ready = sem("ai_ready")
            qk_ready = sem("qk_ready")
            ea_ready = sem("ea_ready")
            sq_ready = sem("sq_ready")
            qs_ready = sem("qs_ready")
            qe_ready = sem("qe_ready")
            stat_ready = sem("stat_ready")
            root_ready = sem("root_ready")
            space_ready = sem("space_ready")
            hy_ready = sem("hy_ready")
            hi_ready = sem("hi_ready")
            lo_ready = sem("lo_ready")
            stage_ready = [sem(f"stage_ready{s}") for s in range(NG)]
            m_full = sem("m_full")
            m_free = sem("m_free")
            msq_ready = sem("msq_ready")
            rt_ready = sem("rt_ready")
            sum_ready = sem("sum_ready")
            ln_ready = sem("ln_ready")
            hyp_ready = sem("hyp_ready")
            se_full = sem("se_full")
            comb_ready = sem("comb_ready")
            p_ready = sem("p_ready")
            pt_full = sem("pt_full")
            ph_ready = sem("ph_ready")
            pt_ready = sem("pt_ready")
            vh_ready = sem("vh_ready")
            vl_ready = sem("vl_ready")
            av_full = sem("av_full")
            av_tile = sem("av_tile")
            y_ready = sem("y_ready")
            yT_ready = sem("yT_ready")
            sd_ready = sem("sd_ready")
            var_ready = sem("var_ready")
            dve_a = sem("dve_a")
            SD = 16 * 5 * G
            SE = H * NT
            MU = 7 * NT

            def use_pre(b, i, k):
                return b * MU + (5 * i + k)

            def use_post(b, i, k):
                return b * MU + (5 * NT + 2 * i + k)

            with nc.Block() as block:
                @block.sync
                def _(sp):
                    with sp.Fori(0, B) as b:
                        sp.wait_ge(x_used, b + 1)
                        sp.dma_start(XI[:, :, :], x_t[bass.ds(b, 1)].rearrange("a p t c -> (a p) t c")).then_inc(x_loaded, 16)
                        sp.wait_ge(hi_ready, 2 * NT * b + 2 * NT)
                        sp.wait_ge(lo_ready, 2 * NT * b + 2 * NT)
                        for g in range(NG):
                            slot, c = g, g // 2
                            sp.wait_ge(se_full, b * (H * NT) + G * NT * (g + 1))
                            for j in range(G):
                                par, s = j % 2, j // 2
                                src = 16 * ((G * g + j) % HPC)
                                dst = 64 * par
                                sp.dma_start(STG[dst:dst + D, slot, :, s, :],
                                             HI[src:src + D, c:4 * CH:2, :]).then_inc(stage_ready[slot], 16)
                                for jj, planes in [(1, (HI, LO)), (2, (LO, HI))]:
                                    dst = 64 * par + D * jj
                                    for qk in range(2):
                                        sp.dma_start(STG[dst:dst + D, slot, qk:4:2, s, :],
                                                     planes[qk][src:src + D, 2 * qk + c:4 * CH:4, :]).then_inc(stage_ready[slot], 16)

                @block.gpsimd
                def _(pool):
                    with pool.Fori(0, B) as b:
                        for i in range(NT):
                            pool.wait_ge(qk_ready, NT * b + (i + 1))
                            pool.tensor_tensor(SQ[:, :, :].rearrange("p h d -> p (h d)"), QK[:, i % 2, :], QK[:, i % 2, :],
                                               ALU.mult).then_inc(sq_ready, 1)
                            q3 = QK[:, i % 2, :].rearrange("p (h d) -> p h d", d=D)
                            pool.wait_ge(ai_ready, NT * b + (i + 1))
                            pool.sem_inc(passed, 1)
                            pool.tensor_copy(VH[:, i, :, :], V[:, :, :]).then_inc(vh_ready, 1)
                            pool.wait_ge(vh_ready, NT * b + (i + 1))
                            pool.tensor_tensor(VL[:, i, :, :], V[:, :, :], VH[:, i, :, :], ALU.subtract).then_inc(vl_ready, 1)
                            pool.wait_ge(qs_ready, NT * b + (i + 1))
                            pool.tensor_tensor(QE[:, :].rearrange("p (h d) -> p h d", d=D), q3[:, 0:H, :],
                                               st[:, 9, 0:H].unsqueeze(2).broadcast_to([P, H, D]), ALU.mult).then_inc(qe_ready, 1)
                            pool.wait_ge(root_ready, NT * b + (i + 1))
                            pool.tensor_tensor(HY[:, :, :], q3,
                                               root[:, i, 0:2 * H].unsqueeze(2).broadcast_to([P, 2 * H, D]),
                                               ALU.mult).then_inc(space_ready, 1)

                        def square(g):
                            for j in range(G):
                                pool.wait_ge(m_free, b * (3 * H) + (2 + 3 * (G * g + j + 1)))
                                if g >= 2:
                                    pool.wait_ge(pt_full, b * (H * NT) + NT * (G * (g - 2) + j + 1))
                                pool.tensor_tensor(TT[:, g % 2, j, :], MC[:, g % 2, j, :], MC[:, g % 2, j, :],
                                                   ALU.mult).then_inc(msq_ready, 1)

                        def add(g):
                            pool.wait_ge(rt_ready, NG * b + (g + 1))
                            for j in range(G):
                                pool.tensor_tensor(TT[:, g % 2, j, :], MC[:, g % 2, j, :], TT[:, g % 2, j, :],
                                                   ALU.add).then_inc(sum_ready, 1)

                        for g in range(NG):
                            square(g)
                            add(g)

                @block.scalar
                def _(act):
                    with act.Fori(0, B) as b:
                        for i in range(NT):
                            act.wait_ge(misc_full, use_pre(b, i, 0) + 1)
                            act.activation(xT[:, i % 2, :, :].rearrange("p k t -> p (k t)"), mis[:, 0:C], ACT.Copy).then_inc(misc_free, 1)
                            act.wait_ge(ai_ready, NT * b + (i + 1))
                            act.activation(AI[:, 1, :], AI[:, 0, :], ACT.Exp, scale=-1.0).then_inc(ea_ready, 1)
                            act.wait_ge(stat_ready, NT * b + (i + 1))
                            act.activation(root[:, i, :], stat[:, :], ACT.Sqrt).then_inc(root_ready, 1)
                            for r in range(2):
                                act.wait_ge(misc_full, use_pre(b, i, 3 + r) + 1)
                                act.activation(HI[:, 4 * r:4 * r + 4, i * P:(i + 1) * P],
                                               mis[:, :].rearrange("p (k t) -> p k t", k=4), ACT.Copy).then_inc(hi_ready, 1)

                        def roots(g):
                            act.wait_ge(msq_ready, b * H + G * (g + 1))
                            w = TT[:, g % 2, :, :].rearrange("p j w -> p (j w)")
                            act.activation(w, w, ACT.Sqrt, bias=neg1[:, :]).then_inc(rt_ready, 1)

                        def logs(g):
                            for j in range(G):
                                act.wait_ge(sum_ready, b * H + (G * g + j + 1))
                                w = TT[:, g % 2, j, :]
                                act.activation(w, w, ACT.Ln).then_inc(ln_ready, 1)
                                act.wait_ge(ln_ready, b * H + (G * g + j + 1))
                                for i in range(NT):
                                    w = TT[:, g % 2, j, OFF[i]:OFF[i] + W[i]]
                                    h = G * g + j
                                    ins = act.activation(w, w, ACT.Square, scale=root[:, i, 4 * H + h:4 * H + h + 1])
                                ins.then_inc(hyp_ready, 1)

                        def exps(g):
                            for j in range(G):
                                for i in range(NT):
                                    act.wait_ge(comb_ready, b * (H * NT) + (NT * (G * g + j) + i + 3))
                                    w = TT[:, g % 2, j, OFF[i]:OFF[i] + W[i]]
                                    act.activation(w, w, ACT.Exp, bias=mn[:, g % 2, j, i:i + 1], scale=-1.0).then_inc(p_ready, 1)

                        for g in range(NG + 1):
                            if g < NG:
                                roots(g)
                            if g >= 1:
                                exps(g - 1)
                            if g < NG:
                                logs(g)

                        for i in range(NT):
                            act.wait_ge(misc_full, use_post(b, i, 0) + 1)
                            act.activation(YT[:, :, :].rearrange("p k t -> p (k t)"), mis[:, 0:C], ACT.Copy).then_inc(misc_free, 1)
                            act.wait_ge(var_ready, NT * b + (i + 1))
                            act.activation(sd[:, 0:1], mv[:, 1:2], ACT.Sqrt, bias=epsc[:, :]).then_inc(sd_ready, 1)

                @block.tensor
                def _(pe):
                    with pe.Fori(0, B) as b:
                        for i in range(NT):
                            if i == 0:
                                pe.wait_ge(x_loaded, 16 * b + 16)
                            pe.wait_ge(misc_free, use_pre(b, i, 0) + 1)
                            for k in range(CH):
                                mm = pe.transpose(mis[:, k * P:(k + 1) * P], XI[:, i, k * P:(k + 1) * P], ident[:, :])
                            mm.then_inc(misc_full, 1)
                            for part, (c0, c1) in enumerate([(0, QKW), (QKW, WCOL)]):
                                pe.wait_ge(misc_free, use_pre(b, i, 1 + part) + 1)
                                for k in range(CH):
                                    mm = pe.matmul(mis[:, 0:c1 - c0], xT[:, i % 2, k, :], WT[:, k, c0:c1],
                                                   start=(k == 0), stop=(k == CH - 1))
                                mm.then_inc(misc_full, 1)
                            pe.wait_ge(misc_free, use_pre(b, i, 3) + 1)
                            pe.wait_ge(qe_ready, NT * b + (i + 1))
                            for k in range(CH):
                                pe.transpose(mis[:, k * P:(k + 1) * P], QE[:, k * P:(k + 1) * P], ident[:, :])
                                mm = pe.transpose(mis[:, (2 + k) * P:(3 + k) * P], QK[:, i % 2, C + k * P:C + (k + 1) * P], ident[:, :])
                            mm.then_inc(misc_full, 1)
                            pe.wait_ge(misc_free, use_pre(b, i, 4) + 1)
                            pe.wait_ge(hy_ready, NT * b + (i + 1))
                            hy = HY[:, :, :].rearrange("p h d -> p (h d)")
                            for k in range(4):
                                mm = pe.transpose(mis[:, k * P:(k + 1) * P], hy[:, k * P:(k + 1) * P], ident[:, :])
                            mm.then_inc(misc_full, 1)

                        def op(g, j, o, lo, hi):
                            return STG[64 * (j % 2):64 * (j % 2) + R3, g, o, j // 2, lo:hi]

                        def inner(g, j):
                            if j == 0:
                                pe.wait_ge(stage_ready[g], b * SD + SD)
                            for r, tiles in enumerate(REGIONS):
                                rc = 3 * (G * g + j) + r
                                pe.wait_ge(m_free, b * (3 * H) + (rc + 1))
                                at = 0
                                for i in tiles:
                                    mm = pe.matmul(mP[rc % 2][:, at:at + W[i]], op(g, j, 2, i * P, (i + 1) * P),
                                                   op(g, j, 3, 0, W[i]), start=True, stop=True)
                                    at += W[i]
                                mm.then_inc(m_full, 1)

                        def euclid(g):
                            for j in range(G):
                                for i in range(NT):
                                    tc = NT * (G * g + j) + i
                                    pe.wait_ge(comb_ready, b * (H * NT) + (tc + 1))
                                    pe.matmul(SeP[tc % 2][:, 0:W[i]], op(g, j, 0, i * P, (i + 1) * P),
                                              op(g, j, 1, 0, W[i]), start=True, stop=False)
                                    mm = pe.matmul(SeP[tc % 2][:, i * P:W[i]], identb[:, :], mask[:, :], start=False, stop=True)
                                    mm.then_inc(se_full, 1)

                        def turn(g, j, i):
                            tc = NT * (G * g + j) + i
                            pe.wait_ge(p_ready, b * (H * NT) + (tc + 1))
                            pe.wait_ge(pt_ready, b * (H * NT) + (tc + 1))
                            for k in range(i + 1):
                                mm = pe.transpose(PTP[tc % 2][:, k * P:(k + 1) * P],
                                                  TT[:, g % 2, j, OFF[i] + k * P:OFF[i] + (k + 1) * P], ident[:, :])
                            mm.then_inc(pt_full, 1)

                        def product(g, j, i):
                            tc = NT * (G * g + j) + i
                            pe.wait_ge(pt_ready, b * (H * NT) + (tc + 3))
                            if j == 0 and i == 0:
                                pe.wait_ge(y_ready, NG * b + (g + 1))
                                pe.wait_ge(vl_ready, NT * b + NT)
                            for k in range(i + 1):
                                blk = slice(OFF[i] + k * P, OFF[i] + (k + 1) * P)
                                pe.matmul(avP[:, i, j, :], PH[:, j % 2, blk], VH[:, k, G * g + j, :], start=(k == 0), stop=False)
                                pe.matmul(avP[:, i, j, :], PH[:, j % 2, blk], VL[:, k, G * g + j, :], start=False, stop=False)
                                mm = pe.matmul(avP[:, i, j, :], PL[:, j % 2, blk], VH[:, k, G * g + j, :], start=False, stop=(k == i))
                            mm.then_inc(av_tile, 1)

                        def outputs(g):
                            order = [(j, i) for j in range(G) for i in range(NT)]
                            for n, (j, i) in enumerate(order):
                                turn(g, j, i)
                                if n >= 2:
                                    product(g, *order[n - 2])
                                if i == NT - 1 and g + 2 < NG:
                                    inner(g + 2, j)
                            product(g, *order[-2])
                            product(g, *order[-1])

                        for g in range(2):
                            for j in range(G):
                                inner(g, j)
                        for g in range(NG):
                            euclid(g)
                            outputs(g)

                        for i in range(NT):
                            pe.wait_ge(misc_free, use_post(b, i, 0) + 1)
                            if i == 0:
                                pe.wait_ge(y_ready, NG * b + (NG + 1))
                            for k in range(CH):
                                mm = pe.transpose(mis[:, k * P:(k + 1) * P], Y[:, i, k * P:(k + 1) * P], ident[:, :])
                            mm.then_inc(misc_full, 1)
                            pe.wait_ge(misc_free, use_post(b, i, 1) + 1)
                            for k in range(CH):
                                mm = pe.matmul(mis[:, 0:C], YT[:, k, :], WOT[:, k, :], start=(k == 0), stop=(k == CH - 1))
                            mm.then_inc(misc_full, 1)

                @block.vector
                def _(dve):
                    dve.sem_inc(x_used, 1)
                    dve.sem_inc(misc_free, 1)
                    dve.sem_inc(m_free, 2)
                    dve.sem_inc(comb_ready, 2)
                    dve.sem_inc(pt_ready, 2)
                    dve.sem_inc(se_full, SE)
                    dve.sem_inc(y_ready, 1)
                    steps = NT * 25 + NG * 2 + NT * 5
                    with dve.Fori(0, B) as b:
                        step = [0]

                        def chain(ins):
                            step[0] += 1
                            ins.then_inc(dve_a, 1)
                            dve.wait_ge(dve_a, steps * b + step[0])

                        for i in range(NT):
                            dve.wait_ge(misc_full, use_pre(b, i, 1) + 1)
                            dve.tensor_tensor(QK[:, i % 2, :], mis[:, :], bias[:, 0:QKW], ALU.add).then_inc(qk_ready, 1)
                            dve.wait_ge(qk_ready, NT * b + (i + 1))
                            dve.sem_inc(misc_free, 1)
                            dve.wait_ge(misc_full, use_pre(b, i, 2) + 1)
                            if i >= 1:
                                dve.wait_ge(vl_ready, NT * b + i)
                            dve.tensor_tensor(V[:, :, 0:D], mis[:, 0:C].rearrange("p (h d) -> p h d", d=D),
                                              bias[:, QKW:QKW + C].rearrange("p (h d) -> p h d", d=D), ALU.add)
                            dve.tensor_tensor(AI[:, 0, :], mis[:, C:VAI], bias[:, QKW + C:WCOL], ALU.add).then_inc(ai_ready, 1)
                            dve.wait_ge(ai_ready, NT * b + (i + 1))
                            dve.sem_inc(misc_free, 1)
                            SS, SQ0, A, MK, G1, R2, Q, F2 = (st[:, k, :] for k in (0, 1, 2, 3, 4, 5, 6, 7))
                            dve.wait_ge(sq_ready, NT * b + (i + 1))
                            chain(dve.tensor_reduce(SS, SQ[:, :, :], AX.X, ALU.add))
                            chain(dve.tensor_copy(SQ0, SQ[:, :, 0]))
                            chain(dve.tensor_scalar(A, SS, 1e-24, None, ALU.max))
                            chain(dve.reciprocal(G1, A))
                            chain(dve.tensor_scalar(R2, G1, s2[:, 0:1], None, ALU.mult))
                            chain(dve.scalar_tensor_tensor(A, SQ0, -2.0, SS, ALU.mult, ALU.add))
                            chain(dve.tensor_tensor(G1, A, R2, ALU.mult))
                            chain(dve.tensor_scalar(MK, G1, 1e-8, None, ALU.max))
                            chain(dve.tensor_scalar(Q, MK, SINH[7], None, ALU.mult))
                            for k in range(6, 0, -1):
                                chain(dve.scalar_tensor_tensor(Q, Q, SINH[k], MK, ALU.add, ALU.mult))
                            chain(dve.tensor_scalar(G1, Q, 1.0, None, ALU.add))
                            chain(dve.tensor_tensor(A, G1, G1, ALU.mult))
                            chain(dve.tensor_tensor(stat[:, 0:2 * H], A, R2, ALU.mult))
                            chain(dve.tensor_tensor(Q, SS, SQ0, ALU.subtract))
                            chain(dve.tensor_tensor(A, Q, stat[:, 0:2 * H], ALU.mult))
                            chain(dve.tensor_scalar(stat[:, 2 * H:4 * H], A, 1.0, None, ALU.add))
                            dve.wait_ge(ea_ready, NT * b + (i + 1))
                            al = st[:, 8, 0:H + 1]
                            chain(dve.tensor_scalar(AI[:, 0, :], AI[:, 1, :], 1.0, None, ALU.add))
                            chain(dve.reciprocal(al, AI[:, 0, :]))
                            dve.tensor_scalar(st[:, 9, 0:H], al[:, 0:H], 0.25, -0.25, ALU.mult, ALU.add).then_inc(qs_ready, 1)
                            chain(dve.tensor_scalar(spk[:, i:i + 1], al[:, H:H + 1], thr[:, 0:1], None, ALU.is_gt))
                            dve.tensor_tensor(stat[:, 4 * H:5 * H], al[:, 0:H], rcurv[:, :], ALU.mult).then_inc(stat_ready, 1)
                            dve.wait_ge(space_ready, NT * b + (i + 1))
                            chain(dve.tensor_scalar(HY[:, 0:H, 0], root[:, i, 2 * H:3 * H], -1.0, None, ALU.mult))
                            dve.tensor_copy(HY[:, H:2 * H, 0], root[:, i, 3 * H:4 * H]).then_inc(hy_ready, 1)
                            for r in range(2):
                                dve.wait_ge(hi_ready, 2 * NT * b + (2 * i + r + 1))
                                dve.tensor_tensor(LO[:, 4 * r:4 * r + 4, i * P:(i + 1) * P],
                                                  mis[:, :].rearrange("p (k t) -> p k t", k=4),
                                                  HI[:, 4 * r:4 * r + 4, i * P:(i + 1) * P], ALU.subtract).then_inc(lo_ready, 1)
                                dve.wait_ge(lo_ready, 2 * NT * b + (2 * i + r + 1))
                                dve.sem_inc(misc_free, 1)

                        def clamps(g, j):
                            for r, tiles in enumerate(REGIONS):
                                rc = 3 * (G * g + j) + r
                                w = sum(W[i] for i in tiles)
                                dve.wait_ge(m_full, b * (3 * H) + (rc + 1))
                                if r == 0 and j == 0 and g >= 2:
                                    dve.wait_ge(sum_ready, b * H + G * (g - 1))
                                at = OFF[tiles[0]]
                                dve.tensor_scalar(MC[:, g % 2, j, at:at + w], mP[rc % 2][:, 0:w], -1.0, 1.0 + 1e-6,
                                                  ALU.mult, ALU.max).then_inc(m_free, 1)

                        def combines(g):
                            for j in range(G):
                                dve.wait_ge(hyp_ready, b * H + (G * g + j + 1))
                                for i in range(NT):
                                    tc = NT * (G * g + j) + i
                                    dve.wait_ge(se_full, b * (H * NT) + (SE + tc + 1))
                                    w = TT[:, g % 2, j, OFF[i]:OFF[i] + W[i]]
                                    dve.sem_inc(passed, 1)
                                    dve.tensor_tensor_reduce(out=w, in0=SeP[tc % 2][:, 0:W[i]], in1=w, scale=1.0, scalar=3e38,
                                                             op0=ALU.add, op1=ALU.min,
                                                             accum_out=mn[:, g % 2, j, i:i + 1]).then_inc(comb_ready, 1)

                        def copies(g, j):
                            for i in range(NT):
                                tc = NT * (G * g + j) + i
                                dve.wait_ge(pt_full, b * (H * NT) + (tc + 1))
                                if tc >= 2 * NT:
                                    dve.wait_ge(av_tile, b * (H * NT) + (tc - 2 * NT + 1))
                                seg = slice(OFF[i], OFF[i] + W[i])
                                dve.tensor_copy(PH[:, j % 2, seg], PTP[tc % 2][:, 0:W[i]]).then_inc(ph_ready, 1)
                                dve.wait_ge(ph_ready, b * (H * NT) + (tc + 1))
                                dve.tensor_tensor(PL[:, j % 2, seg], PTP[tc % 2][:, 0:W[i]], PH[:, j % 2, seg],
                                                  ALU.subtract).then_inc(pt_ready, 1)

                        def normalise(g):
                            dve.wait_ge(av_tile, b * (H * NT) + NT * G * (g + 1))
                            chain(dve.reciprocal(rin[:, :, :], avP[:, :, :, D]))
                            chain(dve.tensor_tensor(rin[:, :, :], rin[:, :, :],
                                                    spk[:, :].unsqueeze(2).broadcast_to([P, NT, G]), ALU.mult))
                            dve.tensor_tensor(Y[:, :, G * g * D:G * (g + 1) * D].rearrange("p i (j d) -> p i j d", d=D),
                                              avP[:, :, :, 0:D], rin[:, :, :].unsqueeze(3).broadcast_to([P, NT, G, D]),
                                              ALU.mult).then_inc(y_ready, 1)

                        for g in range(2):
                            for j in range(G):
                                clamps(g, j)
                        for g in range(NG):
                            combines(g)
                            for j in range(G):
                                copies(g, j)
                                if g + 2 < NG:
                                    clamps(g + 2, j)
                            normalise(g)

                        for i in range(NT):
                            dve.wait_ge(misc_full, use_post(b, i, 1) + 1)
                            chain(dve.tensor_tensor(z[:, :], mis[:, 0:C], XI[:, i, :], ALU.add))
                            dve.sem_inc(misc_free, 1)
                            chain(dve.tensor_tensor(z[:, :], z[:, :], bout[:, :], ALU.add))
                            if i == NT - 1:
                                dve.sem_inc(x_used, 1)
                            chain(dve.bn_stats(bst[:, :], z[:, :]))
                            dve.sem_inc(passed, 1)
                            dve.bn_aggr(mv[:, :], bst[:, :]).then_inc(var_ready, 1)
                            dve.wait_ge(var_ready, NT * b + (i + 1))
                            dve.wait_ge(sd_ready, NT * b + (i + 1))
                            chain(dve.reciprocal(sd[:, 1:2], sd[:, 0:1]))
                            chain(dve.tensor_scalar(X[:, bass.ds(NT * b + i, 1), :].rearrange("p a c -> p (a c)"), z[:, :],
                                                    mv[:, 0:1], sd[:, 1:2], ALU.subtract, ALU.mult))
                        assert step[0] == steps, step[0]

        W1S = sb(top, "W1S", [P, E, CH, F])
        LG = sb(top, "LG", [P, N, E])
        w1_loaded = sem("w1_loaded")
        x2_stored = sem("x2_stored")
        with ExitStack() as ctx:
            WQ = sb(ctx, "WQ", [P, CH, 3 * C])
            WO = sb(ctx, "WO", [P, CH, C])
            WG = sb(ctx, "WG", [P, CH, E])
            lng = sb(ctx, "lng", [P, 4, C])
            XN = sb(ctx, "XN", [P, 2, C])
            hT = sb(ctx, "hT", [P, CH, T])
            HB = sb(ctx, "HB", [P, C])
            VH = sb(ctx, "VHb", [P, NT, H, D + 1], F16)
            VL = sb(ctx, "VLb", [P, NT, H, D + 1], F16)
            HI = sb(ctx, "HIb", [P, 2 * CH, T], F16)
            LO = sb(ctx, "LOb", [P, 2 * CH, T], F16)
            STG = sb(ctx, "STGb", [P, 2, 2, 2, T], F16)
            RING = 8
            PR = sb(ctx, "PR", [P, RING, T])
            PH = sb(ctx, "PHb", [P, RING, T], F16)
            PL = sb(ctx, "PLb", [P, RING, T], F16)
            nm = sb(ctx, "nm", [P, RING])
            Y = sb(ctx, "Yb", [P, NT, C])
            YT = sb(ctx, "YTb", [P, CH, P])
            MTs = sb(ctx, "MTs", [P, CH, P])
            rin = sb(ctx, "rinb", [P, NT, G])
            X2 = sb(ctx, "X2", [P, 2, C])
            RS = sb(ctx, "RS", [P, 2, C])
            bst = sb(ctx, "bstb", [P, 6])
            mv = sb(ctx, "mvb", [P, 2])
            sd = sb(ctx, "sdb", [P, 2])
            sP = [ctx.enter_context(nc.psum_tensor(f"sP{i}", [P, 512], F32)) for i in range(4)]
            PTP = [ctx.enter_context(nc.psum_tensor(f"PTPb{i}", [P, 512], F32)) for i in range(2)]
            avP = ctx.enter_context(nc.psum_tensor("avPb", [P, NT, G, D + 1], F32))

            b_loaded = sem("b_loaded")
            v_ones = sem("v_ones")
            zeroed = sem("zeroed")
            stored_x = [sem(f"stored_x{i}") for i in range(2)]
            var1 = sem("var1")
            sd1 = sem("sd1")
            n1_ready = sem("n1_ready")
            g1_ready = sem("g1_ready")
            h_ready = sem("h_ready")
            bm_full = sem("bm_full")
            bm_free = sem("bm_free")
            pr_full = sem("pr_full")
            bhi = sem("bhi")
            blo = sem("blo")
            v_ready = sem("v_ready")
            bstage = [sem(f"bstage{i}") for i in range(2)]
            s_full = sem("s_full")
            nm_ready = sem("nm_ready")
            bp_ready = sem("bp_ready")
            bpt_full = sem("bpt_full")
            bph_ready = sem("bph_ready")
            bpl_ready = sem("bpl_ready")
            bvh_ready = sem("bvh_ready")
            bav = sem("bav")
            by_ready = sem("by_ready")
            x2_ready = sem("x2_ready")
            rs_ready = sem("rs_ready")
            var2 = sem("var2")
            sd2 = sem("sd2")
            n2_ready = sem("n2_ready")
            g2_ready = sem("g2_ready")
            m_ready = sem("m_ready")
            mt_ready = sem("mt_ready")
            kept = sem("kept")
            lg_ready = sem("lg_ready")
            dve_b = sem("dve_b")
            TC = H * NT
            AHEAD = 3
            BEHIND = 2
            BU = 5 * NT
            BD = 16 * 6 * G // 2 * 2

            def use_h(b, i):
                return b * BU + i

            def use_o(b, i, k):
                return b * BU + (NT + 4 * i + k)

            with nc.Block() as block:
                @block.sync
                def _(sp):
                    sp.wait_ge(v_ones, 3)
                    sp.dma_start(xs_d.rearrange("s p c -> p s c"), PR[:, 0, 0:C].unsqueeze(1).broadcast_to([P, SLOTS, C])).then_inc(zeroed, 16)
                    sp.wait_ge(zeroed, 16)
                    for n, name in enumerate(["Wq", "Wk", "Wv"]):
                        sp.dma_start(WQ[:, :, n * C:(n + 1) * C],
                                     a["L0_ffn_" + name].rearrange("(k p) c -> p k c", p=P)).then_inc(b_loaded, 16)
                    sp.dma_start(WO[:, :, :], a["L0_ffn_Wo"].rearrange("(k p) c -> p k c", p=P)).then_inc(b_loaded, 16)
                    sp.dma_start(WG[:, :, :], a["L0_ffn_Wg"].rearrange("(k p) c -> p k c", p=P)).then_inc(b_loaded, 16)
                    for n, name in enumerate(["ln1_g", "ln1_b", "ln2_g", "ln2_b"]):
                        sp.dma_start(lng[:, n, :], a["L0_ffn_" + name].partition_broadcast(P)).then_inc(b_loaded, 16)
                    sp.wait_ge(b_loaded, 144)
                    for e in range(E):
                        sp.dma_start(W1S[:, e, :, :], a["L0_ffn_W1"][e].rearrange("(k p) f -> p k f", p=P)).then_inc(w1_loaded, 16)
                    with sp.Fori(0, B) as b:
                        sp.wait_ge(bhi, 4 * b + 4)
                        sp.wait_ge(blo, 4 * b + 4)
                        for g in range(NG):
                            slot, c = g % 2, g // 2
                            sp.wait_ge(s_full, b * TC + G * NT * (g + 1))
                            for j in range(G):
                                par, s = j % 2, j // 2
                                src = 16 * ((G * g + j) % HPC)
                                for jj, planes in enumerate([(HI, HI), (HI, LO), (LO, HI)]):
                                    dst = 64 * par + D * jj
                                    for qk in range(2):
                                        sp.dma_start(STG[dst:dst + D, slot, qk, s, :],
                                                     planes[qk][src:src + D, 2 * qk + c, :]).then_inc(bstage[slot], 16)
                        for i in range(NT):
                            sp.wait_ge(rs_ready, NT * b + (i + 1))
                            sp.dma_start(x2_d[bass.ds(b, 1), :, i, :].rearrange("a p c -> (a p) c"), RS[:, i % 2, :]).then_inc(stored_x[i % 2], 16)

                @block.gpsimd
                def _(pool):
                    pool.memset(VH[:, :, :, D], 1.0).then_inc(v_ones, 1)
                    pool.memset(VL[:, :, :, D], 0.0).then_inc(v_ones, 1)
                    pool.memset(PR[:, 0, 0:C], 0.0).then_inc(v_ones, 1)
                    pool.wait_ge(b_loaded, 144)
                    with pool.Fori(0, B) as b:
                        for i in range(NT):
                            pool.wait_ge(n1_ready, NT * b + (i + 1))
                            pool.tensor_tensor(XN[:, 1, :], XN[:, 0, :], lng[:, 0, :], ALU.mult).then_inc(g1_ready, 1)
                            pool.wait_ge(g1_ready, NT * b + (i + 1))
                            pool.tensor_tensor(HB[:, :], XN[:, 1, :], lng[:, 1, :], ALU.add).then_inc(h_ready, 1)
                        for i in range(NT):
                            pool.wait_ge(x2_ready, NT * b + (i + 1))
                            pool.wait_ge(stored_x[i % 2], 8 * NT * b + 16 * (i // 2 + 1))
                            pool.tensor_tensor(RS[:, i % 2, :], X2[:, i % 2, :],
                                               X[:, bass.ds(NT * b + i, 1), :].rearrange("p a c -> p (a c)"), ALU.add).then_inc(rs_ready, 1)
                            pool.wait_ge(n2_ready, NT * b + (i + 1))
                            pool.tensor_tensor(XN[:, 1, :], XN[:, 0, :], lng[:, 2, :], ALU.mult).then_inc(g2_ready, 1)
                            pool.wait_ge(g2_ready, NT * b + (i + 1))
                            pool.tensor_tensor(HB[:, :], XN[:, 1, :], lng[:, 3, :], ALU.add).then_inc(m_ready, 1)

                @block.scalar
                def _(act):
                    with act.Fori(0, B) as b:
                        for i in range(NT):
                            act.wait_ge(var1, NT * b + (i + 1))
                            act.activation(sd[:, 0:1], mv[:, 1:2], ACT.Sqrt, bias=epsc[:, :]).then_inc(sd1, 1)
                            act.wait_ge(bm_full, use_h(b, i) + 1)
                            act.activation(hT[:, :, i * P:(i + 1) * P], mis[:, 0:C].rearrange("p (k t) -> p k t", k=CH),
                                           ACT.Copy).then_inc(bm_free, 1)
                        for u in range(2 * CH):
                            act.wait_ge(pr_full, 6 * b + (u + 1))
                            act.activation(HI[:, u, :], sP[u % 4][:, :], ACT.Copy,
                                           scale=float(D) ** -0.5 if u < CH else 1.0).then_inc(bhi, 1)

                        for v in range(NT // 2):
                            act.wait_ge(pr_full, 6 * b + (2 * CH + v + 1))
                            for i in range(2):
                                ins = act.activation(VH[:, 2 * v + i, :, 0:D],
                                                     sP[v][:, i * C:(i + 1) * C].rearrange("p (h d) -> p h d", d=D), ACT.Copy)
                            ins.then_inc(bvh_ready, 1)

                        def exp(tc):
                            act.wait_ge(nm_ready, b * TC + (tc + 1))
                            act.wait_ge(bpt_full, b * TC + (tc + 1))
                            act.activation(PR[:, tc % RING, :], sP[tc % 4][:, :], ACT.Exp,
                                           bias=nm[:, tc % RING:tc % RING + 1]).then_inc(bp_ready, 1)

                        def copy(tc):
                            act.wait_ge(bpt_full, b * TC + (tc + 1 + RING))
                            act.wait_ge(bav, b * TC + (tc + 1))
                            act.activation(PH[:, tc % RING, :], PTP[tc % 2][:, :], ACT.Copy).then_inc(bph_ready, 1)

                        for tc in range(-AHEAD, TC):
                            if tc >= 0:
                                copy(tc)
                            if tc + AHEAD < TC:
                                exp(tc + AHEAD)
                        for i in range(NT):
                            act.wait_ge(bm_full, use_o(b, i, 0) + 1)
                            act.activation(YT[:, :, :].rearrange("p k t -> p (k t)"), mis[:, 0:C], ACT.Copy).then_inc(bm_free, 1)
                            act.wait_ge(var2, NT * b + (i + 1))
                            act.activation(sd[:, 0:1], mv[:, 1:2], ACT.Sqrt, bias=epsc[:, :]).then_inc(sd2, 1)
                            act.wait_ge(m_ready, NT * b + (i + 1))
                            act.activation(X[:, bass.ds(NT * b + i, 1), :].rearrange("p a c -> p (a c)"), HB[:, :], ACT.Copy).then_inc(kept, 1)
                            act.wait_ge(bm_full, use_o(b, i, 2) + 1)
                            act.activation(MTs[:, :, :].rearrange("p k t -> p (k t)"), mis[:, 0:C], ACT.Copy).then_inc(bm_free, 1)

                @block.tensor
                def _(pe):
                    pe.wait_ge(b_loaded, 144)
                    with pe.Fori(0, B) as b:
                        for i in range(NT):
                            pe.wait_ge(bm_free, use_h(b, i) + 1)
                            pe.wait_ge(h_ready, NT * b + (i + 1))
                            for k in range(CH):
                                mm = pe.transpose(mis[:, k * P:(k + 1) * P], HB[:, k * P:(k + 1) * P], ident[:, :])
                            mm.then_inc(bm_full, 1)
                        pe.wait_ge(bm_free, use_h(b, NT) + 1)
                        for u in range(2 * CH):
                            for k in range(CH):
                                mm = pe.matmul(sP[u % 4][:, :], WQ[:, k, u * P:(u + 1) * P], hT[:, k, :],
                                               start=(k == 0), stop=(k == CH - 1))
                            mm.then_inc(pr_full, 1)
                        for v in range(NT // 2):
                            pe.wait_ge(blo, 4 * b + (v + 1))
                            for i in (2 * v, 2 * v + 1):
                                for k in range(CH):
                                    mm = pe.matmul(sP[v][:, (i % 2) * C:(i % 2 + 1) * C], hT[:, k, i * P:(i + 1) * P],
                                                   WQ[:, k, 2 * C:3 * C], start=(k == 0), stop=(k == CH - 1))
                            mm.then_inc(pr_full, 1)
                        pe.wait_ge(v_ready, 2 * b + 2)
                        pe.wait_ge(blo, 4 * b + 4)

                        def score(tc):
                            g, j, i = tc // (G * NT), tc // NT % G, tc % NT
                            if j == 0 and i == 0:
                                pe.wait_ge(bstage[g % 2], b * (BD * NG // 2) + BD * (g // 2 + 1))
                            pe.wait_ge(bp_ready, b * TC + (tc + 1))
                            base = 64 * (j % 2)
                            pe.matmul(sP[tc % 4][:, :], STG[base:base + R3, g % 2, 0, j // 2, i * P:(i + 1) * P],
                                      STG[base:base + R3, g % 2, 1, j // 2, :], start=True, stop=True).then_inc(s_full, 1)

                        def turn(tc):
                            pe.wait_ge(bp_ready, b * TC + (tc + 1 + 4))
                            pe.wait_ge(bpl_ready, b * TC + (tc + 1))
                            for k in range(NT):
                                mm = pe.transpose(PTP[tc % 2][:, k * P:(k + 1) * P], PR[:, tc % RING, k * P:(k + 1) * P], ident[:, :])
                            mm.then_inc(bpt_full, 1)

                        def product(tc):
                            g, j, i = tc // (G * NT), tc // NT % G, tc % NT
                            pe.wait_ge(bpl_ready, b * TC + (tc + 3))
                            if j == 0 and i == 0:
                                pe.wait_ge(by_ready, NG * b + (g + 1))
                            for k in range(NT):
                                ph, pl = PH[:, tc % RING, k * P:(k + 1) * P], PL[:, tc % RING, k * P:(k + 1) * P]
                                vh, vl = VH[:, k, G * g + j, :], VL[:, k, G * g + j, :]
                                pe.matmul(avP[:, i, j, :], ph, vh, start=(k == 0), stop=False)
                                pe.matmul(avP[:, i, j, :], ph, vl, start=False, stop=False)
                                mm = pe.matmul(avP[:, i, j, :], pl, vh, start=False, stop=(k == NT - 1))
                            mm.then_inc(bav, 1)

                        for tc in range(-AHEAD, TC + BEHIND):
                            if tc + AHEAD < TC:
                                score(tc + AHEAD)
                            if 0 <= tc < TC:
                                turn(tc)
                            if tc >= BEHIND:
                                product(tc - BEHIND)

                        for i in range(NT):
                            if i == 0:
                                pe.wait_ge(by_ready, NG * b + (NG + 1))
                            pe.wait_ge(bm_free, use_o(b, i, 0) + 1)
                            for k in range(CH):
                                mm = pe.transpose(mis[:, k * P:(k + 1) * P], Y[:, i, k * P:(k + 1) * P], ident[:, :])
                            mm.then_inc(bm_full, 1)
                            pe.wait_ge(bm_free, use_o(b, i, 1) + 1)
                            for k in range(CH):
                                mm = pe.matmul(mis[:, 0:C], YT[:, k, :], WO[:, k, :], start=(k == 0), stop=(k == CH - 1))
                            mm.then_inc(bm_full, 1)
                            pe.wait_ge(bm_free, use_o(b, i, 2) + 1)
                            pe.wait_ge(m_ready, NT * b + (i + 1))
                            for k in range(CH):
                                mm = pe.transpose(mis[:, k * P:(k + 1) * P], HB[:, k * P:(k + 1) * P], ident[:, :])
                            mm.then_inc(bm_full, 1)
                            pe.wait_ge(bm_free, use_o(b, i, 3) + 1)
                            for k in range(CH):
                                mm = pe.matmul(mis[:, 0:E], MTs[:, k, :], WG[:, k, :], start=(k == 0), stop=(k == CH - 1))
                            mm.then_inc(bm_full, 1)

                @block.vector
                def _(dve):
                    dve.sem_inc(bm_free, 1)
                    dve.sem_inc(s_full, 2 * G * NT)
                    dve.sem_inc(bp_ready, 4)
                    dve.sem_inc(bpt_full, RING)
                    dve.sem_inc(bav, RING)
                    dve.sem_inc(bpl_ready, 2)
                    dve.sem_inc(by_ready, 1)
                    dve.sem_inc(stored_x[0], 16)
                    dve.sem_inc(stored_x[1], 16)
                    dve.wait_ge(v_ones, 3)
                    steps = NT * 2 + NG + NT * 2
                    with dve.Fori(0, B) as b:
                        step = [0]

                        def chain(ins):
                            step[0] += 1
                            ins.then_inc(dve_b, 1)
                            dve.wait_ge(dve_b, steps * b + step[0])

                        def norm(src, i, var, root, done):
                            chain(dve.bn_stats(bst[:, :], src))
                            dve.sem_inc(passed, 1)
                            dve.bn_aggr(mv[:, :], bst[:, :]).then_inc(var, 1)
                            dve.wait_ge(var, NT * b + (i + 1))
                            dve.wait_ge(root, NT * b + (i + 1))
                            chain(dve.reciprocal(sd[:, 1:2], sd[:, 0:1]))
                            dve.tensor_scalar(XN[:, 0, :], src, mv[:, 0:1], sd[:, 1:2], ALU.subtract, ALU.mult).then_inc(done, 1)

                        for i in range(NT):
                            norm(X[:, bass.ds(NT * b + i, 1), :].rearrange("p a c -> p (a c)"), i, var1, sd1, n1_ready)
                            dve.wait_ge(h_ready, NT * b + (i + 1))
                        for u in range(2 * CH):
                            dve.wait_ge(bhi, 4 * b + (u + 1))
                            dve.scalar_tensor_tensor(LO[:, u, :], sP[u % 4][:, :], float(D) ** -0.5 if u < CH else 1.0,
                                                     HI[:, u, :], ALU.mult, ALU.subtract).then_inc(blo, 1)
                        for v in range(NT // 2):
                            dve.wait_ge(bvh_ready, 2 * b + (v + 1))
                            for i in range(2):
                                ins = dve.tensor_tensor(VL[:, 2 * v + i, :, 0:D],
                                                        sP[v][:, i * C:(i + 1) * C].rearrange("p (h d) -> p h d", d=D),
                                                        VH[:, 2 * v + i, :, 0:D], ALU.subtract)
                            ins.then_inc(v_ready, 1)

                        def maximum(tc):
                            dve.wait_ge(s_full, b * TC + (2 * G * NT + tc + 1))
                            dve.tensor_reduce(nm[:, tc % RING:tc % RING + 1], sP[tc % 4][:, :], AX.X, ALU.max,
                                              negate=True).then_inc(nm_ready, 1)

                        def low(tc):
                            dve.wait_ge(bph_ready, b * TC + (tc + 1))
                            dve.tensor_tensor(PL[:, tc % RING, :], PTP[tc % 2][:, :], PH[:, tc % RING, :],
                                              ALU.subtract).then_inc(bpl_ready, 1)

                        def normalise(g):
                            dve.wait_ge(bav, b * TC + (NT * G * (g + 1) + RING))
                            chain(dve.reciprocal(rin[:, :, :], avP[:, :, :, D]))
                            dve.tensor_tensor(Y[:, :, G * g * D:G * (g + 1) * D].rearrange("p i (j d) -> p i j d", d=D),
                                              avP[:, :, :, 0:D], rin[:, :, :].unsqueeze(3).broadcast_to([P, NT, G, D]),
                                              ALU.mult).then_inc(by_ready, 1)

                        for tc in range(-AHEAD, TC):
                            if tc + AHEAD < TC:
                                maximum(tc + AHEAD)
                            if tc >= 0:
                                low(tc)
                            if tc > BEHIND and (tc - BEHIND + 1) % (G * NT) == 0:
                                normalise((tc - BEHIND + 1) // (G * NT) - 1)
                        normalise(NG - 1)

                        for i in range(NT):
                            dve.wait_ge(bm_full, use_o(b, i, 1) + 1)
                            dve.tensor_tensor(X2[:, i % 2, :], mis[:, 0:C],
                                              X[:, bass.ds(NT * b + i, 1), :].rearrange("p a c -> p (a c)"), ALU.add).then_inc(x2_ready, 1)
                            dve.wait_ge(x2_ready, NT * b + (i + 1))
                            dve.sem_inc(bm_free, 1)
                            norm(X2[:, i % 2, :], i, var2, sd2, n2_ready)
                            dve.wait_ge(bm_full, use_o(b, i, 3) + 1)
                            dve.tensor_copy(LG[:, bass.ds(NT * b + i, 1), :].rearrange("p a c -> p (a c)"), mis[:, 0:E]).then_inc(lg_ready, 1)
                            dve.wait_ge(lg_ready, NT * b + (i + 1))
                            dve.sem_inc(bm_free, 1)
                        assert step[0] == steps, step[0]
                    dve.wait_ge(stored_x[0], 16 + 8 * N)
                    dve.wait_ge(stored_x[1], 16 + 8 * N)


        with ExitStack() as ctx:
            W2S = sb(ctx, "W2S", [P, E, FC, C])
            HS = sb(ctx, "HS", [P, 2, F])
            HT = sb(ctx, "HT", [P, 2, F])
            B1S = sb(ctx, "B1S", [3, E * F], BF16)
            B2S = sb(ctx, "B2S", [3, E * C], BF16)
            tri = sb(ctx, "tri", [P, P], BF16)
            ones = sb(ctx, "ones", [P, P], BF16)
            selb = sb(ctx, "selb", [P, N * E], BF16)
            keys = sb(ctx, "keys", [P, N])
            tilen = sb(ctx, "tilen", [P, SLOTS])
            intsc = sb(ctx, "intsc", [P, N + SLOTS], mybir.dt.int32)
            idx = sb(ctx, "idx", [P, 2, N], mybir.dt.uint32)
            expert = sb(ctx, "expert", [P, SLOTS], mybir.dt.int32)
            gate = sb(ctx, "gate", [P, 2, N])
            bst = sb(ctx, "bstc", [P, 6])
            mv = sb(ctx, "mvc", [P, 2, 2])
            sd = sb(ctx, "sdc", [P, 2, 2])
            hP = [ctx.enter_context(nc.psum_tensor(f"hP{i}", [P, F], F32)) for i in range(2)]
            hTP = ctx.enter_context(nc.psum_tensor("hTP", [P, F], F32))
            yP = ctx.enter_context(nc.psum_tensor("yP", [P, 512], F32))
            tmp = [HS[:, n // 4, (n % 4) * 256:(n % 4) * 256 + N * E].rearrange("p (n e) -> p n e", e=E) for n in range(8)]
            cmp_e = HT[:, 0, 0:E * N].rearrange("p (e n) -> p e n", e=E)
            cmp_s = HT[:, 1, 0:SLOTS * E].rearrange("p (s e) -> p s e", e=E)
            vec = [HT[:, 0, 512 + N * n:512 + N * n + N] for n in range(6)]
            ev = [HT[:, 0, 768 + E * n:768 + E * n + E] for n in range(6)]
            b32 = HT[:, 0, 832:832 + 80]
            bp = sb(ctx, "bp", [P, 3, 80], BF16)
            if N * C >= 20 * C:
                XR = X
            else:
                XR = sb(ctx, "XR", [P, 20, C])
            XS = XR[:, 0:2, :]
            XT = XR[:, 2:4, :].rearrange("p s (k t) -> p s k t", k=CH)
            YS = XR[:, 4:6, :]
            RG = 4
            Y1 = XR[:, 6:6 + RG, :]
            Y2 = XR[:, 10:10 + RG, :]
            XB = XR[:, 14:14 + RG, :]
            ZO = XR[:, 18:20, :]

            w2_loaded = sem("w2_loaded")
            cb_loaded = sem("cb_loaded")
            cb_moved = sem("cb_moved")
            cst = sem("cst")
            lg_off = sem("lg_off")
            lg_exp = sem("lg_exp")
            sel_ready = sem("sel_ready")
            rank_full = sem("rank_full")
            parts_ready = sem("parts_ready")
            idx_ready = sem("idx_ready")
            scattered = sem("scattered")
            xs_loaded = [sem(f"xs_loaded{i}") for i in range(2)]
            xt_full = sem("xt_full")
            xt_ready = sem("xt_ready")
            h_full = sem("h_full")
            h_ready2 = sem("h_ready2")
            ht_full = sem("ht_full")
            ht_ready = sem("ht_ready")
            y_full = sem("y_full")
            ys_ready = sem("ys_ready")
            ys_stored = [sem(f"ys_stored{i}") for i in range(2)]
            gathered = [sem(f"gathered{i}") for i in range(RG)]
            xb_loaded = [sem(f"xb_loaded{i}") for i in range(RG)]
            z_ready = sem("z_ready")
            var3 = sem("var3")
            sd3 = sem("sd3")
            o_ready = sem("o_ready")
            o_stored = [sem(f"o_stored{i}") for i in range(2)]
            dve_c = sem("dve_c")
            HALF = SLOTS // 2

            with nc.Block() as block:
                @block.sync
                def _(sp):
                    sp.dma_start(b32[:, 0:64], a["L0_ffn_b1"].rearrange("e f -> (e f)").rearrange("(p j) -> p j", p=P)).then_inc(cb_loaded, 16)
                    sp.dma_start(b32[:, 64:80], a["L0_ffn_b2"].rearrange("e f -> (e f)").rearrange("(p j) -> p j", p=P)).then_inc(cb_loaded, 16)
                    for e in range(E):
                        sp.dma_start(W2S[:, e, :, :], a["L0_ffn_W2"][e].rearrange("(k p) c -> p k c", p=P)).then_inc(w2_loaded, 16)
                    sp.wait_ge(parts_ready, 3)
                    for r in range(3):
                        sp.dma_start(B1S[r:r + 1, :], bp[:, r, 0:64]).then_inc(cb_moved, 16)
                        sp.dma_start(B2S[r:r + 1, :], bp[:, r, 64:80]).then_inc(cb_moved, 16)
                    sp.wait_ge(scattered, 16 * 2 * N)

                    def load(q, s):
                        sp.wait_ge(xt_full, 2 * q + (s + 1))
                        sp.dma_start(XS[:, s, :], xs_d[bass.ds(2 * q + s, 1)].rearrange("a p c -> (a p) c")).then_inc(xs_loaded[s], 16)

                    def store(q, s):
                        sp.wait_ge(ys_ready, 2 * q + (s + 2))
                        sp.dma_start(ys_d[bass.ds(2 * q + s, 1)].rearrange("a p c -> (a p) c"), YS[:, s, :]).then_inc(ys_stored[s], 16)

                    load(0, 0)
                    load(0, 1)
                    with sp.Fori(0, HALF - 1) as q:
                        for s in range(2):
                            load(q + 1, s)
                            store(q, s)
                    store(HALF - 1, 0)
                    store(HALF - 1, 1)
                    for n in range(N):
                        if n >= RG:
                            sp.wait_ge(z_ready, n - RG + 1)
                        sp.dma_start(XB[:, n % RG, :], x2_d[n // NT, :, n % NT, :]).then_inc(xb_loaded[n % RG], 16)
                        if n >= 2:
                            sp.wait_ge(o_ready, n - 1)
                            sp.dma_start(out_t[(n - 2) // NT, :, (n - 2) % NT, :], ZO[:, n % 2, :]).then_inc(o_stored[n % 2], 16)
                    for n in range(N - 2, N):
                        sp.wait_ge(o_ready, n + 1)
                        sp.dma_start(out_t[n // NT, :, n % NT, :], ZO[:, n % 2, :]).then_inc(o_stored[n % 2], 16)
                    for s in range(2):
                        sp.wait_ge(o_stored[s], 16 * N // 2)

                @block.gpsimd
                def _(pool):
                    pool.memset(tri[:, :], 1.0).then_inc(cst, 1)
                    pool.memset(ones[:, :], 1.0).then_inc(cst, 1)
                    pool.iota(intsc[:, 0:N], pattern=[[P, N]], base=0, channel_multiplier=0).then_inc(cst, 1)
                    pool.iota(intsc[:, N:N + SLOTS], pattern=[[1, SLOTS]], base=0, channel_multiplier=0).then_inc(cst, 1)
                    pool.wait_ge(cst, 4)
                    pool.affine_select(out=tri[:, :], in_=tri[:, :], compare_op=ALU.is_gt, fill=0.0,
                                       base=0, pattern=[[1, P]], channel_multiplier=-1).then_inc(cst, 1)
                    pool.tensor_copy(keys[:, :], intsc[:, 0:N]).then_inc(cst, 1)
                    pool.tensor_copy(tilen[:, :], intsc[:, N:N + SLOTS]).then_inc(cst, 1)
                    pool.wait_ge(idx_ready, 1)
                    for n in range(N):
                        for k in range(2):
                            pool.indirect_dma_start(out=xs_d.rearrange("s p c -> (s p) c"),
                                                    out_offset=bass.IndirectOffsetOnAxis(ap=idx[:, k, n:n + 1], axis=0),
                                                    in_=X[:, n, :], in_offset=None).then_inc(scattered, 16)
                    for s in range(2):
                        pool.wait_ge(ys_stored[s], 16 + 16 * HALF)
                    for n in range(N):
                        if n >= RG:
                            pool.wait_ge(z_ready, n - RG + 1)
                        for k, dst in enumerate((Y1, Y2)):
                            pool.indirect_dma_start(out=dst[:, n % RG, :], out_offset=None,
                                                    in_=ys_d.rearrange("s p c -> (s p) c"),
                                                    in_offset=bass.IndirectOffsetOnAxis(ap=idx[:, k, n:n + 1], axis=0)).then_inc(gathered[n % RG], 16)

                @block.scalar
                def _(act):
                    act.wait_ge(lg_off, 1)
                    act.activation(tmp[1], tmp[0], ACT.Exp).then_inc(lg_exp, 1)

                    def body(q, s):
                        j1 = 2 * q + (s + 1)
                        act.wait_ge(xt_full, j1 + 2)
                        act.activation(XT[:, s, :, :].rearrange("p k t -> p (k t)"), mis[:, 0:C], ACT.Copy).then_inc(xt_ready, 1)

                    def gelu(q, s):
                        j1 = 2 * q + (s + 1)
                        act.wait_ge(h_full, j1)
                        act.wait_ge(ht_full, 2 * j1)
                        act.activation(HS[:, s, :], hP[s][:, :], ACT.Gelu_apprx_tanh).then_inc(h_ready2, 1)

                    body(0, 0)
                    with act.Fori(0, HALF - 1) as q:
                        body(q, 1)
                        gelu(q, 0)
                        body(q + 1, 0)
                        gelu(q, 1)
                    body(HALF - 1, 1)
                    gelu(HALF - 1, 0)
                    gelu(HALF - 1, 1)
                    for n in range(N):
                        act.wait_ge(var3, n + 1)
                        act.activation(sd[:, n % 2, 0:1], mv[:, n % 2, 1:2], ACT.Sqrt, bias=epsc[:, :]).then_inc(sd3, 1)

                @block.tensor
                def _(pe):
                    pe.wait_ge(cst, 7)
                    pe.wait_ge(sel_ready, 1)
                    pe.matmul(hP[0][:, 0:N * E], tri[:, :], selb[:, :], start=True, stop=True)
                    pe.matmul(hP[1][:, 0:N * E], ones[:, :], selb[:, :], start=True, stop=True).then_inc(rank_full, 1)
                    pe.wait_ge(idx_ready, 1)
                    pe.wait_ge(cb_moved, 96)
                    pe.wait_ge(w1_loaded, 16 * E)
                    pe.wait_ge(w2_loaded, 16 * E)
                    w1f = W1S[:, :, :, :].rearrange("p e k f -> p (e k f)")
                    w2f = W2S[:, :, :, :].rearrange("p e k c -> p (e k c)")

                    def turn_x(q, s):
                        j1 = 2 * q + (s + 1)
                        pe.wait_ge(xs_loaded[s], 16 * q + 16)
                        pe.wait_ge(xt_ready, j1)
                        for k in range(CH):
                            mm = pe.transpose(mis[:, k * P:(k + 1) * P], XS[:, s, k * P:(k + 1) * P], ident[:, :])
                        mm.then_inc(xt_full, 1)

                    def hidden(q, s, half, e):
                        j1 = 2 * q + (s + 1)
                        if half == 0:
                            pe.wait_ge(xt_ready, j1 + 1)
                            pe.wait_ge(h_ready2, j1)
                        dst = hP[s][:, half * 512:(half + 1) * 512]
                        for k in range(CH):
                            pe.matmul(dst, XT[:, s, k, :], w1f[:, bass.ds(e * (CH * F) + (k * F + half * 512), 512)],
                                      start=(k == 0), stop=False)
                        mm = pe.matmul(dst, ones[0:3, :], B1S[:, bass.ds(e * F + half * 512, 512)], start=False, stop=True)
                        if half == 1:
                            mm.then_inc(h_full, 1)

                    def turn_h(q, s):
                        j1 = 2 * q + (s + 1)
                        pe.wait_ge(h_ready2, j1 + 2)
                        for half in range(2):
                            pe.wait_ge(ht_ready, 2 * j1 + (half - 1))
                            for k in range(FC // 2 * half, FC // 2 * (half + 1)):
                                mm = pe.transpose(hTP[:, k * P:(k + 1) * P], HS[:, s, k * P:(k + 1) * P], ident[:, :])
                            mm.then_inc(ht_full, 1)

                    def outputs(q, s, e):
                        j1 = 2 * q + (s + 1)
                        pe.wait_ge(ys_ready, j1)
                        for k in range(FC):
                            if k % (FC // 2) == 0:
                                pe.wait_ge(ht_ready, 2 * j1 + (1 + k // (FC // 2)))
                            pe.matmul(yP[:, 0:C], HT[:, s, k * P:(k + 1) * P], w2f[:, bass.ds(e * (FC * C) + k * C, C)],
                                      start=(k == 0), stop=False)
                        pe.matmul(yP[:, 0:C], ones[0:3, :], B2S[:, bass.ds(e * C, C)], start=False, stop=True).then_inc(y_full, 1)

                    def expert_of(j):
                        return pe.value_load(expert[0:1, bass.ds(j, 1)], min_val=0, max_val=E - 1)

                    def step(q, s, pq, ps):
                        e = expert_of(2 * q + s)
                        hidden(q, s, 0, e)
                        if pq is not None:
                            turn_h(pq, ps)
                        hidden(q, s, 1, e)
                        return e

                    turn_x(0, 0)
                    step(0, 0, None, None)
                    turn_x(0, 1)
                    with pe.Fori(0, HALF - 1) as q:
                        step(q, 1, q, 0)
                        turn_x(q + 1, 0)
                        outputs(q, 0, expert_of(2 * q))
                        step(q + 1, 0, q, 1)
                        turn_x(q + 1, 1)
                        outputs(q, 1, expert_of(2 * q + 1))
                    last = HALF - 1
                    step(last, 1, last, 0)
                    outputs(last, 0, expert_of(2 * last))
                    turn_h(last, 1)
                    outputs(last, 1, expert_of(2 * last + 1))

                @block.vector
                def _(dve):
                    step = [0]

                    def chain(ins):
                        step[0] += 1
                        ins.then_inc(dve_c, 1)
                        dve.wait_ge(dve_c, step[0])

                    dve.sem_inc(xt_full, 2)
                    dve.sem_inc(xt_ready, 1)
                    dve.sem_inc(h_ready2, 2)
                    dve.sem_inc(ht_full, 4)
                    dve.sem_inc(ht_ready, 2)
                    dve.sem_inc(ys_ready, 1)
                    dve.sem_inc(ys_stored[0], 16)
                    dve.sem_inc(ys_stored[1], 16)

                    def over_e(v):
                        return v.unsqueeze(2).broadcast_to([P, N, E])

                    dve.wait_ge(cb_loaded, 32)
                    rest = HT[:, 0, 912:992]
                    chain(dve.tensor_copy(bp[:, 0, :], b32))
                    dve.sem_inc(parts_ready, 1)
                    chain(dve.tensor_tensor(rest, b32, bp[:, 0, :], ALU.subtract))
                    chain(dve.tensor_copy(bp[:, 1, :], rest))
                    dve.sem_inc(parts_ready, 1)
                    chain(dve.tensor_tensor(rest, rest, bp[:, 1, :], ALU.subtract))
                    chain(dve.tensor_copy(bp[:, 2, :], rest))
                    dve.sem_inc(parts_ready, 1)

                    chain(dve.tensor_reduce(vec[0], LG[:, :, :], AX.X, ALU.max))
                    dve.tensor_tensor(tmp[0], LG[:, :, :], over_e(vec[0]), ALU.subtract).then_inc(lg_off, 1)
                    dve.wait_ge(lg_exp, 1)
                    chain(dve.tensor_reduce(vec[1], tmp[1], AX.X, ALU.add))
                    chain(dve.reciprocal(vec[2], vec[1]))
                    chain(dve.tensor_tensor(tmp[2], tmp[1], over_e(vec[2]), ALU.mult))

                    def prefix(src, bufs, n, at):
                        d, turn = 1, 0
                        while d < n:
                            dst = bufs[turn]
                            chain(dve.tensor_copy(at(dst, 0, d), at(src, 0, d)))
                            chain(dve.tensor_tensor(at(dst, d, n), at(src, d, n), at(src, 0, n - d), ALU.add))
                            src, turn, d = dst, 1 - turn, 2 * d
                        return src

                    probs, top_p = tmp[2], [vec[3], vec[4]]
                    first = [tmp[5], tmp[6]]
                    for k in range(2):
                        chain(dve.tensor_reduce(top_p[k], probs, AX.X, ALU.max))
                        chain(dve.tensor_tensor(tmp[0], probs, over_e(top_p[k]), ALU.is_equal))
                        count = prefix(tmp[0], [tmp[3], tmp[4]], E, lambda v, lo, hi: v[:, :, lo:hi])
                        chain(dve.scalar_tensor_tensor(first[k], count, 1.0, tmp[0], ALU.is_equal, ALU.mult))
                        if k == 0:
                            chain(dve.scalar_tensor_tensor(tmp[1], first[0], -2.0, probs, ALU.mult, ALU.add))
                            probs = tmp[1]
                    chain(dve.tensor_tensor(selb[:, :].rearrange("p (n e) -> p n e", e=E), first[0], first[1], ALU.add))
                    dve.sem_inc(sel_ready, 1)
                    chain(dve.tensor_tensor(vec[0], vec[3], vec[4], ALU.add))
                    chain(dve.reciprocal(vec[1], vec[0]))
                    for k in range(2):
                        chain(dve.tensor_tensor(gate[:, k, :], top_p[k], vec[1], ALU.mult))

                    dve.wait_ge(rank_full, 1)
                    dve.wait_ge(cst, 7)
                    tot = tmp[0]
                    chain(dve.tensor_copy(tot, hP[1][:, 0:N * E].rearrange("p (n e) -> p n e", e=E)))
                    inc = prefix(tot, [tmp[1], tmp[2]], N, lambda v, lo, hi: v[:, lo:hi, :])
                    chain(dve.tensor_copy(ev[0], inc[:, N - 1, :]))
                    chain(dve.tensor_tensor(cmp_e, ev[0].unsqueeze(2).broadcast_to([P, E, N]),
                                            keys[:, :].unsqueeze(1).broadcast_to([P, E, N]), ALU.is_gt))
                    chain(dve.tensor_reduce(ev[1], cmp_e, AX.X, ALU.add))
                    tinc = prefix(ev[1], [ev[2], ev[3]], E, lambda v, lo, hi: v[:, lo:hi])
                    chain(dve.tensor_tensor(ev[4], tinc, ev[1], ALU.subtract))
                    chain(dve.tensor_tensor(tmp[3], inc, tot, ALU.subtract))
                    chain(dve.tensor_tensor(tmp[4], hP[0][:, 0:N * E].rearrange("p (n e) -> p n e", e=E), tmp[3], ALU.add))
                    chain(dve.scalar_tensor_tensor(tmp[7], ev[4].unsqueeze(1).broadcast_to([P, N, E]), float(P), tmp[4],
                                                   ALU.mult, ALU.add))
                    for k in range(2):
                        chain(dve.tensor_tensor(tmp[3], first[k], tmp[7], ALU.mult))
                        chain(dve.tensor_reduce(vec[5], tmp[3], AX.X, ALU.add))
                        chain(dve.tensor_copy(idx[:, k, :], vec[5]))
                    chain(dve.tensor_tensor(cmp_s, tilen[:, :].unsqueeze(2).broadcast_to([P, SLOTS, E]),
                                            ev[4].unsqueeze(1).broadcast_to([P, SLOTS, E]), ALU.is_ge))
                    count = HT[:, 1, E * SLOTS:E * SLOTS + SLOTS]
                    chain(dve.tensor_reduce(count, cmp_s, AX.X, ALU.add))
                    chain(dve.tensor_scalar(expert[:, :], count, -1.0, None, ALU.add))
                    dve.sem_inc(idx_ready, 1)

                    def copies(q, s):
                        j1 = 2 * q + (s + 1)
                        for half in range(2):
                            dve.wait_ge(ht_full, 2 * j1 + (3 + half))
                            dve.tensor_copy(HT[:, s, half * 512:(half + 1) * 512], hTP[:, half * 512:(half + 1) * 512]).then_inc(ht_ready, 1)

                    def result(q, s):
                        j1 = 2 * q + (s + 1)
                        dve.wait_ge(y_full, j1)
                        dve.wait_ge(ys_stored[s], 16 * q + 16)
                        dve.tensor_copy(YS[:, s, :], yP[:, 0:C]).then_inc(ys_ready, 1)

                    with dve.Fori(0, HALF) as q:
                        for s in range(2):
                            copies(q, s)
                            result(q, s)

                    for n in range(N):
                        z = Y1[:, n % RG, :]
                        dve.wait_ge(gathered[n % RG], 32 * (n // RG + 1))
                        dve.wait_ge(xb_loaded[n % RG], 16 * (n // RG + 1))
                        chain(dve.scalar_tensor_tensor(XB[:, n % RG, :], z, gate[:, 0, n:n + 1], XB[:, n % RG, :], ALU.mult, ALU.add))
                        if n >= 2:
                            dve.wait_ge(o_stored[n % 2], 16 * (n // 2))
                        chain(dve.scalar_tensor_tensor(ZO[:, n % 2, :], Y2[:, n % RG, :], gate[:, 1, n:n + 1], XB[:, n % RG, :],
                                                       ALU.mult, ALU.add))
                        dve.sem_inc(z_ready, 1)
                        chain(dve.bn_stats(bst[:, :], ZO[:, n % 2, :]))
                        dve.bn_aggr(mv[:, n % 2, :], bst[:, :]).then_inc(var3, 1)
                        dve.wait_ge(var3, n + 1)
                        dve.wait_ge(sd3, n + 1)
                        chain(dve.reciprocal(sd[:, n % 2, 1:2], sd[:, n % 2, 0:1]))
                        dve.tensor_scalar(ZO[:, n % 2, :], ZO[:, n % 2, :], mv[:, n % 2, 0:1], sd[:, n % 2, 1:2],
                                          ALU.subtract, ALU.mult).then_inc(o_ready, 1)


def kernel(**inputs):
    import numpy as np
    import concourse.bacc as bacc
    from concourse.bass_utils import run_bass_kernel_spmd

    nc = bacc.Bacc("TRN2", target_bir_lowering=False, num_devices=1)
    arrays, args = {}, {}
    for name, value in inputs.items():
        v = np.ascontiguousarray(value)
        if v.ndim == 0:
            v = v.reshape(1)
        arrays[f"in_{name}"] = v
        args[name] = nc.dram_tensor(f"in_{name}", v.shape, mybir.dt.from_np(v.dtype), kind="ExternalInput").ap()
    shape = inputs["L0_attn_x"].shape
    out = nc.dram_tensor("out_x", shape, F32, kind="ExternalOutput").ap()
    build(nc, args, out)
    return run_bass_kernel_spmd(nc, [arrays], core_ids=[0]).results[0]["out_x"]
```

```python
from contextlib import ExitStack
from math import factorial

import concourse.bass as bass
from concourse import mybir

ALU = mybir.AluOpType
ACT = mybir.ActivationFunctionType
AX = mybir.AxisListType
F32 = mybir.dt.float32
F16 = mybir.dt.float16
BF16 = mybir.dt.bfloat16

P = 128
EPS = 1e-5
MASKED = 1e30
SINH = [1.0 / factorial(2 * k + 1) for k in range(8)]


def build(nc, a, out):
    x_d = a["L0_attn_x"]
    B, T, C = x_d.shape
    H = a["L0_attn_log_k"].shape[0]
    D = C // H
    E, _, F = a["L0_ffn_W1"].shape
    NT = T // P
    N = B * NT
    CH = C // P
    FC = F // P
    HPC = H // CH
    G = 4
    NG = H // G
    R3 = 3 * D
    QKW = 2 * C
    VAI = C + H + 1
    WCOL = QKW + VAI
    W = [P * (i + 1) for i in range(NT)]
    OFF = {3: 0, 2: 512, 0: 896, 1: 1024}
    SW = sum(W)
    REGIONS = [[3], [2, 0], [1]]
    assert D == 16 and NT == 4 and T == 512 and H == 16 and C == 256 and SW == 1280

    x_t = x_d.rearrange("b (t p) c -> b p t c", p=P)
    out_t = out.rearrange("b (t p) c -> b p t c", p=P)

    SLOTS = 2 * N + E
    x2_d = nc.dram_tensor("x2_scratch", [B, P, NT, C], F32, kind="Internal").ap()

    xs_d = nc.dram_tensor("rows_scratch", [SLOTS, P, C], F32, kind="Internal").ap()
    ys_d = nc.dram_tensor("results_scratch", [SLOTS, P, C], F32, kind="Internal").ap()

    with ExitStack() as top:
        def sem(name):
            return top.enter_context(nc.semaphore(name))

        def sb(ctx, name, shape, dt=F32):
            return ctx.enter_context(nc.sbuf_tensor(name, shape, dt))

        X = sb(top, "X", [P, N, C])
        ident = sb(top, "ident", [P, P])
        identb = sb(top, "identb", [P, P], BF16)
        neg1 = sb(top, "neg1", [P, 1])
        epsc = sb(top, "epsc", [P, 1])
        mis = top.enter_context(nc.psum_tensor("misc", [P, 512], F32))

        setup_pool = sem("setup_pool")
        passed = sem("passed")

        with ExitStack() as ctx:
            WT = sb(ctx, "WT", [P, CH, WCOL])
            WOT = sb(ctx, "WOT", [P, CH, C])
            mask = sb(ctx, "mask", [P, P], BF16)
            bias = sb(ctx, "bias", [P, WCOL])
            bout = sb(ctx, "bout", [P, C])
            thr = sb(ctx, "thr", [P, 1])
            s2 = sb(ctx, "s2", [P, 1])
            rcurv = sb(ctx, "rcurv", [P, H])
            XI = sb(ctx, "XI", [P, NT, C])
            AI = sb(ctx, "AI", [P, 2, NT, H + 1])
            V = sb(ctx, "V", [P, H, D + 1])
            st = sb(ctx, "st", [P, 10, NT * 2 * H])
            stat = sb(ctx, "stat", [P, NT, 5 * H])
            root = sb(ctx, "root", [P, NT, 5 * H])
            spk = sb(ctx, "spk", [P, NT])
            HI = sb(ctx, "HI", [P, 4 * CH, T], F16)
            LO = sb(ctx, "LO", [P, 4 * CH, T], F16)
            STG = sb(ctx, "STG", [P, NG, 4, 2, T], F16)
            MC = sb(ctx, "MC", [P, 2, G, SW])
            TT = sb(ctx, "TT", [P, 2, G, SW])
            PH = sb(ctx, "PH", [P, 2, SW], F16)
            PL = sb(ctx, "PL", [P, 2, SW], F16)
            VH = sb(ctx, "VH", [P, NT, H, D + 1], F16)
            VL = sb(ctx, "VL", [P, NT, H, D + 1], F16)
            mn = sb(ctx, "mn", [P, 2, G, NT])
            Y = sb(ctx, "Y", [P, NT, C])
            YT = sb(ctx, "YT", [P, CH, P])
            rin = sb(ctx, "rin", [P, NT, G])
            bst = sb(ctx, "bst", [P, NT, 6])
            mv = sb(ctx, "mv", [P, NT, 2])
            sd = sb(ctx, "sd", [P, 2, NT])
            mP = [ctx.enter_context(nc.psum_tensor(f"mP{i}", [P, 512], F32)) for i in range(2)]
            SeP = [ctx.enter_context(nc.psum_tensor(f"SeP{i}", [P, 512], F32)) for i in range(2)]
            PTP = [ctx.enter_context(nc.psum_tensor(f"PTP{i}", [P, 512], F32)) for i in range(2)]
            avP = ctx.enter_context(nc.psum_tensor("avP", [P, NT, G, D + 1], F32))

            before = TT[:, :, :, :].rearrange("p s j w -> p (s j w)")
            QK = before[:, 0:NT * QKW].rearrange("p (i c) -> p i c", i=NT)
            SQ = before[:, NT * QKW:2 * NT * QKW].rearrange("p (i h d) -> p i h d", i=NT, d=D)
            HY = before[:, 2 * NT * QKW:3 * NT * QKW].rearrange("p (i h d) -> p i h d", i=NT, d=D)
            QE = before[:, 3 * NT * QKW:3 * NT * QKW + NT * C].rearrange("p (i c) -> p i c", i=NT)
            xT = before[:, 3 * NT * QKW + NT * C:4 * NT * QKW].rearrange("p (i k t) -> p i k t", i=NT, k=CH)
            z = before[:, 4 * NT * QKW:4 * NT * QKW + NT * C].rearrange("p (i c) -> p i c", i=NT)

            WL = TT[:, 0, :, :].rearrange("p g w -> p (g w)")
            WQR = WL[:, 0:6 * C].rearrange("p (r c) -> p r c", r=6)
            WOR = WL[:, 6 * C:8 * C].rearrange("p (r c) -> p r c", r=2)
            WAR = WL[:, 8 * C:9 * C]
            lk = st[:, 0, 0:H]

            a_w_loaded = sem("a_w_loaded")
            a_c_loaded = sem("a_c_loaded")
            wt_full = sem("wt_full")
            wt_free = sem("wt_free")
            sc_exp = sem("sc_exp")
            sc_one = sem("sc_one")
            sc_ln = sem("sc_ln")
            sc_done = sem("sc_done")
            dve_a0 = sem("dve_a0")

            with nc.Block() as block:
                @block.sync
                def _(sp):
                    sp.dma_start(WQR, a["L0_attn_Wqkv"].rearrange("(r p) c -> p r c", p=P)).then_inc(a_w_loaded, 16)
                    sp.dma_start(WOR, a["L0_attn_Wout"].rearrange("(r p) c -> p r c", p=P)).then_inc(a_w_loaded, 16)
                    sp.dma_start(WAR[0:H, :], a["L0_attn_Walpha"]).then_inc(a_w_loaded, 16)
                    sp.dma_start(WAR[H:H + 1, :], a["L0_attn_Wimp"]).then_inc(a_w_loaded, 16)

                @block.scalar
                def _(act):
                    act.dma_start(lk, a["L0_attn_log_k"].partition_broadcast(P)).then_inc(a_c_loaded, 16)
                    act.dma_start(s2[:, :], a["L0_attn_qk_scale"].partition_broadcast(P)).then_inc(a_c_loaded, 16)
                    act.dma_start(thr[:, :], a["L0_attn_spike_threshold"].partition_broadcast(P)).then_inc(a_c_loaded, 16)
                    act.dma_start(bias[:, 0:3 * C], a["L0_attn_bqkv"].partition_broadcast(P)).then_inc(a_c_loaded, 16)
                    act.dma_start(bias[:, 3 * C:3 * C + H], a["L0_attn_balpha"].partition_broadcast(P)).then_inc(a_c_loaded, 16)
                    act.dma_start(bias[:, 3 * C + H:], a["L0_attn_bimp"].partition_broadcast(P)).then_inc(a_c_loaded, 16)
                    act.dma_start(bout[:, :], a["L0_attn_bout"].partition_broadcast(P)).then_inc(a_c_loaded, 16)
                    act.wait_ge(sc_one, 1)
                    act.activation(st[:, 2, 0:H], st[:, 1, 0:H], ACT.Exp).then_inc(sc_exp, 1)
                    act.activation(sd[:, 0, 0:1], s2[:, :], ACT.Exp, scale=-1.0).then_inc(sc_exp, 1)
                    act.wait_ge(sc_one, 2)
                    act.activation(st[:, 4, 0:H], st[:, 3, 0:H], ACT.Ln).then_inc(sc_ln, 1)

                @block.gpsimd
                def _(pool):
                    pool.memset(ident[:, :], 0.0).then_inc(setup_pool, 1)
                    pool.memset(mask[:, :], 0.0).then_inc(setup_pool, 1)
                    pool.memset(neg1[:, :], -1.0).then_inc(setup_pool, 1)
                    pool.memset(epsc[:, :], EPS).then_inc(setup_pool, 1)
                    pool.memset(V[:, :, :], 1.0).then_inc(setup_pool, 1)
                    pool.wait_ge(setup_pool, 5)
                    pool.affine_select(out=ident[:, :], in_=ident[:, :], compare_op=ALU.not_equal, fill=1.0,
                                       base=0, pattern=[[-1, P]], channel_multiplier=1).then_inc(setup_pool, 1)
                    pool.affine_select(out=mask[:, :], in_=mask[:, :], compare_op=ALU.is_ge, fill=MASKED,
                                       base=0, pattern=[[-1, P]], channel_multiplier=1).then_inc(setup_pool, 1)
                    pool.wait_ge(setup_pool, 7)
                    pool.tensor_copy(identb[:, :], ident[:, :]).then_inc(setup_pool, 1)

                @block.tensor
                def _(pe):
                    pe.wait_ge(setup_pool, 8)
                    pe.wait_ge(a_w_loaded, 64)
                    n = 0
                    for r in range(8):
                        src = WQR[:, r, :] if r < 6 else WOR[:, r - 6, :]
                        if n >= 1:
                            pe.wait_ge(wt_free, n)
                        for k in range(CH):
                            mm = pe.transpose(mis[:, k * P:(k + 1) * P], src[:, k * P:(k + 1) * P], ident[:, :])
                        mm.then_inc(wt_full, 1)
                        n += 1
                    pe.wait_ge(wt_free, n)
                    for k in range(CH):
                        mm = pe.transpose(mis[:, k * 32:k * 32 + H + 1], WAR[0:H + 1, k * P:(k + 1) * P],
                                          ident[0:H + 1, 0:H + 1])
                    mm.then_inc(wt_full, 1)

                @block.vector
                def _(dve):
                    step = [0]

                    def chain(ins):
                        step[0] += 1
                        ins.then_inc(dve_a0, 1)
                        dve.wait_ge(dve_a0, step[0])

                    dve.wait_ge(a_c_loaded, 112)
                    chain(dve.tensor_scalar(st[:, 9, 0:H], lk, -1.0, None, ALU.mult))
                    chain(dve.tensor_tensor(st[:, 8, 0:H], lk, st[:, 9, 0:H], ALU.max))
                    dve.tensor_scalar(st[:, 1, 0:H], st[:, 8, 0:H], -1.0, None, ALU.mult).then_inc(sc_one, 1)
                    dve.wait_ge(sc_exp, 2)
                    dve.tensor_scalar(st[:, 3, 0:H], st[:, 2, 0:H], 1.0, None, ALU.add).then_inc(sc_one, 1)
                    chain(dve.tensor_scalar(sd[:, 1, 0:1], sd[:, 0, 0:1], 1.0, None, ALU.add))
                    chain(dve.reciprocal(sd[:, 0, 0:1], sd[:, 1, 0:1]))
                    chain(dve.tensor_scalar(sd[:, 1, 0:1], sd[:, 0, 0:1], 1.5, None, ALU.mult))
                    chain(dve.tensor_tensor(s2[:, :], sd[:, 1, 0:1], sd[:, 1, 0:1], ALU.mult))
                    dve.wait_ge(sc_ln, 1)
                    chain(dve.tensor_scalar(st[:, 5, 0:H], lk, 0.0, None, ALU.max))
                    chain(dve.tensor_tensor(st[:, 6, 0:H], st[:, 5, 0:H], st[:, 4, 0:H], ALU.add))
                    chain(dve.tensor_scalar(st[:, 7, 0:H], st[:, 6, 0:H], 1e-6, None, ALU.add))
                    chain(dve.reciprocal(rcurv[:, :], st[:, 7, 0:H]))
                    for r in range(8):
                        dve.wait_ge(wt_full, r + 1)
                        dst = WT[:, :, r * P:(r + 1) * P] if r < 6 else WOT[:, :, (r - 6) * P:(r - 5) * P]
                        dve.tensor_copy(dst, mis[:, 0:C].rearrange("p (k c) -> p k c", k=CH)).then_inc(wt_free, 1)
                    dve.wait_ge(wt_full, 9)
                    dve.tensor_copy(WT[:, :, 3 * C:WCOL],
                                    mis[:, 0:32 * CH].rearrange("p (k c) -> p k c", k=CH)[:, :, 0:H + 1]).then_inc(wt_free, 1)

            x_loaded = sem("x_loaded")
            x_used = sem("x_used")
            misc_full = sem("misc_full")
            misc_free = sem("misc_free")
            x_turned = sem("x_turned")
            xT_ready = sem("xT_ready")
            pq_full = sem("pq_full")
            pv_full = sem("pv_full")
            op_full = sem("op_full")
            ai_ready = sem("ai_ready")
            qk_ready = sem("qk_ready")
            ea_ready = sem("ea_ready")
            sq_ready = sem("sq_ready")
            qs_ready = sem("qs_ready")
            qe_ready = sem("qe_ready")
            stat_ready = sem("stat_ready")
            root_ready = sem("root_ready")
            space_ready = sem("space_ready")
            hy_ready = sem("hy_ready")
            hi_ready = sem("hi_ready")
            lo_ready = sem("lo_ready")
            stage_ready = [sem(f"stage_ready{s}") for s in range(NG)]
            m_full = sem("m_full")
            m_free = sem("m_free")
            msq_ready = sem("msq_ready")
            rt_ready = sem("rt_ready")
            sum_ready = sem("sum_ready")
            dsq_ready = sem("dsq_ready")
            dsum_ready = sem("dsum_ready")
            ln_ready = sem("ln_ready")
            hyp_ready = sem("hyp_ready")
            se_full = sem("se_full")
            comb_ready = sem("comb_ready")
            p_ready = sem("p_ready")
            pt_full = sem("pt_full")
            ph_ready = sem("ph_ready")
            pt_ready = sem("pt_ready")
            vh_ready = sem("vh_ready")
            vl_ready = sem("vl_ready")
            av_full = sem("av_full")
            av_tile = sem("av_tile")
            y_ready = sem("y_ready")
            yT_ready = sem("yT_ready")
            sd_ready = sem("sd_ready")
            var_ready = sem("var_ready")
            dve_a = sem("dve_a")
            SD = 16 * 5 * G
            SE = H * NT
            MSQ = H - G
            SUM = H - G // 2
            MU = 2 * NT

            def msq_count(g, j):
                return (G // 2) * (g + 1) if g < 2 else G * (g - 1) + j + 1

            def sum_count(g, j):
                return G * g + j + 1 - G // 2

            def use_post(b, i, k):
                return b * MU + (2 * i + k)

            opP = [mP[0], mP[1], SeP[0], SeP[1]]

            with nc.Block() as block:
                @block.sync
                def _(sp):
                    with sp.Fori(0, B) as b:
                        sp.wait_ge(x_used, b + 1)
                        sp.dma_start(XI[:, :, :], x_t[bass.ds(b, 1)].rearrange("a p t c -> (a p) t c")).then_inc(x_loaded, 16)
                        sp.wait_ge(hi_ready, 2 * NT * b + 2 * NT)
                        sp.wait_ge(lo_ready, 2 * NT * b + 2 * NT)
                        for g in range(NG):
                            slot, c = g, g // 2
                            sp.wait_ge(se_full, b * (H * NT) + G * NT * (g + 1))
                            for j in range(G):
                                par, s = j % 2, j // 2
                                src = 16 * ((G * g + j) % HPC)
                                dst = 64 * par
                                sp.dma_start(STG[dst:dst + D, slot, :, s, :],
                                             HI[src:src + D, c:4 * CH:2, :]).then_inc(stage_ready[slot], 16)
                                for jj, planes in [(1, (HI, LO)), (2, (LO, HI))]:
                                    dst = 64 * par + D * jj
                                    for qk in range(2):
                                        sp.dma_start(STG[dst:dst + D, slot, qk:4:2, s, :],
                                                     planes[qk][src:src + D, 2 * qk + c:4 * CH:4, :]).then_inc(stage_ready[slot], 16)

                @block.gpsimd
                def _(pool):
                    with pool.Fori(0, B) as b:
                        for i in range(NT):
                            pool.wait_ge(qk_ready, NT * b + (i + 1))
                            pool.tensor_tensor(SQ[:, i, :, :].rearrange("p h d -> p (h d)"), QK[:, i, :], QK[:, i, :],
                                               ALU.mult).then_inc(sq_ready, 1)
                            pool.wait_ge(ai_ready, NT * b + (i + 1))
                            pool.sem_inc(passed, 1)
                            pool.tensor_copy(VH[:, i, :, :], V[:, :, :]).then_inc(vh_ready, 1)
                            pool.wait_ge(vh_ready, NT * b + (i + 1))
                            pool.tensor_tensor(VL[:, i, :, :], V[:, :, :], VH[:, i, :, :], ALU.subtract).then_inc(vl_ready, 1)
                        pool.wait_ge(qs_ready, b + 1)
                        for i in range(NT):
                            q3 = QK[:, i, :].rearrange("p (h d) -> p h d", d=D)
                            pool.tensor_tensor(QE[:, i, :].rearrange("p (h d) -> p h d", d=D), q3[:, 0:H, :],
                                               st[:, 9, i * H:(i + 1) * H].unsqueeze(2).broadcast_to([P, H, D]),
                                               ALU.mult).then_inc(qe_ready, 1)
                        pool.wait_ge(root_ready, b + 1)
                        for i in range(NT // 2, NT):
                            q3 = QK[:, i, :].rearrange("p (h d) -> p h d", d=D)
                            pool.tensor_tensor(HY[:, i, :, :], q3,
                                               root[:, i, 0:2 * H].unsqueeze(2).broadcast_to([P, 2 * H, D]),
                                               ALU.mult).then_inc(space_ready, 1)

                        def square(g):
                            for j in range(G // 2 if g < 2 else G):
                                pool.wait_ge(m_free, b * (3 * H) + (2 + 3 * (G * g + j + 1)))
                                if g >= 2:
                                    pool.wait_ge(pt_full, b * (H * NT) + NT * (G * (g - 2) + j + 1))
                                pool.tensor_tensor(TT[:, g % 2, j, :], MC[:, g % 2, j, :], MC[:, g % 2, j, :],
                                                   ALU.mult).then_inc(msq_ready, 1)

                        def add(g):
                            pool.wait_ge(rt_ready, NG * b + (g + 1))
                            for j in range(G // 2 if g == 0 else 0, G):
                                pool.tensor_tensor(TT[:, g % 2, j, :], MC[:, g % 2, j, :], TT[:, g % 2, j, :],
                                                   ALU.add).then_inc(sum_ready, 1)

                        for g in range(NG):
                            square(g)
                            add(g)

                @block.scalar
                def _(act):
                    with act.Fori(0, B) as b:
                        for h in range(2):
                            act.wait_ge(x_turned, 2 * b + (h + 1))
                            act.activation(xT[:, (NT // 2) * h:(NT // 2) * (h + 1), :, :].rearrange("p i k t -> p (i k t)"),
                                           PTP[h][:, :], ACT.Copy).then_inc(xT_ready, 1)
                        act.wait_ge(ai_ready, NT * b + NT)
                        act.activation(AI[:, 1, :, :], AI[:, 0, :, :], ACT.Exp, scale=-1.0).then_inc(ea_ready, 1)

                        def high(u):
                            r, i = u // NT, u % NT
                            act.wait_ge(op_full, 2 * NT * b + (u + 1))
                            act.activation(HI[:, 4 * r:4 * r + 4, i * P:(i + 1) * P],
                                           opP[u % 4][:, :].rearrange("p (k t) -> p k t", k=4), ACT.Copy).then_inc(hi_ready, 1)

                        act.wait_ge(stat_ready, b + 1)
                        act.activation(root[:, :, :], stat[:, :, :], ACT.Sqrt).then_inc(root_ready, 1)
                        for u in range(2 * NT):
                            high(u)

                        def roots(g):
                            act.wait_ge(msq_ready, b * MSQ + msq_count(g, G - 1))
                            if g < 2:
                                act.wait_ge(dsq_ready, b * G + (G // 2) * (g + 1))
                            w = TT[:, g % 2, :, :].rearrange("p j w -> p (j w)")
                            act.activation(w, w, ACT.Sqrt, bias=neg1[:, :]).then_inc(rt_ready, 1)

                        def logs(g):
                            for j in range(G):
                                if g == 0 and j < G // 2:
                                    act.wait_ge(dsum_ready, b * (G // 2) + (j + 1))
                                else:
                                    act.wait_ge(sum_ready, b * SUM + sum_count(g, j))
                                w = TT[:, g % 2, j, :]
                                act.activation(w, w, ACT.Ln).then_inc(ln_ready, 1)
                                act.wait_ge(ln_ready, b * H + (G * g + j + 1))
                                for i in range(NT):
                                    w = TT[:, g % 2, j, OFF[i]:OFF[i] + W[i]]
                                    h = G * g + j
                                    ins = act.activation(w, w, ACT.Square, scale=root[:, i, 4 * H + h:4 * H + h + 1])
                                ins.then_inc(hyp_ready, 1)

                        def exps(g):
                            for j in range(G):
                                for i in range(NT):
                                    act.wait_ge(comb_ready, b * (H * NT) + (NT * (G * g + j) + i + 3))
                                    w = TT[:, g % 2, j, OFF[i]:OFF[i] + W[i]]
                                    act.activation(w, w, ACT.Exp, bias=mn[:, g % 2, j, i:i + 1], scale=-1.0).then_inc(p_ready, 1)

                        for g in range(NG):
                            roots(g)
                            logs(g)
                            exps(g)

                        for i in range(NT):
                            act.wait_ge(misc_full, use_post(b, i, 0) + 1)
                            act.activation(YT[:, :, :].rearrange("p k t -> p (k t)"), mis[:, 0:C], ACT.Copy).then_inc(misc_free, 1)
                        act.wait_ge(var_ready, NT * b + NT)
                        act.activation(sd[:, 0, :], mv[:, :, 1], ACT.Sqrt, bias=epsc[:, :]).then_inc(sd_ready, 1)

                @block.tensor
                def _(pe):
                    with pe.Fori(0, B) as b:
                        pe.wait_ge(x_loaded, 16 * b + 16)
                        for i in range(NT):
                            at = (i % 2) * C
                            for k in range(CH):
                                mm = pe.transpose(PTP[i // 2][:, at + k * P:at + (k + 1) * P], XI[:, i, k * P:(k + 1) * P], ident[:, :])
                            if i % 2 == 1:
                                mm.then_inc(x_turned, 1)
                        for i in range(NT):
                            pe.wait_ge(xT_ready, 2 * b + (i // 2 + 1))
                            if i >= 2:
                                pe.wait_ge(qk_ready, NT * b + (i - 1))
                            for k in range(CH):
                                mm = pe.matmul(mP[i % 2][:, 0:QKW], xT[:, i, k, :], WT[:, k, 0:QKW],
                                               start=(k == 0), stop=(k == CH - 1))
                            mm.then_inc(pq_full, 1)
                            if i >= 2:
                                pe.wait_ge(ai_ready, NT * b + (i - 1))
                            for k in range(CH):
                                mm = pe.matmul(SeP[i % 2][:, 0:WCOL - QKW], xT[:, i, k, :], WT[:, k, QKW:WCOL],
                                               start=(k == 0), stop=(k == CH - 1))
                            mm.then_inc(pv_full, 1)
                        pe.wait_ge(ai_ready, NT * b + NT)
                        for i in range(NT):
                            pe.wait_ge(qe_ready, NT * b + (i + 1))
                            for k in range(CH):
                                pe.transpose(opP[i % 4][:, k * P:(k + 1) * P], QE[:, i, k * P:(k + 1) * P], ident[:, :])
                                mm = pe.transpose(opP[i % 4][:, (2 + k) * P:(3 + k) * P], QK[:, i, C + k * P:C + (k + 1) * P], ident[:, :])
                            mm.then_inc(op_full, 1)
                        for i in range(NT):
                            u = NT + i
                            pe.wait_ge(lo_ready, 2 * NT * b + (u - 3))
                            pe.wait_ge(hy_ready, NT * b + (i + 1))
                            hy = HY[:, i, :, :].rearrange("p h d -> p (h d)")
                            for k in range(4):
                                mm = pe.transpose(opP[u % 4][:, k * P:(k + 1) * P], hy[:, k * P:(k + 1) * P], ident[:, :])
                            mm.then_inc(op_full, 1)

                        def op(g, j, o, lo, hi):
                            return STG[64 * (j % 2):64 * (j % 2) + R3, g, o, j // 2, lo:hi]

                        def inner(g, j):
                            if j == 0:
                                pe.wait_ge(stage_ready[g], b * SD + SD)
                            for r, tiles in enumerate(REGIONS):
                                rc = 3 * (G * g + j) + r
                                pe.wait_ge(m_free, b * (3 * H) + (rc + 1))
                                at = 0
                                for i in tiles:
                                    mm = pe.matmul(mP[rc % 2][:, at:at + W[i]], op(g, j, 2, i * P, (i + 1) * P),
                                                   op(g, j, 3, 0, W[i]), start=True, stop=True)
                                    at += W[i]
                                mm.then_inc(m_full, 1)

                        def euclid(g):
                            for j in range(G):
                                for i in range(NT):
                                    tc = NT * (G * g + j) + i
                                    pe.wait_ge(comb_ready, b * (H * NT) + (tc + 1))
                                    pe.matmul(SeP[tc % 2][:, 0:W[i]], op(g, j, 0, i * P, (i + 1) * P),
                                              op(g, j, 1, 0, W[i]), start=True, stop=False)
                                    mm = pe.matmul(SeP[tc % 2][:, i * P:W[i]], identb[:, :], mask[:, :], start=False, stop=True)
                                    mm.then_inc(se_full, 1)

                        def turn(g, j, i):
                            tc = NT * (G * g + j) + i
                            pe.wait_ge(p_ready, b * (H * NT) + (tc + 1))
                            pe.wait_ge(pt_ready, b * (H * NT) + (tc + 1))
                            for k in range(i + 1):
                                mm = pe.transpose(PTP[tc % 2][:, k * P:(k + 1) * P],
                                                  TT[:, g % 2, j, OFF[i] + k * P:OFF[i] + (k + 1) * P], ident[:, :])
                            mm.then_inc(pt_full, 1)

                        def product(g, j, i):
                            tc = NT * (G * g + j) + i
                            pe.wait_ge(pt_ready, b * (H * NT) + (tc + 3))
                            if j == 0 and i == 0:
                                pe.wait_ge(y_ready, NG * b + (g + 1))
                                pe.wait_ge(vl_ready, NT * b + NT)
                            for k in range(i + 1):
                                blk = slice(OFF[i] + k * P, OFF[i] + (k + 1) * P)
                                pe.matmul(avP[:, i, j, :], PH[:, j % 2, blk], VH[:, k, G * g + j, :], start=(k == 0), stop=False)
                                pe.matmul(avP[:, i, j, :], PH[:, j % 2, blk], VL[:, k, G * g + j, :], start=False, stop=False)
                                mm = pe.matmul(avP[:, i, j, :], PL[:, j % 2, blk], VH[:, k, G * g + j, :], start=False, stop=(k == i))
                            mm.then_inc(av_tile, 1)

                        def outputs(g):
                            order = [(j, i) for j in range(G) for i in range(NT)]
                            for n, (j, i) in enumerate(order):
                                turn(g, j, i)
                                if n >= 2:
                                    product(g, *order[n - 2])
                                if i == NT - 1 and g + 2 < NG:
                                    inner(g + 2, j)
                            product(g, *order[-2])
                            product(g, *order[-1])

                        for g in range(2):
                            for j in range(G):
                                inner(g, j)
                        for g in range(NG):
                            euclid(g)
                            outputs(g)

                        for i in range(NT):
                            pe.wait_ge(misc_free, use_post(b, i, 0) + 1)
                            if i == 0:
                                pe.wait_ge(y_ready, NG * b + (NG + 1))
                            for k in range(CH):
                                mm = pe.transpose(mis[:, k * P:(k + 1) * P], Y[:, i, k * P:(k + 1) * P], ident[:, :])
                            mm.then_inc(misc_full, 1)
                            pe.wait_ge(misc_free, use_post(b, i, 1) + 1)
                            for k in range(CH):
                                mm = pe.matmul(mis[:, 0:C], YT[:, k, :], WOT[:, k, :], start=(k == 0), stop=(k == CH - 1))
                            mm.then_inc(misc_full, 1)

                @block.vector
                def _(dve):
                    dve.sem_inc(x_used, 1)
                    dve.sem_inc(misc_free, 1)
                    dve.sem_inc(m_free, 2)
                    dve.sem_inc(comb_ready, 2)
                    dve.sem_inc(pt_ready, 2)
                    dve.sem_inc(se_full, SE)
                    dve.sem_inc(y_ready, 1)
                    steps = NT * 2 + 2 + 7 + 6 + 8 + NT // 2 + NT + NG * 2 + NT * 3 + 2
                    with dve.Fori(0, B) as b:
                        step = [0]

                        def chain(ins):
                            step[0] += 1
                            ins.then_inc(dve_a, 1)
                            dve.wait_ge(dve_a, steps * b + step[0])

                        SS, SQ0, A, MK, G1, R2, Q, F2 = (st[:, k, :] for k in (0, 1, 2, 3, 4, 5, 6, 7))

                        def reduces(i):
                            dve.wait_ge(sq_ready, NT * b + (i + 1))
                            chain(dve.tensor_reduce(SS[:, 2 * H * i:2 * H * (i + 1)], SQ[:, i, :, :], AX.X, ALU.add))
                            chain(dve.tensor_copy(SQ0[:, 2 * H * i:2 * H * (i + 1)], SQ[:, i, :, 0]))

                        for i in range(NT):
                            dve.wait_ge(pq_full, NT * b + (i + 1))
                            dve.tensor_tensor(QK[:, i, :], mP[i % 2][:, :], bias[:, 0:QKW], ALU.add).then_inc(qk_ready, 1)
                            dve.wait_ge(pv_full, NT * b + (i + 1))
                            if i >= 1:
                                dve.wait_ge(vl_ready, NT * b + i)
                            dve.tensor_tensor(V[:, :, 0:D], SeP[i % 2][:, 0:C].rearrange("p (h d) -> p h d", d=D),
                                              bias[:, QKW:QKW + C].rearrange("p (h d) -> p h d", d=D), ALU.add)
                            dve.tensor_tensor(AI[:, 0, i, :], SeP[i % 2][:, C:VAI], bias[:, QKW + C:WCOL], ALU.add).then_inc(ai_ready, 1)
                            if i >= 1:
                                reduces(i - 1)
                        al = st[:, 8, 0:NT * (H + 1)].rearrange("p (i h) -> p i h", i=NT)
                        dve.wait_ge(ea_ready, b + 1)
                        chain(dve.tensor_scalar(AI[:, 0, :, :], AI[:, 1, :, :], 1.0, None, ALU.add))
                        chain(dve.reciprocal(al, AI[:, 0, :, :]))
                        dve.tensor_scalar(st[:, 9, 0:NT * H].rearrange("p (i h) -> p i h", i=NT), al[:, :, 0:H],
                                          0.25, -0.25, ALU.mult, ALU.add).then_inc(qs_ready, 1)
                        reduces(NT - 1)
                        chain(dve.tensor_scalar(A, SS, 1e-24, None, ALU.max))
                        chain(dve.reciprocal(G1, A))
                        chain(dve.tensor_scalar(R2, G1, s2[:, 0:1], None, ALU.mult))
                        chain(dve.scalar_tensor_tensor(A, SQ0, -2.0, SS, ALU.mult, ALU.add))
                        chain(dve.tensor_tensor(G1, A, R2, ALU.mult))
                        chain(dve.tensor_scalar(MK, G1, 1e-8, None, ALU.max))
                        chain(dve.tensor_scalar(Q, MK, SINH[7], None, ALU.mult))
                        for k in range(6, 0, -1):
                            chain(dve.scalar_tensor_tensor(Q, Q, SINH[k], MK, ALU.add, ALU.mult))
                        chain(dve.tensor_scalar(G1, Q, 1.0, None, ALU.add))
                        chain(dve.tensor_tensor(A, G1, G1, ALU.mult))
                        chain(dve.tensor_tensor(F2, A, R2, ALU.mult))
                        chain(dve.tensor_tensor(Q, SS, SQ0, ALU.subtract))
                        chain(dve.tensor_tensor(A, Q, F2, ALU.mult))
                        by_tile = lambda w: w.rearrange("p (i h) -> p i h", i=NT)
                        chain(dve.tensor_copy(stat[:, :, 0:2 * H], by_tile(F2)))
                        chain(dve.tensor_scalar(stat[:, :, 2 * H:4 * H], by_tile(A), 1.0, None, ALU.add))
                        dve.tensor_tensor(stat[:, :, 4 * H:5 * H], al[:, :, 0:H],
                                          rcurv[:, :].unsqueeze(1).broadcast_to([P, NT, H]), ALU.mult).then_inc(stat_ready, 1)
                        chain(dve.tensor_scalar(spk[:, :], al[:, :, H], thr[:, 0:1], None, ALU.is_gt))

                        def times(i):
                            chain(dve.tensor_scalar(HY[:, i, 0:H, 0], root[:, i, 2 * H:3 * H], -1.0, None, ALU.mult))
                            dve.tensor_copy(HY[:, i, H:2 * H, 0], root[:, i, 3 * H:4 * H]).then_inc(hy_ready, 1)

                        def low(u):
                            r, i = u // NT, u % NT
                            dve.wait_ge(hi_ready, 2 * NT * b + (u + 1))
                            dve.tensor_tensor(LO[:, 4 * r:4 * r + 4, i * P:(i + 1) * P],
                                              opP[u % 4][:, :].rearrange("p (k t) -> p k t", k=4),
                                              HI[:, 4 * r:4 * r + 4, i * P:(i + 1) * P], ALU.subtract).then_inc(lo_ready, 1)

                        dve.wait_ge(root_ready, b + 1)
                        for i in range(NT // 2):
                            chain(dve.tensor_tensor(HY[:, i, :, :], QK[:, i, :].rearrange("p (h d) -> p h d", d=D),
                                                    root[:, i, 0:2 * H].unsqueeze(2).broadcast_to([P, 2 * H, D]), ALU.mult))
                            times(i)
                        for u in range(NT):
                            low(u)
                            if u < NT // 2:
                                i = NT // 2 + u
                                dve.wait_ge(space_ready, (NT // 2) * b + (u + 1))
                                times(i)
                        for u in range(NT, 2 * NT):
                            low(u)

                        def clamps(g, j):
                            for r, tiles in enumerate(REGIONS):
                                rc = 3 * (G * g + j) + r
                                w = sum(W[i] for i in tiles)
                                dve.wait_ge(m_full, b * (3 * H) + (rc + 1))
                                if r == 0 and j == 0 and g >= 2:
                                    dve.wait_ge(sum_ready, b * SUM + sum_count(g - 2, G - 1))
                                at = OFF[tiles[0]]
                                dve.tensor_scalar(MC[:, g % 2, j, at:at + w], mP[rc % 2][:, 0:w], -1.0, 1.0 + 1e-6,
                                                  ALU.mult, ALU.max).then_inc(m_free, 1)

                        def combines(g):
                            for j in range(G):
                                dve.wait_ge(hyp_ready, b * H + (G * g + j + 1))
                                for i in range(NT):
                                    tc = NT * (G * g + j) + i
                                    dve.wait_ge(se_full, b * (H * NT) + (SE + tc + 1))
                                    w = TT[:, g % 2, j, OFF[i]:OFF[i] + W[i]]
                                    dve.sem_inc(passed, 1)
                                    dve.tensor_tensor_reduce(out=w, in0=SeP[tc % 2][:, 0:W[i]], in1=w, scale=1.0, scalar=3e38,
                                                             op0=ALU.add, op1=ALU.min,
                                                             accum_out=mn[:, g % 2, j, i:i + 1]).then_inc(comb_ready, 1)

                        def copies(g, j):
                            for i in range(NT):
                                tc = NT * (G * g + j) + i
                                dve.wait_ge(pt_full, b * (H * NT) + (tc + 1))
                                if tc >= 2 * NT:
                                    dve.wait_ge(av_tile, b * (H * NT) + (tc - 2 * NT + 1))
                                seg = slice(OFF[i], OFF[i] + W[i])
                                dve.tensor_copy(PH[:, j % 2, seg], PTP[tc % 2][:, 0:W[i]]).then_inc(ph_ready, 1)
                                dve.wait_ge(ph_ready, b * (H * NT) + (tc + 1))
                                dve.tensor_tensor(PL[:, j % 2, seg], PTP[tc % 2][:, 0:W[i]], PH[:, j % 2, seg],
                                                  ALU.subtract).then_inc(pt_ready, 1)

                        def normalise(g):
                            dve.wait_ge(av_tile, b * (H * NT) + NT * G * (g + 1))
                            chain(dve.reciprocal(rin[:, :, :], avP[:, :, :, D]))
                            chain(dve.tensor_tensor(rin[:, :, :], rin[:, :, :],
                                                    spk[:, :].unsqueeze(2).broadcast_to([P, NT, G]), ALU.mult))
                            dve.tensor_tensor(Y[:, :, G * g * D:G * (g + 1) * D].rearrange("p i (j d) -> p i j d", d=D),
                                              avP[:, :, :, 0:D], rin[:, :, :].unsqueeze(3).broadcast_to([P, NT, G, D]),
                                              ALU.mult).then_inc(y_ready, 1)

                        def dve_squares(g):
                            for j in range(G // 2, G):
                                dve.wait_ge(m_free, b * (3 * H) + (2 + 3 * (G * g + j + 1)))
                                dve.tensor_tensor(TT[:, g % 2, j, :], MC[:, g % 2, j, :], MC[:, g % 2, j, :],
                                                  ALU.mult).then_inc(dsq_ready, 1)

                        for j in range(G):
                            clamps(0, j)
                        dve_squares(0)
                        for j in range(G // 2):
                            clamps(1, j)
                        dve.wait_ge(rt_ready, NG * b + 1)
                        for j in range(G // 2):
                            dve.tensor_tensor(TT[:, 0, j, :], MC[:, 0, j, :], TT[:, 0, j, :], ALU.add).then_inc(dsum_ready, 1)
                        for j in range(G // 2, G):
                            clamps(1, j)
                        dve_squares(1)
                        for g in range(NG):
                            combines(g)
                            for j in range(G):
                                copies(g, j)
                                if g + 2 < NG:
                                    clamps(g + 2, j)
                            normalise(g)

                        for i in range(NT):
                            dve.wait_ge(misc_full, use_post(b, i, 1) + 1)
                            chain(dve.tensor_tensor(z[:, i, :], mis[:, 0:C], XI[:, i, :], ALU.add))
                            dve.sem_inc(misc_free, 1)
                            if i == NT - 1:
                                dve.sem_inc(x_used, 1)
                            chain(dve.tensor_tensor(z[:, i, :], z[:, i, :], bout[:, :], ALU.add))
                            chain(dve.bn_stats(bst[:, i, :], z[:, i, :]))
                            dve.sem_inc(passed, 1)
                            dve.bn_aggr(mv[:, i, :], bst[:, i, :]).then_inc(var_ready, 1)
                        dve.wait_ge(var_ready, NT * b + NT)
                        dve.wait_ge(sd_ready, b + 1)
                        chain(dve.reciprocal(sd[:, 1, :], sd[:, 0, :]))
                        for i in range(NT):
                            ins = dve.tensor_scalar(X[:, bass.ds(NT * b + i, 1), :].rearrange("p a c -> p (a c)"), z[:, i, :],
                                                    mv[:, i, 0:1], sd[:, 1, i:i + 1], ALU.subtract, ALU.mult)
                            if i == NT - 1:
                                chain(ins)
                        assert step[0] == steps, step[0]

        W1S = sb(top, "W1S", [P, E, CH, F])
        LG = sb(top, "LG", [P, N, E])
        w1_loaded = sem("w1_loaded")
        x2_stored = sem("x2_stored")
        with ExitStack() as ctx:
            WQ = sb(ctx, "WQ", [P, CH, 3 * C])
            WO = sb(ctx, "WO", [P, CH, C])
            WG = sb(ctx, "WG", [P, CH, E])
            lng = sb(ctx, "lng", [P, 4, C])
            XN = sb(ctx, "XN", [P, 2, C])
            hT = sb(ctx, "hT", [P, CH, T])
            HB = sb(ctx, "HB", [P, C])
            VH = sb(ctx, "VHb", [P, NT, H, D + 1], F16)
            VL = sb(ctx, "VLb", [P, NT, H, D + 1], F16)
            HI = sb(ctx, "HIb", [P, 2 * CH, T], F16)
            LO = sb(ctx, "LOb", [P, 2 * CH, T], F16)
            STG = sb(ctx, "STGb", [P, 2, 2, 2, T], F16)
            RING = 8
            PR = sb(ctx, "PR", [P, RING, T])
            PH = sb(ctx, "PHb", [P, RING, T], F16)
            PL = sb(ctx, "PLb", [P, RING, T], F16)
            nm = sb(ctx, "nm", [P, RING])
            Y = sb(ctx, "Yb", [P, NT, C])
            YT = sb(ctx, "YTb", [P, CH, P])
            MTs = sb(ctx, "MTs", [P, CH, P])
            rin = sb(ctx, "rinb", [P, NT, G])
            X2 = sb(ctx, "X2", [P, 2, C])
            RS = sb(ctx, "RS", [P, 2, C])
            bst = sb(ctx, "bstb", [P, 6])
            mv = sb(ctx, "mvb", [P, 2])
            sd = sb(ctx, "sdb", [P, 2])
            sP = [ctx.enter_context(nc.psum_tensor(f"sP{i}", [P, 512], F32)) for i in range(4)]
            PTP = [ctx.enter_context(nc.psum_tensor(f"PTPb{i}", [P, 512], F32)) for i in range(2)]
            avP = ctx.enter_context(nc.psum_tensor("avPb", [P, NT, G, D + 1], F32))

            b_loaded = sem("b_loaded")
            v_ones = sem("v_ones")
            zeroed = sem("zeroed")
            stored_x = [sem(f"stored_x{i}") for i in range(2)]
            var1 = sem("var1")
            sd1 = sem("sd1")
            n1_ready = sem("n1_ready")
            g1_ready = sem("g1_ready")
            h_ready = sem("h_ready")
            bm_full = sem("bm_full")
            bm_free = sem("bm_free")
            pr_full = sem("pr_full")
            bhi = sem("bhi")
            blo = sem("blo")
            v_ready = sem("v_ready")
            bstage = [sem(f"bstage{i}") for i in range(2)]
            s_full = sem("s_full")
            nm_ready = sem("nm_ready")
            bp_ready = sem("bp_ready")
            bpt_full = sem("bpt_full")
            bph_ready = sem("bph_ready")
            bpl_ready = sem("bpl_ready")
            bvh_ready = sem("bvh_ready")
            bav = sem("bav")
            by_ready = sem("by_ready")
            x2_ready = sem("x2_ready")
            rs_ready = sem("rs_ready")
            var2 = sem("var2")
            sd2 = sem("sd2")
            n2_ready = sem("n2_ready")
            g2_ready = sem("g2_ready")
            m_ready = sem("m_ready")
            mt_ready = sem("mt_ready")
            kept = sem("kept")
            lg_ready = sem("lg_ready")
            dve_b = sem("dve_b")
            TC = H * NT
            AHEAD = 3
            BEHIND = 2
            BU = 5 * NT
            BD = 16 * 6 * G // 2 * 2

            def use_h(b, i):
                return b * BU + i

            def use_o(b, i, k):
                return b * BU + (NT + 4 * i + k)

            with nc.Block() as block:
                @block.sync
                def _(sp):
                    sp.wait_ge(v_ones, 3)
                    sp.dma_start(xs_d.rearrange("s p c -> p s c"), PR[:, 0, 0:C].unsqueeze(1).broadcast_to([P, SLOTS, C])).then_inc(zeroed, 16)
                    sp.wait_ge(zeroed, 16)
                    for n, name in enumerate(["Wq", "Wk", "Wv"]):
                        sp.dma_start(WQ[:, :, n * C:(n + 1) * C],
                                     a["L0_ffn_" + name].rearrange("(k p) c -> p k c", p=P)).then_inc(b_loaded, 16)
                    sp.dma_start(WO[:, :, :], a["L0_ffn_Wo"].rearrange("(k p) c -> p k c", p=P)).then_inc(b_loaded, 16)
                    sp.dma_start(WG[:, :, :], a["L0_ffn_Wg"].rearrange("(k p) c -> p k c", p=P)).then_inc(b_loaded, 16)
                    for n, name in enumerate(["ln1_g", "ln1_b", "ln2_g", "ln2_b"]):
                        sp.dma_start(lng[:, n, :], a["L0_ffn_" + name].partition_broadcast(P)).then_inc(b_loaded, 16)
                    sp.wait_ge(b_loaded, 144)
                    for e in range(E):
                        sp.dma_start(W1S[:, e, :, :], a["L0_ffn_W1"][e].rearrange("(k p) f -> p k f", p=P)).then_inc(w1_loaded, 16)
                    with sp.Fori(0, B) as b:
                        sp.wait_ge(bhi, 4 * b + 4)
                        sp.wait_ge(blo, 4 * b + 4)
                        for g in range(NG):
                            slot, c = g % 2, g // 2
                            sp.wait_ge(s_full, b * TC + G * NT * (g + 1))
                            for j in range(G):
                                par, s = j % 2, j // 2
                                src = 16 * ((G * g + j) % HPC)
                                for jj, planes in enumerate([(HI, HI), (HI, LO), (LO, HI)]):
                                    dst = 64 * par + D * jj
                                    for qk in range(2):
                                        sp.dma_start(STG[dst:dst + D, slot, qk, s, :],
                                                     planes[qk][src:src + D, 2 * qk + c, :]).then_inc(bstage[slot], 16)
                        for i in range(NT):
                            sp.wait_ge(rs_ready, NT * b + (i + 1))
                            sp.dma_start(x2_d[bass.ds(b, 1), :, i, :].rearrange("a p c -> (a p) c"), RS[:, i % 2, :]).then_inc(stored_x[i % 2], 16)

                @block.gpsimd
                def _(pool):
                    pool.memset(VH[:, :, :, D], 1.0).then_inc(v_ones, 1)
                    pool.memset(VL[:, :, :, D], 0.0).then_inc(v_ones, 1)
                    pool.memset(PR[:, 0, 0:C], 0.0).then_inc(v_ones, 1)
                    pool.wait_ge(b_loaded, 144)
                    with pool.Fori(0, B) as b:
                        for i in range(NT):
                            pool.wait_ge(n1_ready, NT * b + (i + 1))
                            pool.tensor_tensor(XN[:, 1, :], XN[:, 0, :], lng[:, 0, :], ALU.mult).then_inc(g1_ready, 1)
                            pool.wait_ge(g1_ready, NT * b + (i + 1))
                            pool.tensor_tensor(HB[:, :], XN[:, 1, :], lng[:, 1, :], ALU.add).then_inc(h_ready, 1)
                        for i in range(NT):
                            pool.wait_ge(x2_ready, NT * b + (i + 1))
                            pool.wait_ge(stored_x[i % 2], 8 * NT * b + 16 * (i // 2 + 1))
                            pool.tensor_tensor(RS[:, i % 2, :], X2[:, i % 2, :],
                                               X[:, bass.ds(NT * b + i, 1), :].rearrange("p a c -> p (a c)"), ALU.add).then_inc(rs_ready, 1)
                            pool.wait_ge(n2_ready, NT * b + (i + 1))
                            pool.tensor_tensor(XN[:, 1, :], XN[:, 0, :], lng[:, 2, :], ALU.mult).then_inc(g2_ready, 1)
                            pool.wait_ge(g2_ready, NT * b + (i + 1))
                            pool.tensor_tensor(HB[:, :], XN[:, 1, :], lng[:, 3, :], ALU.add).then_inc(m_ready, 1)

                @block.scalar
                def _(act):
                    with act.Fori(0, B) as b:
                        for i in range(NT):
                            act.wait_ge(var1, NT * b + (i + 1))
                            act.activation(sd[:, 0:1], mv[:, 1:2], ACT.Sqrt, bias=epsc[:, :]).then_inc(sd1, 1)
                            act.wait_ge(bm_full, use_h(b, i) + 1)
                            act.activation(hT[:, :, i * P:(i + 1) * P], mis[:, 0:C].rearrange("p (k t) -> p k t", k=CH),
                                           ACT.Copy).then_inc(bm_free, 1)
                        for u in range(2 * CH):
                            act.wait_ge(pr_full, 6 * b + (u + 1))
                            act.activation(HI[:, u, :], sP[u % 4][:, :], ACT.Copy,
                                           scale=float(D) ** -0.5 if u < CH else 1.0).then_inc(bhi, 1)

                        for v in range(NT // 2):
                            act.wait_ge(pr_full, 6 * b + (2 * CH + v + 1))
                            for i in range(2):
                                ins = act.activation(VH[:, 2 * v + i, :, 0:D],
                                                     sP[v][:, i * C:(i + 1) * C].rearrange("p (h d) -> p h d", d=D), ACT.Copy)
                            ins.then_inc(bvh_ready, 1)

                        def exp(tc):
                            act.wait_ge(nm_ready, b * TC + (tc + 1))
                            act.wait_ge(bpt_full, b * TC + (tc + 1))
                            act.activation(PR[:, tc % RING, :], sP[tc % 4][:, :], ACT.Exp,
                                           bias=nm[:, tc % RING:tc % RING + 1]).then_inc(bp_ready, 1)

                        def copy(tc):
                            act.wait_ge(bpt_full, b * TC + (tc + 1 + RING))
                            act.wait_ge(bav, b * TC + (tc + 1))
                            act.activation(PH[:, tc % RING, :], PTP[tc % 2][:, :], ACT.Copy).then_inc(bph_ready, 1)

                        for tc in range(-AHEAD, TC):
                            if tc >= 0:
                                copy(tc)
                            if tc + AHEAD < TC:
                                exp(tc + AHEAD)
                        for i in range(NT):
                            act.wait_ge(bm_full, use_o(b, i, 0) + 1)
                            act.activation(YT[:, :, :].rearrange("p k t -> p (k t)"), mis[:, 0:C], ACT.Copy).then_inc(bm_free, 1)
                            act.wait_ge(var2, NT * b + (i + 1))
                            act.activation(sd[:, 0:1], mv[:, 1:2], ACT.Sqrt, bias=epsc[:, :]).then_inc(sd2, 1)
                            act.wait_ge(m_ready, NT * b + (i + 1))
                            act.activation(X[:, bass.ds(NT * b + i, 1), :].rearrange("p a c -> p (a c)"), HB[:, :], ACT.Copy).then_inc(kept, 1)
                            act.wait_ge(bm_full, use_o(b, i, 2) + 1)
                            act.activation(MTs[:, :, :].rearrange("p k t -> p (k t)"), mis[:, 0:C], ACT.Copy).then_inc(bm_free, 1)

                @block.tensor
                def _(pe):
                    pe.wait_ge(b_loaded, 144)
                    with pe.Fori(0, B) as b:
                        for i in range(NT):
                            pe.wait_ge(bm_free, use_h(b, i) + 1)
                            pe.wait_ge(h_ready, NT * b + (i + 1))
                            for k in range(CH):
                                mm = pe.transpose(mis[:, k * P:(k + 1) * P], HB[:, k * P:(k + 1) * P], ident[:, :])
                            mm.then_inc(bm_full, 1)
                        pe.wait_ge(bm_free, use_h(b, NT) + 1)
                        for u in range(2 * CH):
                            for k in range(CH):
                                mm = pe.matmul(sP[u % 4][:, :], WQ[:, k, u * P:(u + 1) * P], hT[:, k, :],
                                               start=(k == 0), stop=(k == CH - 1))
                            mm.then_inc(pr_full, 1)
                        for v in range(NT // 2):
                            pe.wait_ge(blo, 4 * b + (v + 1))
                            for i in (2 * v, 2 * v + 1):
                                for k in range(CH):
                                    mm = pe.matmul(sP[v][:, (i % 2) * C:(i % 2 + 1) * C], hT[:, k, i * P:(i + 1) * P],
                                                   WQ[:, k, 2 * C:3 * C], start=(k == 0), stop=(k == CH - 1))
                            mm.then_inc(pr_full, 1)
                        pe.wait_ge(v_ready, 2 * b + 2)
                        pe.wait_ge(blo, 4 * b + 4)

                        def score(tc):
                            g, j, i = tc // (G * NT), tc // NT % G, tc % NT
                            if j == 0 and i == 0:
                                pe.wait_ge(bstage[g % 2], b * (BD * NG // 2) + BD * (g // 2 + 1))
                            pe.wait_ge(bp_ready, b * TC + (tc + 1))
                            base = 64 * (j % 2)
                            pe.matmul(sP[tc % 4][:, :], STG[base:base + R3, g % 2, 0, j // 2, i * P:(i + 1) * P],
                                      STG[base:base + R3, g % 2, 1, j // 2, :], start=True, stop=True).then_inc(s_full, 1)

                        def turn(tc):
                            pe.wait_ge(bp_ready, b * TC + (tc + 1 + 4))
                            pe.wait_ge(bpl_ready, b * TC + (tc + 1))
                            for k in range(NT):
                                mm = pe.transpose(PTP[tc % 2][:, k * P:(k + 1) * P], PR[:, tc % RING, k * P:(k + 1) * P], ident[:, :])
                            mm.then_inc(bpt_full, 1)

                        def product(tc):
                            g, j, i = tc // (G * NT), tc // NT % G, tc % NT
                            pe.wait_ge(bpl_ready, b * TC + (tc + 3))
                            if j == 0 and i == 0:
                                pe.wait_ge(by_ready, NG * b + (g + 1))
                            for k in range(NT):
                                ph, pl = PH[:, tc % RING, k * P:(k + 1) * P], PL[:, tc % RING, k * P:(k + 1) * P]
                                vh, vl = VH[:, k, G * g + j, :], VL[:, k, G * g + j, :]
                                pe.matmul(avP[:, i, j, :], ph, vh, start=(k == 0), stop=False)
                                pe.matmul(avP[:, i, j, :], ph, vl, start=False, stop=False)
                                mm = pe.matmul(avP[:, i, j, :], pl, vh, start=False, stop=(k == NT - 1))
                            mm.then_inc(bav, 1)

                        for tc in range(-AHEAD, TC + BEHIND):
                            if tc + AHEAD < TC:
                                score(tc + AHEAD)
                            if 0 <= tc < TC:
                                turn(tc)
                            if tc >= BEHIND:
                                product(tc - BEHIND)

                        for i in range(NT):
                            if i == 0:
                                pe.wait_ge(by_ready, NG * b + (NG + 1))
                            pe.wait_ge(bm_free, use_o(b, i, 0) + 1)
                            for k in range(CH):
                                mm = pe.transpose(mis[:, k * P:(k + 1) * P], Y[:, i, k * P:(k + 1) * P], ident[:, :])
                            mm.then_inc(bm_full, 1)
                            pe.wait_ge(bm_free, use_o(b, i, 1) + 1)
                            for k in range(CH):
                                mm = pe.matmul(mis[:, 0:C], YT[:, k, :], WO[:, k, :], start=(k == 0), stop=(k == CH - 1))
                            mm.then_inc(bm_full, 1)
                            pe.wait_ge(bm_free, use_o(b, i, 2) + 1)
                            pe.wait_ge(m_ready, NT * b + (i + 1))
                            for k in range(CH):
                                mm = pe.transpose(mis[:, k * P:(k + 1) * P], HB[:, k * P:(k + 1) * P], ident[:, :])
                            mm.then_inc(bm_full, 1)
                            pe.wait_ge(bm_free, use_o(b, i, 3) + 1)
                            for k in range(CH):
                                mm = pe.matmul(mis[:, 0:E], MTs[:, k, :], WG[:, k, :], start=(k == 0), stop=(k == CH - 1))
                            mm.then_inc(bm_full, 1)

                @block.vector
                def _(dve):
                    dve.sem_inc(bm_free, 1)
                    dve.sem_inc(s_full, 2 * G * NT)
                    dve.sem_inc(bp_ready, 4)
                    dve.sem_inc(bpt_full, RING)
                    dve.sem_inc(bav, RING)
                    dve.sem_inc(bpl_ready, 2)
                    dve.sem_inc(by_ready, 1)
                    dve.sem_inc(stored_x[0], 16)
                    dve.sem_inc(stored_x[1], 16)
                    dve.wait_ge(v_ones, 3)
                    steps = NT * 2 + NG + NT * 2
                    with dve.Fori(0, B) as b:
                        step = [0]

                        def chain(ins):
                            step[0] += 1
                            ins.then_inc(dve_b, 1)
                            dve.wait_ge(dve_b, steps * b + step[0])

                        def norm(src, i, var, root, done):
                            chain(dve.bn_stats(bst[:, :], src))
                            dve.sem_inc(passed, 1)
                            dve.bn_aggr(mv[:, :], bst[:, :]).then_inc(var, 1)
                            dve.wait_ge(var, NT * b + (i + 1))
                            dve.wait_ge(root, NT * b + (i + 1))
                            chain(dve.reciprocal(sd[:, 1:2], sd[:, 0:1]))
                            dve.tensor_scalar(XN[:, 0, :], src, mv[:, 0:1], sd[:, 1:2], ALU.subtract, ALU.mult).then_inc(done, 1)

                        for i in range(NT):
                            norm(X[:, bass.ds(NT * b + i, 1), :].rearrange("p a c -> p (a c)"), i, var1, sd1, n1_ready)
                            dve.wait_ge(h_ready, NT * b + (i + 1))
                        for u in range(2 * CH):
                            dve.wait_ge(bhi, 4 * b + (u + 1))
                            dve.scalar_tensor_tensor(LO[:, u, :], sP[u % 4][:, :], float(D) ** -0.5 if u < CH else 1.0,
                                                     HI[:, u, :], ALU.mult, ALU.subtract).then_inc(blo, 1)
                        for v in range(NT // 2):
                            dve.wait_ge(bvh_ready, 2 * b + (v + 1))
                            for i in range(2):
                                ins = dve.tensor_tensor(VL[:, 2 * v + i, :, 0:D],
                                                        sP[v][:, i * C:(i + 1) * C].rearrange("p (h d) -> p h d", d=D),
                                                        VH[:, 2 * v + i, :, 0:D], ALU.subtract)
                            ins.then_inc(v_ready, 1)

                        def maximum(tc):
                            dve.wait_ge(s_full, b * TC + (2 * G * NT + tc + 1))
                            dve.tensor_reduce(nm[:, tc % RING:tc % RING + 1], sP[tc % 4][:, :], AX.X, ALU.max,
                                              negate=True).then_inc(nm_ready, 1)

                        def low(tc):
                            dve.wait_ge(bph_ready, b * TC + (tc + 1))
                            dve.tensor_tensor(PL[:, tc % RING, :], PTP[tc % 2][:, :], PH[:, tc % RING, :],
                                              ALU.subtract).then_inc(bpl_ready, 1)

                        def normalise(g):
                            dve.wait_ge(bav, b * TC + (NT * G * (g + 1) + RING))
                            chain(dve.reciprocal(rin[:, :, :], avP[:, :, :, D]))
                            dve.tensor_tensor(Y[:, :, G * g * D:G * (g + 1) * D].rearrange("p i (j d) -> p i j d", d=D),
                                              avP[:, :, :, 0:D], rin[:, :, :].unsqueeze(3).broadcast_to([P, NT, G, D]),
                                              ALU.mult).then_inc(by_ready, 1)

                        for tc in range(-AHEAD, TC):
                            if tc + AHEAD < TC:
                                maximum(tc + AHEAD)
                            if tc >= 0:
                                low(tc)
                            if tc > BEHIND and (tc - BEHIND + 1) % (G * NT) == 0:
                                normalise((tc - BEHIND + 1) // (G * NT) - 1)
                        normalise(NG - 1)

                        for i in range(NT):
                            dve.wait_ge(bm_full, use_o(b, i, 1) + 1)
                            dve.tensor_tensor(X2[:, i % 2, :], mis[:, 0:C],
                                              X[:, bass.ds(NT * b + i, 1), :].rearrange("p a c -> p (a c)"), ALU.add).then_inc(x2_ready, 1)
                            dve.wait_ge(x2_ready, NT * b + (i + 1))
                            dve.sem_inc(bm_free, 1)
                            norm(X2[:, i % 2, :], i, var2, sd2, n2_ready)
                            dve.wait_ge(bm_full, use_o(b, i, 3) + 1)
                            dve.tensor_copy(LG[:, bass.ds(NT * b + i, 1), :].rearrange("p a c -> p (a c)"), mis[:, 0:E]).then_inc(lg_ready, 1)
                            dve.wait_ge(lg_ready, NT * b + (i + 1))
                            dve.sem_inc(bm_free, 1)
                        assert step[0] == steps, step[0]
                    dve.wait_ge(stored_x[0], 16 + 8 * N)
                    dve.wait_ge(stored_x[1], 16 + 8 * N)


        with ExitStack() as ctx:
            W2S = sb(ctx, "W2S", [P, E, FC, C])
            HS = sb(ctx, "HS", [P, 2, F])
            HT = sb(ctx, "HT", [P, 2, F])
            B1S = sb(ctx, "B1S", [3, E * F], BF16)
            B2S = sb(ctx, "B2S", [3, E * C], BF16)
            tri = sb(ctx, "tri", [P, P], BF16)
            ones = sb(ctx, "ones", [P, P], BF16)
            selb = sb(ctx, "selb", [P, N * E], BF16)
            keys = sb(ctx, "keys", [P, N])
            tilen = sb(ctx, "tilen", [P, SLOTS])
            intsc = sb(ctx, "intsc", [P, N + SLOTS], mybir.dt.int32)
            idx = sb(ctx, "idx", [P, 2, N], mybir.dt.uint32)
            expert = sb(ctx, "expert", [P, SLOTS], mybir.dt.int32)
            gate = sb(ctx, "gate", [P, 2, N])
            bst = sb(ctx, "bstc", [P, 6])
            mv = sb(ctx, "mvc", [P, 2, 2])
            sd = sb(ctx, "sdc", [P, 2, 2])
            hP = [ctx.enter_context(nc.psum_tensor(f"hP{i}", [P, F], F32)) for i in range(2)]
            hTP = ctx.enter_context(nc.psum_tensor("hTP", [P, F], F32))
            yP = ctx.enter_context(nc.psum_tensor("yP", [P, 512], F32))
            tmp = [HS[:, n // 4, (n % 4) * 256:(n % 4) * 256 + N * E].rearrange("p (n e) -> p n e", e=E) for n in range(8)]
            cmp_e = HT[:, 0, 0:E * N].rearrange("p (e n) -> p e n", e=E)
            cmp_s = HT[:, 1, 0:SLOTS * E].rearrange("p (s e) -> p s e", e=E)
            vec = [HT[:, 0, 512 + N * n:512 + N * n + N] for n in range(6)]
            ev = [HT[:, 0, 768 + E * n:768 + E * n + E] for n in range(6)]
            b32 = HT[:, 0, 832:832 + 80]
            bp = sb(ctx, "bp", [P, 3, 80], BF16)
            if N * C >= 20 * C:
                XR = X
            else:
                XR = sb(ctx, "XR", [P, 20, C])
            XS = XR[:, 0:2, :]
            XT = XR[:, 2:4, :].rearrange("p s (k t) -> p s k t", k=CH)
            YS = XR[:, 4:6, :]
            RG = 4
            Y1 = XR[:, 6:6 + RG, :]
            Y2 = XR[:, 10:10 + RG, :]
            XB = XR[:, 14:14 + RG, :]
            ZO = XR[:, 18:20, :]

            w2_loaded = sem("w2_loaded")
            cb_loaded = sem("cb_loaded")
            cb_moved = sem("cb_moved")
            cst = sem("cst")
            lg_off = sem("lg_off")
            lg_exp = sem("lg_exp")
            sel_ready = sem("sel_ready")
            rank_full = sem("rank_full")
            parts_ready = sem("parts_ready")
            idx_ready = sem("idx_ready")
            scattered = sem("scattered")
            xs_loaded = [sem(f"xs_loaded{i}") for i in range(2)]
            xt_full = sem("xt_full")
            xt_ready = sem("xt_ready")
            h_full = sem("h_full")
            h_ready2 = sem("h_ready2")
            ht_full = sem("ht_full")
            ht_ready = sem("ht_ready")
            y_full = sem("y_full")
            ys_ready = sem("ys_ready")
            ys_stored = [sem(f"ys_stored{i}") for i in range(2)]
            gathered = [sem(f"gathered{i}") for i in range(RG)]
            xb_loaded = [sem(f"xb_loaded{i}") for i in range(RG)]
            z_ready = sem("z_ready")
            var3 = sem("var3")
            sd3 = sem("sd3")
            o_ready = sem("o_ready")
            o_stored = [sem(f"o_stored{i}") for i in range(2)]
            dve_c = sem("dve_c")
            HALF = SLOTS // 2

            with nc.Block() as block:
                @block.sync
                def _(sp):
                    sp.dma_start(b32[:, 0:64], a["L0_ffn_b1"].rearrange("e f -> (e f)").rearrange("(p j) -> p j", p=P)).then_inc(cb_loaded, 16)
                    sp.dma_start(b32[:, 64:80], a["L0_ffn_b2"].rearrange("e f -> (e f)").rearrange("(p j) -> p j", p=P)).then_inc(cb_loaded, 16)
                    for e in range(E):
                        sp.dma_start(W2S[:, e, :, :], a["L0_ffn_W2"][e].rearrange("(k p) c -> p k c", p=P)).then_inc(w2_loaded, 16)
                    sp.wait_ge(parts_ready, 3)
                    for r in range(3):
                        sp.dma_start(B1S[r:r + 1, :], bp[:, r, 0:64]).then_inc(cb_moved, 16)
                        sp.dma_start(B2S[r:r + 1, :], bp[:, r, 64:80]).then_inc(cb_moved, 16)
                    sp.wait_ge(scattered, 16 * 2 * N)

                    def load(q, s):
                        sp.wait_ge(xt_full, 2 * q + (s + 1))
                        sp.dma_start(XS[:, s, :], xs_d[bass.ds(2 * q + s, 1)].rearrange("a p c -> (a p) c")).then_inc(xs_loaded[s], 16)

                    def store(q, s):
                        sp.wait_ge(ys_ready, 2 * q + (s + 2))
                        sp.dma_start(ys_d[bass.ds(2 * q + s, 1)].rearrange("a p c -> (a p) c"), YS[:, s, :]).then_inc(ys_stored[s], 16)

                    load(0, 0)
                    load(0, 1)
                    with sp.Fori(0, HALF - 1) as q:
                        for s in range(2):
                            load(q + 1, s)
                            store(q, s)
                    store(HALF - 1, 0)
                    store(HALF - 1, 1)
                    for n in range(N):
                        if n >= RG:
                            sp.wait_ge(z_ready, n - RG + 1)
                        sp.dma_start(XB[:, n % RG, :], x2_d[n // NT, :, n % NT, :]).then_inc(xb_loaded[n % RG], 16)
                        if n >= 2:
                            sp.wait_ge(o_ready, n - 1)
                            sp.dma_start(out_t[(n - 2) // NT, :, (n - 2) % NT, :], ZO[:, n % 2, :]).then_inc(o_stored[n % 2], 16)
                    for n in range(N - 2, N):
                        sp.wait_ge(o_ready, n + 1)
                        sp.dma_start(out_t[n // NT, :, n % NT, :], ZO[:, n % 2, :]).then_inc(o_stored[n % 2], 16)
                    for s in range(2):
                        sp.wait_ge(o_stored[s], 16 * N // 2)

                @block.gpsimd
                def _(pool):
                    pool.memset(tri[:, :], 1.0).then_inc(cst, 1)
                    pool.memset(ones[:, :], 1.0).then_inc(cst, 1)
                    pool.iota(intsc[:, 0:N], pattern=[[P, N]], base=0, channel_multiplier=0).then_inc(cst, 1)
                    pool.iota(intsc[:, N:N + SLOTS], pattern=[[1, SLOTS]], base=0, channel_multiplier=0).then_inc(cst, 1)
                    pool.wait_ge(cst, 4)
                    pool.affine_select(out=tri[:, :], in_=tri[:, :], compare_op=ALU.is_gt, fill=0.0,
                                       base=0, pattern=[[1, P]], channel_multiplier=-1).then_inc(cst, 1)
                    pool.tensor_copy(keys[:, :], intsc[:, 0:N]).then_inc(cst, 1)
                    pool.tensor_copy(tilen[:, :], intsc[:, N:N + SLOTS]).then_inc(cst, 1)
                    pool.wait_ge(idx_ready, 1)
                    for n in range(N):
                        for k in range(2):
                            pool.indirect_dma_start(out=xs_d.rearrange("s p c -> (s p) c"),
                                                    out_offset=bass.IndirectOffsetOnAxis(ap=idx[:, k, n:n + 1], axis=0),
                                                    in_=X[:, n, :], in_offset=None).then_inc(scattered, 16)
                    for s in range(2):
                        pool.wait_ge(ys_stored[s], 16 + 16 * HALF)
                    for n in range(N):
                        if n >= RG:
                            pool.wait_ge(z_ready, n - RG + 1)
                        for k, dst in enumerate((Y1, Y2)):
                            pool.indirect_dma_start(out=dst[:, n % RG, :], out_offset=None,
                                                    in_=ys_d.rearrange("s p c -> (s p) c"),
                                                    in_offset=bass.IndirectOffsetOnAxis(ap=idx[:, k, n:n + 1], axis=0)).then_inc(gathered[n % RG], 16)

                @block.scalar
                def _(act):
                    act.wait_ge(lg_off, 1)
                    act.activation(tmp[1], tmp[0], ACT.Exp).then_inc(lg_exp, 1)

                    def body(q, s):
                        j1 = 2 * q + (s + 1)
                        act.wait_ge(xt_full, j1 + 2)
                        act.activation(XT[:, s, :, :].rearrange("p k t -> p (k t)"), mis[:, 0:C], ACT.Copy).then_inc(xt_ready, 1)

                    def gelu(q, s):
                        j1 = 2 * q + (s + 1)
                        act.wait_ge(h_full, j1)
                        act.wait_ge(ht_full, 2 * j1)
                        act.activation(HS[:, s, :], hP[s][:, :], ACT.Gelu_apprx_tanh).then_inc(h_ready2, 1)

                    body(0, 0)
                    with act.Fori(0, HALF - 1) as q:
                        body(q, 1)
                        gelu(q, 0)
                        body(q + 1, 0)
                        gelu(q, 1)
                    body(HALF - 1, 1)
                    gelu(HALF - 1, 0)
                    gelu(HALF - 1, 1)
                    for n in range(N):
                        act.wait_ge(var3, n + 1)
                        act.activation(sd[:, n % 2, 0:1], mv[:, n % 2, 1:2], ACT.Sqrt, bias=epsc[:, :]).then_inc(sd3, 1)

                @block.tensor
                def _(pe):
                    pe.wait_ge(cst, 7)
                    pe.wait_ge(sel_ready, 1)
                    pe.matmul(hP[0][:, 0:N * E], tri[:, :], selb[:, :], start=True, stop=True)
                    pe.matmul(hP[1][:, 0:N * E], ones[:, :], selb[:, :], start=True, stop=True).then_inc(rank_full, 1)
                    pe.wait_ge(idx_ready, 1)
                    pe.wait_ge(cb_moved, 96)
                    pe.wait_ge(w1_loaded, 16 * E)
                    pe.wait_ge(w2_loaded, 16 * E)
                    w1f = W1S[:, :, :, :].rearrange("p e k f -> p (e k f)")
                    w2f = W2S[:, :, :, :].rearrange("p e k c -> p (e k c)")

                    def turn_x(q, s):
                        j1 = 2 * q + (s + 1)
                        pe.wait_ge(xs_loaded[s], 16 * q + 16)
                        pe.wait_ge(xt_ready, j1)
                        for k in range(CH):
                            mm = pe.transpose(mis[:, k * P:(k + 1) * P], XS[:, s, k * P:(k + 1) * P], ident[:, :])
                        mm.then_inc(xt_full, 1)

                    def hidden(q, s, half, e):
                        j1 = 2 * q + (s + 1)
                        if half == 0:
                            pe.wait_ge(xt_ready, j1 + 1)
                            pe.wait_ge(h_ready2, j1)
                        dst = hP[s][:, half * 512:(half + 1) * 512]
                        for k in range(CH):
                            pe.matmul(dst, XT[:, s, k, :], w1f[:, bass.ds(e * (CH * F) + (k * F + half * 512), 512)],
                                      start=(k == 0), stop=False)
                        mm = pe.matmul(dst, ones[0:3, :], B1S[:, bass.ds(e * F + half * 512, 512)], start=False, stop=True)
                        if half == 1:
                            mm.then_inc(h_full, 1)

                    def turn_h(q, s):
                        j1 = 2 * q + (s + 1)
                        pe.wait_ge(h_ready2, j1 + 2)
                        for half in range(2):
                            pe.wait_ge(ht_ready, 2 * j1 + (half - 1))
                            for k in range(FC // 2 * half, FC // 2 * (half + 1)):
                                mm = pe.transpose(hTP[:, k * P:(k + 1) * P], HS[:, s, k * P:(k + 1) * P], ident[:, :])
                            mm.then_inc(ht_full, 1)

                    def outputs(q, s, e):
                        j1 = 2 * q + (s + 1)
                        pe.wait_ge(ys_ready, j1)
                        for k in range(FC):
                            if k % (FC // 2) == 0:
                                pe.wait_ge(ht_ready, 2 * j1 + (1 + k // (FC // 2)))
                            pe.matmul(yP[:, 0:C], HT[:, s, k * P:(k + 1) * P], w2f[:, bass.ds(e * (FC * C) + k * C, C)],
                                      start=(k == 0), stop=False)
                        pe.matmul(yP[:, 0:C], ones[0:3, :], B2S[:, bass.ds(e * C, C)], start=False, stop=True).then_inc(y_full, 1)

                    def expert_of(j):
                        return pe.value_load(expert[0:1, bass.ds(j, 1)], min_val=0, max_val=E - 1)

                    def step(q, s, pq, ps):
                        e = expert_of(2 * q + s)
                        hidden(q, s, 0, e)
                        if pq is not None:
                            turn_h(pq, ps)
                        hidden(q, s, 1, e)
                        return e

                    turn_x(0, 0)
                    step(0, 0, None, None)
                    turn_x(0, 1)
                    with pe.Fori(0, HALF - 1) as q:
                        step(q, 1, q, 0)
                        turn_x(q + 1, 0)
                        outputs(q, 0, expert_of(2 * q))
                        step(q + 1, 0, q, 1)
                        turn_x(q + 1, 1)
                        outputs(q, 1, expert_of(2 * q + 1))
                    last = HALF - 1
                    step(last, 1, last, 0)
                    outputs(last, 0, expert_of(2 * last))
                    turn_h(last, 1)
                    outputs(last, 1, expert_of(2 * last + 1))

                @block.vector
                def _(dve):
                    step = [0]

                    def chain(ins):
                        step[0] += 1
                        ins.then_inc(dve_c, 1)
                        dve.wait_ge(dve_c, step[0])

                    dve.sem_inc(xt_full, 2)
                    dve.sem_inc(xt_ready, 1)
                    dve.sem_inc(h_ready2, 2)
                    dve.sem_inc(ht_full, 4)
                    dve.sem_inc(ht_ready, 2)
                    dve.sem_inc(ys_ready, 1)
                    dve.sem_inc(ys_stored[0], 16)
                    dve.sem_inc(ys_stored[1], 16)

                    def over_e(v):
                        return v.unsqueeze(2).broadcast_to([P, N, E])

                    dve.wait_ge(cb_loaded, 32)
                    rest = HT[:, 0, 912:992]
                    chain(dve.tensor_copy(bp[:, 0, :], b32))
                    dve.sem_inc(parts_ready, 1)
                    chain(dve.tensor_tensor(rest, b32, bp[:, 0, :], ALU.subtract))
                    chain(dve.tensor_copy(bp[:, 1, :], rest))
                    dve.sem_inc(parts_ready, 1)
                    chain(dve.tensor_tensor(rest, rest, bp[:, 1, :], ALU.subtract))
                    chain(dve.tensor_copy(bp[:, 2, :], rest))
                    dve.sem_inc(parts_ready, 1)

                    chain(dve.tensor_reduce(vec[0], LG[:, :, :], AX.X, ALU.max))
                    dve.tensor_tensor(tmp[0], LG[:, :, :], over_e(vec[0]), ALU.subtract).then_inc(lg_off, 1)
                    dve.wait_ge(lg_exp, 1)
                    chain(dve.tensor_reduce(vec[1], tmp[1], AX.X, ALU.add))
                    chain(dve.reciprocal(vec[2], vec[1]))
                    chain(dve.tensor_tensor(tmp[2], tmp[1], over_e(vec[2]), ALU.mult))

                    def prefix(src, bufs, n, at):
                        d, turn = 1, 0
                        while d < n:
                            dst = bufs[turn]
                            chain(dve.tensor_copy(at(dst, 0, d), at(src, 0, d)))
                            chain(dve.tensor_tensor(at(dst, d, n), at(src, d, n), at(src, 0, n - d), ALU.add))
                            src, turn, d = dst, 1 - turn, 2 * d
                        return src

                    probs, top_p = tmp[2], [vec[3], vec[4]]
                    first = [tmp[5], tmp[6]]
                    for k in range(2):
                        chain(dve.tensor_reduce(top_p[k], probs, AX.X, ALU.max))
                        chain(dve.tensor_tensor(tmp[0], probs, over_e(top_p[k]), ALU.is_equal))
                        count = prefix(tmp[0], [tmp[3], tmp[4]], E, lambda v, lo, hi: v[:, :, lo:hi])
                        chain(dve.scalar_tensor_tensor(first[k], count, 1.0, tmp[0], ALU.is_equal, ALU.mult))
                        if k == 0:
                            chain(dve.scalar_tensor_tensor(tmp[1], first[0], -2.0, probs, ALU.mult, ALU.add))
                            probs = tmp[1]
                    chain(dve.tensor_tensor(selb[:, :].rearrange("p (n e) -> p n e", e=E), first[0], first[1], ALU.add))
                    dve.sem_inc(sel_ready, 1)
                    chain(dve.tensor_tensor(vec[0], vec[3], vec[4], ALU.add))
                    chain(dve.reciprocal(vec[1], vec[0]))
                    for k in range(2):
                        chain(dve.tensor_tensor(gate[:, k, :], top_p[k], vec[1], ALU.mult))

                    dve.wait_ge(rank_full, 1)
                    dve.wait_ge(cst, 7)
                    tot = tmp[0]
                    chain(dve.tensor_copy(tot, hP[1][:, 0:N * E].rearrange("p (n e) -> p n e", e=E)))
                    inc = prefix(tot, [tmp[1], tmp[2]], N, lambda v, lo, hi: v[:, lo:hi, :])
                    chain(dve.tensor_copy(ev[0], inc[:, N - 1, :]))
                    chain(dve.tensor_tensor(cmp_e, ev[0].unsqueeze(2).broadcast_to([P, E, N]),
                                            keys[:, :].unsqueeze(1).broadcast_to([P, E, N]), ALU.is_gt))
                    chain(dve.tensor_reduce(ev[1], cmp_e, AX.X, ALU.add))
                    tinc = prefix(ev[1], [ev[2], ev[3]], E, lambda v, lo, hi: v[:, lo:hi])
                    chain(dve.tensor_tensor(ev[4], tinc, ev[1], ALU.subtract))
                    chain(dve.tensor_tensor(tmp[3], inc, tot, ALU.subtract))
                    chain(dve.tensor_tensor(tmp[4], hP[0][:, 0:N * E].rearrange("p (n e) -> p n e", e=E), tmp[3], ALU.add))
                    chain(dve.scalar_tensor_tensor(tmp[7], ev[4].unsqueeze(1).broadcast_to([P, N, E]), float(P), tmp[4],
                                                   ALU.mult, ALU.add))
                    for k in range(2):
                        chain(dve.tensor_tensor(tmp[3], first[k], tmp[7], ALU.mult))
                        chain(dve.tensor_reduce(vec[5], tmp[3], AX.X, ALU.add))
                        chain(dve.tensor_copy(idx[:, k, :], vec[5]))
                    chain(dve.tensor_tensor(cmp_s, tilen[:, :].unsqueeze(2).broadcast_to([P, SLOTS, E]),
                                            ev[4].unsqueeze(1).broadcast_to([P, SLOTS, E]), ALU.is_ge))
                    count = HT[:, 1, E * SLOTS:E * SLOTS + SLOTS]
                    chain(dve.tensor_reduce(count, cmp_s, AX.X, ALU.add))
                    chain(dve.tensor_scalar(expert[:, :], count, -1.0, None, ALU.add))
                    dve.sem_inc(idx_ready, 1)

                    def copies(q, s):
                        j1 = 2 * q + (s + 1)
                        for half in range(2):
                            dve.wait_ge(ht_full, 2 * j1 + (3 + half))
                            dve.tensor_copy(HT[:, s, half * 512:(half + 1) * 512], hTP[:, half * 512:(half + 1) * 512]).then_inc(ht_ready, 1)

                    def result(q, s):
                        j1 = 2 * q + (s + 1)
                        dve.wait_ge(y_full, j1)
                        dve.wait_ge(ys_stored[s], 16 * q + 16)
                        dve.tensor_copy(YS[:, s, :], yP[:, 0:C]).then_inc(ys_ready, 1)

                    with dve.Fori(0, HALF) as q:
                        for s in range(2):
                            copies(q, s)
                            result(q, s)

                    for n in range(N):
                        z = Y1[:, n % RG, :]
                        dve.wait_ge(gathered[n % RG], 32 * (n // RG + 1))
                        dve.wait_ge(xb_loaded[n % RG], 16 * (n // RG + 1))
                        chain(dve.scalar_tensor_tensor(XB[:, n % RG, :], z, gate[:, 0, n:n + 1], XB[:, n % RG, :], ALU.mult, ALU.add))
                        if n >= 2:
                            dve.wait_ge(o_stored[n % 2], 16 * (n // 2))
                        chain(dve.scalar_tensor_tensor(ZO[:, n % 2, :], Y2[:, n % RG, :], gate[:, 1, n:n + 1], XB[:, n % RG, :],
                                                       ALU.mult, ALU.add))
                        dve.sem_inc(z_ready, 1)
                        chain(dve.bn_stats(bst[:, :], ZO[:, n % 2, :]))
                        dve.bn_aggr(mv[:, n % 2, :], bst[:, :]).then_inc(var3, 1)
                        dve.wait_ge(var3, n + 1)
                        dve.wait_ge(sd3, n + 1)
                        chain(dve.reciprocal(sd[:, n % 2, 1:2], sd[:, n % 2, 0:1]))
                        dve.tensor_scalar(ZO[:, n % 2, :], ZO[:, n % 2, :], mv[:, n % 2, 0:1], sd[:, n % 2, 1:2],
                                          ALU.subtract, ALU.mult).then_inc(o_ready, 1)


def kernel(**inputs):
    import numpy as np
    import concourse.bacc as bacc
    from concourse.bass_utils import run_bass_kernel_spmd

    nc = bacc.Bacc("TRN2", target_bir_lowering=False, num_devices=1)
    arrays, args = {}, {}
    for name, value in inputs.items():
        v = np.ascontiguousarray(value)
        if v.ndim == 0:
            v = v.reshape(1)
        arrays[f"in_{name}"] = v
        args[name] = nc.dram_tensor(f"in_{name}", v.shape, mybir.dt.from_np(v.dtype), kind="ExternalInput").ap()
    shape = inputs["L0_attn_x"].shape
    out = nc.dram_tensor("out_x", shape, F32, kind="ExternalOutput").ap()
    build(nc, args, out)
    return run_bass_kernel_spmd(nc, [arrays], core_ids=[0]).results[0]["out_x"]
```

```python
from contextlib import ExitStack
from math import factorial

import concourse.bass as bass
from concourse import mybir

ALU = mybir.AluOpType
ACT = mybir.ActivationFunctionType
AX = mybir.AxisListType
F32 = mybir.dt.float32
F16 = mybir.dt.float16
BF16 = mybir.dt.bfloat16

P = 128
EPS = 1e-5
MASKED = 1e30
SINH = [1.0 / factorial(2 * k + 1) for k in range(8)]


def build(nc, a, out):
    x_d = a["L0_attn_x"]
    B, T, C = x_d.shape
    H = a["L0_attn_log_k"].shape[0]
    D = C // H
    E, _, F = a["L0_ffn_W1"].shape
    NT = T // P
    N = B * NT
    CH = C // P
    FC = F // P
    HPC = H // CH
    G = 4
    NG = H // G
    R3 = 3 * D
    QKW = 2 * C
    VAI = C + H + 1
    WCOL = QKW + VAI
    W = [P * (i + 1) for i in range(NT)]
    OFF = {3: 0, 2: 512, 0: 896, 1: 1024}
    SW = sum(W)
    REGIONS = [[3], [2, 0], [1]]
    assert D == 16 and NT == 4 and T == 512 and H == 16 and C == 256 and SW == 1280

    x_t = x_d.rearrange("b (t p) c -> b p t c", p=P)
    out_t = out.rearrange("b (t p) c -> b p t c", p=P)

    SLOTS = 2 * N + E
    x2_d = nc.dram_tensor("x2_scratch", [B, P, NT, C], F32, kind="Internal").ap()

    xs_d = nc.dram_tensor("rows_scratch", [SLOTS, P, C], F32, kind="Internal").ap()
    ys_d = nc.dram_tensor("results_scratch", [SLOTS, P, C], F32, kind="Internal").ap()

    with ExitStack() as top:
        def sem(name):
            return top.enter_context(nc.semaphore(name))

        def sb(ctx, name, shape, dt=F32):
            return ctx.enter_context(nc.sbuf_tensor(name, shape, dt))

        X = sb(top, "X", [P, N, C])
        ident = sb(top, "ident", [P, P])
        identb = sb(top, "identb", [P, P], BF16)
        neg1 = sb(top, "neg1", [P, 1])
        epsc = sb(top, "epsc", [P, 1])
        mis = top.enter_context(nc.psum_tensor("misc", [P, 512], F32))

        setup_pool = sem("setup_pool")
        passed = sem("passed")

        with ExitStack() as ctx:
            WT = sb(ctx, "WT", [P, CH, WCOL])
            WOT = sb(ctx, "WOT", [P, CH, C])
            mask = sb(ctx, "mask", [P, P], BF16)
            bias = sb(ctx, "bias", [P, WCOL])
            bout = sb(ctx, "bout", [P, C])
            thr = sb(ctx, "thr", [P, 1])
            s2 = sb(ctx, "s2", [P, 1])
            rcurv = sb(ctx, "rcurv", [P, H])
            XI = sb(ctx, "XI", [P, NT, C])
            AI = sb(ctx, "AI", [P, 2, NT, H + 1])
            V = sb(ctx, "V", [P, H, D + 1])
            st = sb(ctx, "st", [P, 10, NT * 2 * H])
            stat = sb(ctx, "stat", [P, NT, 5 * H])
            root = sb(ctx, "root", [P, NT, 5 * H])
            spk = sb(ctx, "spk", [P, NT])
            HI = sb(ctx, "HI", [P, 4 * CH, T], F16)
            LO = sb(ctx, "LO", [P, 4 * CH, T], F16)
            STG = sb(ctx, "STG", [P, NG, 4, 2, T], F16)
            MC = sb(ctx, "MC", [P, 2, G, SW])
            TT = sb(ctx, "TT", [P, 2, G, SW])
            PH = sb(ctx, "PH", [P, 2, SW], F16)
            PL = sb(ctx, "PL", [P, 2, SW], F16)
            VH = sb(ctx, "VH", [P, NT, H, D + 1], F16)
            VL = sb(ctx, "VL", [P, NT, H, D + 1], F16)
            mn = sb(ctx, "mn", [P, 2, G, NT])
            Y = sb(ctx, "Y", [P, NT, C])
            rin = sb(ctx, "rin", [P, NT, G])
            bst = sb(ctx, "bst", [P, NT, 6])
            mv = sb(ctx, "mv", [P, NT, 2])
            sd = sb(ctx, "sd", [P, 2, NT])
            mP = [ctx.enter_context(nc.psum_tensor(f"mP{i}", [P, 512], F32)) for i in range(2)]
            SeP = [ctx.enter_context(nc.psum_tensor(f"SeP{i}", [P, 512], F32)) for i in range(2)]
            PTP = [ctx.enter_context(nc.psum_tensor(f"PTP{i}", [P, 512], F32)) for i in range(2)] + [mis]
            avP = ctx.enter_context(nc.psum_tensor("avP", [P, NT, G, D + 1], F32))

            before = TT[:, :, :, :].rearrange("p s j w -> p (s j w)")
            QK = before[:, 0:NT * QKW].rearrange("p (i c) -> p i c", i=NT)
            SQ = before[:, NT * QKW:2 * NT * QKW].rearrange("p (i h d) -> p i h d", i=NT, d=D)
            HY = before[:, 2 * NT * QKW:3 * NT * QKW].rearrange("p (i h d) -> p i h d", i=NT, d=D)
            QE = before[:, 3 * NT * QKW:3 * NT * QKW + NT * C].rearrange("p (i c) -> p i c", i=NT)
            xT = before[:, 3 * NT * QKW + NT * C:4 * NT * QKW].rearrange("p (i k t) -> p i k t", i=NT, k=CH)
            YT = before[:, 0:CH * T].rearrange("p (k t) -> p k t", k=CH)
            z = before[:, 4 * NT * QKW:4 * NT * QKW + NT * C].rearrange("p (i c) -> p i c", i=NT)

            WL = TT[:, 0, :, :].rearrange("p g w -> p (g w)")
            WQR = WL[:, 0:6 * C].rearrange("p (r c) -> p r c", r=6)
            WOR = WL[:, 6 * C:8 * C].rearrange("p (r c) -> p r c", r=2)
            WAR = WL[:, 8 * C:9 * C]
            lk = st[:, 0, 0:H]

            a_w_loaded = sem("a_w_loaded")
            a_c_loaded = sem("a_c_loaded")
            wt_full = sem("wt_full")
            wt_free = sem("wt_free")
            sc_exp = sem("sc_exp")
            sc_one = sem("sc_one")
            sc_ln = sem("sc_ln")
            dve_a0 = sem("dve_a0")

            with nc.Block() as block:
                @block.sync
                def _(sp):
                    sp.dma_start(WQR, a["L0_attn_Wqkv"].rearrange("(r p) c -> p r c", p=P)).then_inc(a_w_loaded, 16)
                    sp.dma_start(WOR, a["L0_attn_Wout"].rearrange("(r p) c -> p r c", p=P)).then_inc(a_w_loaded, 16)
                    sp.dma_start(WAR[0:H, :], a["L0_attn_Walpha"]).then_inc(a_w_loaded, 16)
                    sp.dma_start(WAR[H:H + 1, :], a["L0_attn_Wimp"]).then_inc(a_w_loaded, 16)

                @block.scalar
                def _(act):
                    act.dma_start(lk, a["L0_attn_log_k"].partition_broadcast(P)).then_inc(a_c_loaded, 16)
                    act.dma_start(s2[:, :], a["L0_attn_qk_scale"].partition_broadcast(P)).then_inc(a_c_loaded, 16)
                    act.dma_start(thr[:, :], a["L0_attn_spike_threshold"].partition_broadcast(P)).then_inc(a_c_loaded, 16)
                    act.dma_start(bias[:, 0:3 * C], a["L0_attn_bqkv"].partition_broadcast(P)).then_inc(a_c_loaded, 16)
                    act.dma_start(bias[:, 3 * C:3 * C + H], a["L0_attn_balpha"].partition_broadcast(P)).then_inc(a_c_loaded, 16)
                    act.dma_start(bias[:, 3 * C + H:], a["L0_attn_bimp"].partition_broadcast(P)).then_inc(a_c_loaded, 16)
                    act.dma_start(bout[:, :], a["L0_attn_bout"].partition_broadcast(P)).then_inc(a_c_loaded, 16)
                    act.wait_ge(sc_one, 1)
                    act.activation(st[:, 2, 0:H], st[:, 1, 0:H], ACT.Exp).then_inc(sc_exp, 1)
                    act.activation(sd[:, 0, 0:1], s2[:, :], ACT.Exp, scale=-1.0).then_inc(sc_exp, 1)
                    act.wait_ge(sc_one, 2)
                    act.activation(st[:, 4, 0:H], st[:, 3, 0:H], ACT.Ln).then_inc(sc_ln, 1)

                @block.gpsimd
                def _(pool):
                    pool.memset(ident[:, :], 0.0).then_inc(setup_pool, 1)
                    pool.memset(mask[:, :], 0.0).then_inc(setup_pool, 1)
                    pool.memset(neg1[:, :], -1.0).then_inc(setup_pool, 1)
                    pool.memset(epsc[:, :], EPS).then_inc(setup_pool, 1)
                    pool.memset(V[:, :, :], 1.0).then_inc(setup_pool, 1)
                    pool.wait_ge(setup_pool, 5)
                    pool.affine_select(out=ident[:, :], in_=ident[:, :], compare_op=ALU.not_equal, fill=1.0,
                                       base=0, pattern=[[-1, P]], channel_multiplier=1).then_inc(setup_pool, 1)
                    pool.affine_select(out=mask[:, :], in_=mask[:, :], compare_op=ALU.is_ge, fill=MASKED,
                                       base=0, pattern=[[-1, P]], channel_multiplier=1).then_inc(setup_pool, 1)
                    pool.wait_ge(setup_pool, 7)
                    pool.tensor_copy(identb[:, :], ident[:, :]).then_inc(setup_pool, 1)

                @block.tensor
                def _(pe):
                    pe.wait_ge(setup_pool, 8)
                    pe.wait_ge(a_w_loaded, 64)
                    n = 0
                    for r in range(8):
                        src = WQR[:, r, :] if r < 6 else WOR[:, r - 6, :]
                        if n >= 1:
                            pe.wait_ge(wt_free, n)
                        for k in range(CH):
                            mm = pe.transpose(mis[:, k * P:(k + 1) * P], src[:, k * P:(k + 1) * P], ident[:, :])
                        mm.then_inc(wt_full, 1)
                        n += 1
                    pe.wait_ge(wt_free, n)
                    for k in range(CH):
                        mm = pe.transpose(mis[:, k * 32:k * 32 + H + 1], WAR[0:H + 1, k * P:(k + 1) * P],
                                          ident[0:H + 1, 0:H + 1])
                    mm.then_inc(wt_full, 1)

                @block.vector
                def _(dve):
                    step = [0]

                    def chain(ins):
                        step[0] += 1
                        ins.then_inc(dve_a0, 1)
                        dve.wait_ge(dve_a0, step[0])

                    dve.wait_ge(a_c_loaded, 112)
                    chain(dve.tensor_scalar(st[:, 9, 0:H], lk, -1.0, None, ALU.mult))
                    chain(dve.tensor_tensor(st[:, 8, 0:H], lk, st[:, 9, 0:H], ALU.max))
                    dve.tensor_scalar(st[:, 1, 0:H], st[:, 8, 0:H], -1.0, None, ALU.mult).then_inc(sc_one, 1)
                    dve.wait_ge(sc_exp, 2)
                    dve.tensor_scalar(st[:, 3, 0:H], st[:, 2, 0:H], 1.0, None, ALU.add).then_inc(sc_one, 1)
                    chain(dve.tensor_scalar(sd[:, 1, 0:1], sd[:, 0, 0:1], 1.0, None, ALU.add))
                    chain(dve.reciprocal(sd[:, 0, 0:1], sd[:, 1, 0:1]))
                    chain(dve.tensor_scalar(sd[:, 1, 0:1], sd[:, 0, 0:1], 1.5, None, ALU.mult))
                    chain(dve.tensor_tensor(s2[:, :], sd[:, 1, 0:1], sd[:, 1, 0:1], ALU.mult))
                    dve.wait_ge(sc_ln, 1)
                    chain(dve.tensor_scalar(st[:, 5, 0:H], lk, 0.0, None, ALU.max))
                    chain(dve.tensor_tensor(st[:, 6, 0:H], st[:, 5, 0:H], st[:, 4, 0:H], ALU.add))
                    chain(dve.tensor_scalar(st[:, 7, 0:H], st[:, 6, 0:H], 1e-6, None, ALU.add))
                    chain(dve.reciprocal(rcurv[:, :], st[:, 7, 0:H]))
                    for r in range(8):
                        dve.wait_ge(wt_full, r + 1)
                        dst = WT[:, :, r * P:(r + 1) * P] if r < 6 else WOT[:, :, (r - 6) * P:(r - 5) * P]
                        dve.tensor_copy(dst, mis[:, 0:C].rearrange("p (k c) -> p k c", k=CH)).then_inc(wt_free, 1)
                    dve.wait_ge(wt_full, 9)
                    dve.tensor_copy(WT[:, :, 3 * C:WCOL],
                                    mis[:, 0:32 * CH].rearrange("p (k c) -> p k c", k=CH)[:, :, 0:H + 1]).then_inc(wt_free, 1)

            x_loaded = sem("x_loaded")
            x_used = sem("x_used")
            yt_full = sem("yt_full")
            yt_ready = sem("yt_ready")
            out_full = sem("out_full")
            x_turned = sem("x_turned")
            xT_ready = sem("xT_ready")
            pq_full = sem("pq_full")
            pv_full = sem("pv_full")
            op_full = sem("op_full")
            ai_ready = sem("ai_ready")
            qk_ready = sem("qk_ready")
            ea_ready = sem("ea_ready")
            sq_ready = sem("sq_ready")
            qs_ready = sem("qs_ready")
            qe_ready = sem("qe_ready")
            stat_ready = sem("stat_ready")
            root_ready = sem("root_ready")
            space_ready = sem("space_ready")
            hy_ready = sem("hy_ready")
            hi_ready = sem("hi_ready")
            lo_ready = sem("lo_ready")
            first_ready = [sem(f"first_ready{j}") for j in range(G)]
            stage_ready = [None] + [sem(f"stage_ready{s}") for s in range(1, NG)]
            m_full = sem("m_full")
            m_free = sem("m_free")
            msq_ready = sem("msq_ready")
            rt_ready = sem("rt_ready")
            sum_ready = sem("sum_ready")
            dsq_ready = sem("dsq_ready")
            dsum_ready = sem("dsum_ready")
            ln_ready = sem("ln_ready")
            hyp_ready = sem("hyp_ready")
            se_full = sem("se_full")
            comb_ready = sem("comb_ready")
            p_ready = sem("p_ready")
            pt_full = sem("pt_full")
            ph_ready = sem("ph_ready")
            aph_ready = sem("aph_ready")
            pt_ready = sem("pt_ready")
            vh_ready = sem("vh_ready")
            vl_ready = sem("vl_ready")
            av_tile = sem("av_tile")
            y_ready = sem("y_ready")
            sd_ready = sem("sd_ready")
            var_ready = sem("var_ready")
            dve_a = sem("dve_a")
            SD = 16 * 5
            SE = H * NT
            MSQ = H - G // 2
            SUM = H - G // 2

            def msq_count(g, j):
                return j + 1 if g == 0 else G * g + j + 1 - G // 2

            def sum_count(g, j):
                return G * g + j + 1 - G // 2

            opP = [mP[0], mP[1], SeP[0], SeP[1]]

            with nc.Block() as block:
                @block.sync
                def _(sp):
                    with sp.Fori(0, B) as b:
                        sp.wait_ge(x_used, b + 1)
                        sp.dma_start(XI[:, :, :], x_t[bass.ds(b, 1)].rearrange("a p t c -> (a p) t c")).then_inc(x_loaded, 16)
                        sp.wait_ge(hi_ready, 2 * NT * b + 2 * NT)
                        sp.wait_ge(lo_ready, 2 * NT * b + 2 * NT)
                        for g in range(NG):
                            slot, c = g, g // 2
                            sp.wait_ge(se_full, b * (H * NT) + G * NT * (g + 1))
                            for j in range(G):
                                par, s = j % 2, j // 2
                                src = 16 * ((G * g + j) % HPC)
                                dst = 64 * par
                                ready = first_ready[j] if g == 0 else stage_ready[slot]
                                sp.dma_start(STG[dst:dst + D, slot, :, s, :],
                                             HI[src:src + D, c:4 * CH:2, :]).then_inc(ready, 16)
                                for jj, planes in [(1, (HI, LO)), (2, (LO, HI))]:
                                    dst = 64 * par + D * jj
                                    for qk in range(2):
                                        sp.dma_start(STG[dst:dst + D, slot, qk:4:2, s, :],
                                                     planes[qk][src:src + D, 2 * qk + c:4 * CH:4, :]).then_inc(ready, 16)

                @block.gpsimd
                def _(pool):
                    with pool.Fori(0, B) as b:
                        for i in range(NT):
                            pool.wait_ge(qk_ready, NT * b + (i + 1))
                            pool.tensor_tensor(SQ[:, i, :, :].rearrange("p h d -> p (h d)"), QK[:, i, :], QK[:, i, :],
                                               ALU.mult).then_inc(sq_ready, 1)
                            pool.wait_ge(ai_ready, NT * b + (i + 1))
                            pool.sem_inc(passed, 1)
                            pool.tensor_copy(VH[:, i, :, :], V[:, :, :]).then_inc(vh_ready, 1)
                            pool.wait_ge(vh_ready, NT * b + (i + 1))
                            pool.tensor_tensor(VL[:, i, :, :], V[:, :, :], VH[:, i, :, :], ALU.subtract).then_inc(vl_ready, 1)
                        pool.wait_ge(qs_ready, b + 1)
                        for i in range(NT):
                            q3 = QK[:, i, :].rearrange("p (h d) -> p h d", d=D)
                            pool.tensor_tensor(QE[:, i, :].rearrange("p (h d) -> p h d", d=D), q3[:, 0:H, :],
                                               st[:, 9, i * H:(i + 1) * H].unsqueeze(2).broadcast_to([P, H, D]),
                                               ALU.mult).then_inc(qe_ready, 1)
                        pool.wait_ge(root_ready, b + 1)
                        for i in range(NT // 2, NT):
                            q3 = QK[:, i, :].rearrange("p (h d) -> p h d", d=D)
                            pool.tensor_tensor(HY[:, i, :, :], q3,
                                               root[:, i, 0:2 * H].unsqueeze(2).broadcast_to([P, 2 * H, D]),
                                               ALU.mult).then_inc(space_ready, 1)

                        def square(g):
                            for j in range(G // 2 if g == 0 else G):
                                pool.wait_ge(m_free, b * (3 * H) + (2 + 3 * (G * g + j + 1)))
                                if g >= 2:
                                    pool.wait_ge(pt_full, b * (H * NT) + NT * (G * (g - 2) + j + 1))
                                pool.tensor_tensor(TT[:, g % 2, j, :], MC[:, g % 2, j, :], MC[:, g % 2, j, :],
                                                   ALU.mult).then_inc(msq_ready, 1)

                        def add(g):
                            for j in range(G // 2 if g == 0 else 0, G):
                                pool.wait_ge(rt_ready, H * b + (G * g + j + 1))
                                pool.tensor_tensor(TT[:, g % 2, j, :], MC[:, g % 2, j, :], TT[:, g % 2, j, :],
                                                   ALU.add).then_inc(sum_ready, 1)

                        for g in range(NG):
                            square(g)
                            add(g)

                @block.scalar
                def _(act):
                    with act.Fori(0, B) as b:
                        for h in range(2):
                            act.wait_ge(x_turned, 2 * b + (h + 1))
                            act.activation(xT[:, (NT // 2) * h:(NT // 2) * (h + 1), :, :].rearrange("p i k t -> p (i k t)"),
                                           PTP[h][:, :], ACT.Copy).then_inc(xT_ready, 1)
                        act.wait_ge(ai_ready, NT * b + NT)
                        act.activation(AI[:, 1, :, :], AI[:, 0, :, :], ACT.Exp, scale=-1.0).then_inc(ea_ready, 1)

                        def high(u):
                            r, i = u // NT, u % NT
                            act.wait_ge(op_full, 2 * NT * b + (u + 1))
                            act.activation(HI[:, 4 * r:4 * r + 4, i * P:(i + 1) * P],
                                           opP[u % 4][:, :].rearrange("p (k t) -> p k t", k=4), ACT.Copy).then_inc(hi_ready, 1)

                        act.wait_ge(stat_ready, b + 1)
                        act.activation(root[:, :, :], stat[:, :, :], ACT.Sqrt).then_inc(root_ready, 1)
                        for u in range(2 * NT):
                            high(u)

                        def roots(g):
                            for j in range(G):
                                if g == 0 and j >= G // 2:
                                    act.wait_ge(dsq_ready, b * (G // 2) + (j - G // 2 + 1))
                                else:
                                    act.wait_ge(msq_ready, b * MSQ + msq_count(g, j))
                                w = TT[:, g % 2, j, :]
                                act.activation(w, w, ACT.Sqrt, bias=neg1[:, :]).then_inc(rt_ready, 1)

                        def logs(g):
                            for j in range(G):
                                if g == 0 and j < G // 2:
                                    act.wait_ge(dsum_ready, b * (G // 2) + (j + 1))
                                else:
                                    act.wait_ge(sum_ready, b * SUM + sum_count(g, j))
                                w = TT[:, g % 2, j, :]
                                act.activation(w, w, ACT.Ln).then_inc(ln_ready, 1)
                                act.wait_ge(ln_ready, b * H + (G * g + j + 1))
                                for i in range(NT):
                                    w = TT[:, g % 2, j, OFF[i]:OFF[i] + W[i]]
                                    h = G * g + j
                                    ins = act.activation(w, w, ACT.Square, scale=root[:, i, 4 * H + h:4 * H + h + 1])
                                ins.then_inc(hyp_ready, 1)

                        def exps(g, j):
                            for i in range(NT):
                                act.wait_ge(comb_ready, b * (H * NT) + (NT * (G * g + j) + i + 3))
                                w = TT[:, g % 2, j, OFF[i]:OFF[i] + W[i]]
                                act.activation(w, w, ACT.Exp, bias=mn[:, g % 2, j, i:i + 1], scale=-1.0).then_inc(p_ready, 1)

                        def highs(j):
                            for i in range(NT):
                                tc = NT * (G * (NG - 1) + j) + i
                                act.wait_ge(pt_full, b * (H * NT) + (tc + 1))
                                act.wait_ge(av_tile, b * (H * NT) + (tc - 2 * NT + 1))
                                act.activation(PH[:, j % 2, OFF[i]:OFF[i] + W[i]], PTP[tc % 3][:, 0:W[i]],
                                               ACT.Copy).then_inc(aph_ready, 1)

                        for g in range(NG):
                            roots(g)
                            logs(g)
                            for j in range(G):
                                exps(g, j)
                                if g == NG - 1 and j >= 1:
                                    highs(j - 1)
                        highs(G - 1)

                        for h in range(2):
                            act.wait_ge(yt_full, 2 * b + (h + 1))
                            act.activation(YT[:, :, 2 * h * P:2 * (h + 1) * P],
                                           PTP[h][:, :].rearrange("p (k t) -> p k t", k=CH), ACT.Copy).then_inc(yt_ready, 1)
                        act.wait_ge(var_ready, NT * b + NT)
                        act.activation(sd[:, 0, :], mv[:, :, 1], ACT.Sqrt, bias=epsc[:, :]).then_inc(sd_ready, 1)

                @block.tensor
                def _(pe):
                    with pe.Fori(0, B) as b:
                        pe.wait_ge(x_loaded, 16 * b + 16)
                        for i in range(NT):
                            at = (i % 2) * C
                            for k in range(CH):
                                mm = pe.transpose(PTP[i // 2][:, at + k * P:at + (k + 1) * P], XI[:, i, k * P:(k + 1) * P], ident[:, :])
                            if i % 2 == 1:
                                mm.then_inc(x_turned, 1)
                        for i in range(NT):
                            pe.wait_ge(xT_ready, 2 * b + (i // 2 + 1))
                            if i >= 2:
                                pe.wait_ge(qk_ready, NT * b + (i - 1))
                            for k in range(CH):
                                mm = pe.matmul(mP[i % 2][:, 0:QKW], xT[:, i, k, :], WT[:, k, 0:QKW],
                                               start=(k == 0), stop=(k == CH - 1))
                            mm.then_inc(pq_full, 1)
                            if i >= 2:
                                pe.wait_ge(ai_ready, NT * b + (i - 1))
                            for k in range(CH):
                                mm = pe.matmul(SeP[i % 2][:, 0:WCOL - QKW], xT[:, i, k, :], WT[:, k, QKW:WCOL],
                                               start=(k == 0), stop=(k == CH - 1))
                            mm.then_inc(pv_full, 1)
                        pe.wait_ge(ai_ready, NT * b + NT)
                        for i in range(NT):
                            pe.wait_ge(qe_ready, NT * b + (i + 1))
                            for k in range(CH):
                                pe.transpose(opP[i % 4][:, k * P:(k + 1) * P], QE[:, i, k * P:(k + 1) * P], ident[:, :])
                                mm = pe.transpose(opP[i % 4][:, (2 + k) * P:(3 + k) * P], QK[:, i, C + k * P:C + (k + 1) * P], ident[:, :])
                            mm.then_inc(op_full, 1)
                        for i in range(NT):
                            u = NT + i
                            pe.wait_ge(lo_ready, 2 * NT * b + (u - 3))
                            pe.wait_ge(hy_ready, NT * b + (i + 1))
                            hy = HY[:, i, :, :].rearrange("p h d -> p (h d)")
                            for k in range(4):
                                mm = pe.transpose(opP[u % 4][:, k * P:(k + 1) * P], hy[:, k * P:(k + 1) * P], ident[:, :])
                            mm.then_inc(op_full, 1)

                        def op(g, j, o, lo, hi):
                            return STG[64 * (j % 2):64 * (j % 2) + R3, g, o, j // 2, lo:hi]

                        def inner(g, j):
                            if g == 0:
                                pe.wait_ge(first_ready[j], b * SD + SD)
                            elif j == 0:
                                pe.wait_ge(stage_ready[g], b * SD * G + SD * G)
                            for r, tiles in enumerate(REGIONS):
                                rc = 3 * (G * g + j) + r
                                pe.wait_ge(m_free, b * (3 * H) + (rc + 1))
                                at = 0
                                for i in tiles:
                                    mm = pe.matmul(mP[rc % 2][:, at:at + W[i]], op(g, j, 2, i * P, (i + 1) * P),
                                                   op(g, j, 3, 0, W[i]), start=True, stop=True)
                                    at += W[i]
                                mm.then_inc(m_full, 1)

                        def euclid(g, j):
                            for i in range(NT):
                                tc = NT * (G * g + j) + i
                                pe.wait_ge(comb_ready, b * (H * NT) + (tc + 1))
                                pe.matmul(SeP[tc % 2][:, 0:W[i]], op(g, j, 0, i * P, (i + 1) * P),
                                          op(g, j, 1, 0, W[i]), start=True, stop=False)
                                mm = pe.matmul(SeP[tc % 2][:, i * P:W[i]], identb[:, :], mask[:, :], start=False, stop=True)
                                mm.then_inc(se_full, 1)

                        def turn(g, j, i):
                            tc = NT * (G * g + j) + i
                            pe.wait_ge(p_ready, b * (H * NT) + (tc + 1))
                            pe.wait_ge(pt_ready, b * (H * NT) + (tc + 1))
                            for k in range(i + 1):
                                mm = pe.transpose(PTP[tc % 3][:, k * P:(k + 1) * P],
                                                  TT[:, g % 2, j, OFF[i] + k * P:OFF[i] + (k + 1) * P], ident[:, :])
                            mm.then_inc(pt_full, 1)

                        def product(g, j, i):
                            tc = NT * (G * g + j) + i
                            pe.wait_ge(pt_ready, b * (H * NT) + (tc + 4))
                            if j == 0 and i == 0:
                                pe.wait_ge(y_ready, NG * b + (g + 1))
                                pe.wait_ge(vl_ready, NT * b + NT)
                            for k in range(i + 1):
                                blk = slice(OFF[i] + k * P, OFF[i] + (k + 1) * P)
                                pe.matmul(avP[:, i, j, :], PH[:, j % 2, blk], VH[:, k, G * g + j, :], start=(k == 0), stop=False)
                                pe.matmul(avP[:, i, j, :], PH[:, j % 2, blk], VL[:, k, G * g + j, :], start=False, stop=False)
                                mm = pe.matmul(avP[:, i, j, :], PL[:, j % 2, blk], VH[:, k, G * g + j, :], start=False, stop=(k == i))
                            mm.then_inc(av_tile, 1)

                        def outputs(g):
                            order = [(j, i) for j in range(G) for i in range(NT)]
                            for n, (j, i) in enumerate(order):
                                turn(g, j, i)
                                if n >= 2:
                                    product(g, *order[n - 2])
                                if i == NT - 1 and g + 2 < NG:
                                    inner(g + 2, j)
                                if i == NT - 1 and j == G // 2 and g + 1 < NG:
                                    euclid(g + 1, 0)
                            product(g, *order[-2])
                            product(g, *order[-1])

                        for j in range(G):
                            inner(0, j)
                        for j in range(G):
                            euclid(0, j)
                            inner(1, j)
                        for g in range(NG):
                            outputs(g)
                            if g + 1 < NG:
                                for j in range(1, G):
                                    euclid(g + 1, j)

                        pe.wait_ge(y_ready, NG * b + (NG + 1))
                        for h in range(2):
                            for k in range(CH):
                                for i in (2 * h, 2 * h + 1):
                                    at = k * 2 * P + (i % 2) * P
                                    mm = pe.transpose(PTP[h][:, at:at + P], Y[:, i, k * P:(k + 1) * P], ident[:, :])
                            mm.then_inc(yt_full, 1)
                        for i in range(NT):
                            pe.wait_ge(yt_ready, 2 * b + (i // 2 + 1))
                            for k in range(CH):
                                mm = pe.matmul(opP[i][:, 0:C], YT[:, k, i * P:(i + 1) * P], WOT[:, k, :], start=(k == 0), stop=(k == CH - 1))
                            mm.then_inc(out_full, 1)

                @block.vector
                def _(dve):
                    dve.sem_inc(x_used, 1)
                    dve.sem_inc(m_free, 2)
                    dve.sem_inc(comb_ready, 2)
                    dve.sem_inc(pt_ready, 3)
                    dve.sem_inc(se_full, SE)
                    dve.sem_inc(y_ready, 1)
                    steps = NT * 2 + 2 + 7 + 6 + 8 + NT // 2 + NT + NG * 2 + NT * 3 + 2
                    with dve.Fori(0, B) as b:
                        step = [0]

                        def chain(ins):
                            step[0] += 1
                            ins.then_inc(dve_a, 1)
                            dve.wait_ge(dve_a, steps * b + step[0])

                        SS, SQ0, A, MK, G1, R2, Q, F2 = (st[:, k, :] for k in (0, 1, 2, 3, 4, 5, 6, 7))

                        def reduces(i):
                            dve.wait_ge(sq_ready, NT * b + (i + 1))
                            chain(dve.tensor_reduce(SS[:, 2 * H * i:2 * H * (i + 1)], SQ[:, i, :, :], AX.X, ALU.add))
                            chain(dve.tensor_copy(SQ0[:, 2 * H * i:2 * H * (i + 1)], SQ[:, i, :, 0]))

                        for i in range(NT):
                            dve.wait_ge(pq_full, NT * b + (i + 1))
                            dve.tensor_tensor(QK[:, i, :], mP[i % 2][:, :], bias[:, 0:QKW], ALU.add).then_inc(qk_ready, 1)
                            dve.wait_ge(pv_full, NT * b + (i + 1))
                            if i >= 1:
                                dve.wait_ge(vl_ready, NT * b + i)
                            dve.tensor_tensor(V[:, :, 0:D], SeP[i % 2][:, 0:C].rearrange("p (h d) -> p h d", d=D),
                                              bias[:, QKW:QKW + C].rearrange("p (h d) -> p h d", d=D), ALU.add)
                            dve.tensor_tensor(AI[:, 0, i, :], SeP[i % 2][:, C:VAI], bias[:, QKW + C:WCOL], ALU.add).then_inc(ai_ready, 1)
                            if i >= 1:
                                reduces(i - 1)
                        al = st[:, 8, 0:NT * (H + 1)].rearrange("p (i h) -> p i h", i=NT)
                        dve.wait_ge(ea_ready, b + 1)
                        chain(dve.tensor_scalar(AI[:, 0, :, :], AI[:, 1, :, :], 1.0, None, ALU.add))
                        chain(dve.reciprocal(al, AI[:, 0, :, :]))
                        dve.tensor_scalar(st[:, 9, 0:NT * H].rearrange("p (i h) -> p i h", i=NT), al[:, :, 0:H],
                                          0.25, -0.25, ALU.mult, ALU.add).then_inc(qs_ready, 1)
                        reduces(NT - 1)
                        chain(dve.tensor_scalar(A, SS, 1e-24, None, ALU.max))
                        chain(dve.reciprocal(G1, A))
                        chain(dve.tensor_scalar(R2, G1, s2[:, 0:1], None, ALU.mult))
                        chain(dve.scalar_tensor_tensor(A, SQ0, -2.0, SS, ALU.mult, ALU.add))
                        chain(dve.tensor_tensor(G1, A, R2, ALU.mult))
                        chain(dve.tensor_scalar(MK, G1, 1e-8, None, ALU.max))
                        chain(dve.tensor_scalar(Q, MK, SINH[7], None, ALU.mult))
                        for k in range(6, 0, -1):
                            chain(dve.scalar_tensor_tensor(Q, Q, SINH[k], MK, ALU.add, ALU.mult))
                        chain(dve.tensor_scalar(G1, Q, 1.0, None, ALU.add))
                        chain(dve.tensor_tensor(A, G1, G1, ALU.mult))
                        chain(dve.tensor_tensor(F2, A, R2, ALU.mult))
                        chain(dve.tensor_tensor(Q, SS, SQ0, ALU.subtract))
                        chain(dve.tensor_tensor(A, Q, F2, ALU.mult))
                        by_tile = lambda w: w.rearrange("p (i h) -> p i h", i=NT)
                        chain(dve.tensor_copy(stat[:, :, 0:2 * H], by_tile(F2)))
                        chain(dve.tensor_scalar(stat[:, :, 2 * H:4 * H], by_tile(A), 1.0, None, ALU.add))
                        dve.tensor_tensor(stat[:, :, 4 * H:5 * H], al[:, :, 0:H],
                                          rcurv[:, :].unsqueeze(1).broadcast_to([P, NT, H]), ALU.mult).then_inc(stat_ready, 1)
                        chain(dve.tensor_scalar(spk[:, :], al[:, :, H], thr[:, 0:1], None, ALU.is_gt))

                        def times(i):
                            chain(dve.tensor_scalar(HY[:, i, 0:H, 0], root[:, i, 2 * H:3 * H], -1.0, None, ALU.mult))
                            dve.tensor_copy(HY[:, i, H:2 * H, 0], root[:, i, 3 * H:4 * H]).then_inc(hy_ready, 1)

                        def low(u):
                            r, i = u // NT, u % NT
                            dve.wait_ge(hi_ready, 2 * NT * b + (u + 1))
                            dve.tensor_tensor(LO[:, 4 * r:4 * r + 4, i * P:(i + 1) * P],
                                              opP[u % 4][:, :].rearrange("p (k t) -> p k t", k=4),
                                              HI[:, 4 * r:4 * r + 4, i * P:(i + 1) * P], ALU.subtract).then_inc(lo_ready, 1)

                        dve.wait_ge(root_ready, b + 1)
                        for i in range(NT // 2):
                            chain(dve.tensor_tensor(HY[:, i, :, :], QK[:, i, :].rearrange("p (h d) -> p h d", d=D),
                                                    root[:, i, 0:2 * H].unsqueeze(2).broadcast_to([P, 2 * H, D]), ALU.mult))
                            times(i)
                        for u in range(NT):
                            low(u)
                            if u < NT // 2:
                                i = NT // 2 + u
                                dve.wait_ge(space_ready, (NT // 2) * b + (u + 1))
                                times(i)
                        for u in range(NT, 2 * NT):
                            low(u)

                        def clamps(g, j):
                            for r, tiles in enumerate(REGIONS):
                                rc = 3 * (G * g + j) + r
                                w = sum(W[i] for i in tiles)
                                dve.wait_ge(m_full, b * (3 * H) + (rc + 1))
                                if r == 0 and j == 0 and g >= 2:
                                    dve.wait_ge(sum_ready, b * SUM + sum_count(g - 2, G - 1))
                                at = OFF[tiles[0]]
                                dve.tensor_scalar(MC[:, g % 2, j, at:at + w], mP[rc % 2][:, 0:w], -1.0, 1.0 + 1e-6,
                                                  ALU.mult, ALU.max).then_inc(m_free, 1)

                        def combines(g, j):
                            dve.wait_ge(hyp_ready, b * H + (G * g + j + 1))
                            for i in range(NT):
                                tc = NT * (G * g + j) + i
                                dve.wait_ge(se_full, b * (H * NT) + (SE + tc + 1))
                                w = TT[:, g % 2, j, OFF[i]:OFF[i] + W[i]]
                                dve.sem_inc(passed, 1)
                                dve.tensor_tensor_reduce(out=w, in0=SeP[tc % 2][:, 0:W[i]], in1=w, scale=1.0, scalar=3e38,
                                                         op0=ALU.add, op1=ALU.min,
                                                         accum_out=mn[:, g % 2, j, i:i + 1]).then_inc(comb_ready, 1)

                        def copies(g, j):
                            for i in range(NT):
                                tc = NT * (G * g + j) + i
                                dve.wait_ge(pt_full, b * (H * NT) + (tc + 1))
                                if tc >= 2 * NT:
                                    dve.wait_ge(av_tile, b * (H * NT) + (tc - 2 * NT + 1))
                                seg = slice(OFF[i], OFF[i] + W[i])
                                if g < NG - 1:
                                    dve.tensor_copy(PH[:, j % 2, seg], PTP[tc % 3][:, 0:W[i]]).then_inc(ph_ready, 1)
                                    dve.wait_ge(ph_ready, b * ((H - G) * NT) + (tc + 1))
                                else:
                                    dve.wait_ge(aph_ready, b * (G * NT) + (NT * j + i + 1))
                                dve.tensor_tensor(PL[:, j % 2, seg], PTP[tc % 3][:, 0:W[i]], PH[:, j % 2, seg],
                                                  ALU.subtract).then_inc(pt_ready, 1)

                        def normalise(g):
                            dve.wait_ge(av_tile, b * (H * NT) + NT * G * (g + 1))
                            chain(dve.reciprocal(rin[:, :, :], avP[:, :, :, D]))
                            chain(dve.tensor_tensor(rin[:, :, :], rin[:, :, :],
                                                    spk[:, :].unsqueeze(2).broadcast_to([P, NT, G]), ALU.mult))
                            dve.tensor_tensor(Y[:, :, G * g * D:G * (g + 1) * D].rearrange("p i (j d) -> p i j d", d=D),
                                              avP[:, :, :, 0:D], rin[:, :, :].unsqueeze(3).broadcast_to([P, NT, G, D]),
                                              ALU.mult).then_inc(y_ready, 1)

                        def dve_squares(g):
                            for j in range(G // 2, G):
                                dve.wait_ge(m_free, b * (3 * H) + (2 + 3 * (G * g + j + 1)))
                                dve.tensor_tensor(TT[:, g % 2, j, :], MC[:, g % 2, j, :], MC[:, g % 2, j, :],
                                                  ALU.mult).then_inc(dsq_ready, 1)

                        for j in range(G):
                            clamps(0, j)
                        dve_squares(0)
                        for j in range(G // 2):
                            dve.wait_ge(rt_ready, H * b + (j + 1))
                            dve.tensor_tensor(TT[:, 0, j, :], MC[:, 0, j, :], TT[:, 0, j, :], ALU.add).then_inc(dsum_ready, 1)
                        for j in range(G):
                            combines(0, j)
                            clamps(1, j)
                        for g in range(NG):
                            for j in range(G):
                                copies(g, j)
                                if g + 2 < NG:
                                    clamps(g + 2, j)
                                if j == G // 2 and g + 1 < NG:
                                    combines(g + 1, 0)
                            normalise(g)
                            if g + 1 < NG:
                                for j in range(1, G):
                                    combines(g + 1, j)

                        for i in range(NT):
                            dve.wait_ge(out_full, NT * b + (i + 1))
                            chain(dve.tensor_tensor(z[:, i, :], opP[i][:, 0:C], XI[:, i, :], ALU.add))
                            if i == NT - 1:
                                dve.sem_inc(x_used, 1)
                            chain(dve.tensor_tensor(z[:, i, :], z[:, i, :], bout[:, :], ALU.add))
                            chain(dve.bn_stats(bst[:, i, :], z[:, i, :]))
                            dve.sem_inc(passed, 1)
                            dve.bn_aggr(mv[:, i, :], bst[:, i, :]).then_inc(var_ready, 1)
                        dve.wait_ge(var_ready, NT * b + NT)
                        dve.wait_ge(sd_ready, b + 1)
                        chain(dve.reciprocal(sd[:, 1, :], sd[:, 0, :]))
                        for i in range(NT):
                            ins = dve.tensor_scalar(X[:, bass.ds(NT * b + i, 1), :].rearrange("p a c -> p (a c)"), z[:, i, :],
                                                    mv[:, i, 0:1], sd[:, 1, i:i + 1], ALU.subtract, ALU.mult)
                            if i == NT - 1:
                                chain(ins)
                        assert step[0] == steps, step[0]

        W1S = sb(top, "W1S", [P, E, CH, F])
        LG = sb(top, "LG", [P, N, E])
        w1_loaded = sem("w1_loaded")
        with ExitStack() as ctx:
            WQ = sb(ctx, "WQ", [P, CH, 3 * C])
            WO = sb(ctx, "WO", [P, CH, C])
            WG = sb(ctx, "WG", [P, CH, E])
            lng = sb(ctx, "lng", [P, 4, C])
            hT = sb(ctx, "hT", [P, CH, T])
            VH = sb(ctx, "VHb", [P, NT, H, D + 1], F16)
            VL = sb(ctx, "VLb", [P, NT, H, D + 1], F16)
            HI = sb(ctx, "HIb", [P, 2 * CH, T], F16)
            LO = sb(ctx, "LOb", [P, 2 * CH, T], F16)
            STG = sb(ctx, "STGb", [P, 2, 2, 2, T], F16)
            RING = 8
            PR = sb(ctx, "PR", [P, RING, T])
            PH = sb(ctx, "PHb", [P, RING, T], F16)
            PL = sb(ctx, "PLb", [P, RING, T], F16)
            nm = sb(ctx, "nm", [P, RING])
            Y = sb(ctx, "Yb", [P, NT, C])
            rin = sb(ctx, "rinb", [P, NT, G])
            RS = sb(ctx, "RS", [P, NT, C])
            bst = sb(ctx, "bstb", [P, NT, 6])
            mv = sb(ctx, "mvb", [P, NT, 2])
            sd = sb(ctx, "sdb", [P, 2, NT])
            R2 = NT * C // T
            XN, HB, X2 = (PR[:, R2 * k:R2 * (k + 1), :].rearrange("p r t -> p (r t)").rearrange("p (i c) -> p i c", c=C)
                          for k in range(3))
            YT = PR[:, 3 * R2:3 * R2 + CH, :]
            sP = [ctx.enter_context(nc.psum_tensor(f"sP{i}", [P, 512], F32)) for i in range(4)]
            PTP = [ctx.enter_context(nc.psum_tensor(f"PTPb{i}", [P, 512], F32)) for i in range(2)] + [mis]
            avP = ctx.enter_context(nc.psum_tensor("avPb", [P, NT, G, D + 1], F32))

            b_loaded = sem("b_loaded")
            v_ones = sem("v_ones")
            zeroed = sem("zeroed")
            stored_x = sem("stored_x")
            var1 = sem("var1")
            sd1 = sem("sd1")
            n1_ready = sem("n1_ready")
            h_ready = sem("h_ready")
            hd_ready = sem("hd_ready")
            g1_ready = sem("g1_ready")
            bht_full = sem("bht_full")
            bht_ready = sem("bht_ready")
            byt_full = sem("byt_full")
            byt_ready = sem("byt_ready")
            bo_full = sem("bo_full")
            bmt_full = sem("bmt_full")
            blg_full = sem("blg_full")
            pr_full = sem("pr_full")
            bhi = sem("bhi")
            blo = sem("blo")
            v_ready = sem("v_ready")
            bstage = [[sem(f"bstage{i}_{j}") for j in range(G)] for i in range(2)]
            s_full = sem("s_full")
            nm_ready = sem("nm_ready")
            bp_ready = sem("bp_ready")
            bpt_full = sem("bpt_full")
            bph_ready = sem("bph_ready")
            bpl_ready = sem("bpl_ready")
            bvh_ready = sem("bvh_ready")
            bav = sem("bav")
            by_ready = sem("by_ready")
            x2_ready = sem("x2_ready")
            rs_ready = sem("rs_ready")
            var2 = sem("var2")
            sd2 = sem("sd2")
            n2_ready = sem("n2_ready")
            g2_ready = sem("g2_ready")
            m_ready = sem("m_ready")
            md_ready = sem("md_ready")
            bmt_ready = sem("bmt_ready")
            kept = sem("kept")
            lg_ready = sem("lg_ready")
            dve_b = sem("dve_b")
            TC = H * NT
            AHEAD = 3
            BEHIND = 2
            BD = 16 * 5

            HN = NT // 2

            with nc.Block() as block:
                @block.sync
                def _(sp):
                    for n, name in enumerate(["Wq", "Wk", "Wv"]):
                        sp.dma_start(WQ[:, :, n * C:(n + 1) * C],
                                     a["L0_ffn_" + name].rearrange("(k p) c -> p k c", p=P)).then_inc(b_loaded, 16)
                    sp.dma_start(WO[:, :, :], a["L0_ffn_Wo"].rearrange("(k p) c -> p k c", p=P)).then_inc(b_loaded, 16)
                    sp.dma_start(WG[:, :, :], a["L0_ffn_Wg"].rearrange("(k p) c -> p k c", p=P)).then_inc(b_loaded, 16)
                    for n, name in enumerate(["ln1_g", "ln1_b", "ln2_g", "ln2_b"]):
                        sp.dma_start(lng[:, n, :], a["L0_ffn_" + name].partition_broadcast(P)).then_inc(b_loaded, 16)
                    sp.wait_ge(v_ones, 3)
                    sp.dma_start(xs_d.rearrange("s p c -> p s c"), PR[:, RING - 1, 0:C].unsqueeze(1).broadcast_to([P, SLOTS, C])).then_inc(zeroed, 16)
                    for e in range(E):
                        sp.dma_start(W1S[:, e, :, :], a["L0_ffn_W1"][e].rearrange("(k p) f -> p k f", p=P)).then_inc(w1_loaded, 16)
                    sp.wait_ge(zeroed, 16)
                    with sp.Fori(0, B) as b:
                        sp.wait_ge(bhi, 4 * b + 4)
                        sp.wait_ge(blo, 4 * b + 4)
                        for g in range(NG):
                            slot, c = g % 2, g // 2
                            sp.wait_ge(s_full, b * TC + G * NT * (g + 1))
                            for j in range(G):
                                par, s = j % 2, j // 2
                                src = 16 * ((G * g + j) % HPC)
                                dst = 64 * par
                                sp.dma_start(STG[dst:dst + D, slot, :, s, :],
                                             HI[src:src + D, c:2 * CH:2, :]).then_inc(bstage[slot][j], 16)
                                for jj, planes in [(1, (HI, LO)), (2, (LO, HI))]:
                                    dst = 64 * par + D * jj
                                    for qk in range(2):
                                        sp.dma_start(STG[dst:dst + D, slot, qk, s, :],
                                                     planes[qk][src:src + D, 2 * qk + c, :]).then_inc(bstage[slot][j], 16)
                        sp.wait_ge(rs_ready, NT * b + NT)
                        sp.dma_start(x2_d[bass.ds(b, 1)].rearrange("a p t c -> (a p) t c"), RS[:, :, :]).then_inc(stored_x, 16)

                @block.gpsimd
                def _(pool):
                    pool.memset(VH[:, :, :, D], 1.0).then_inc(v_ones, 1)
                    pool.memset(VL[:, :, :, D], 0.0).then_inc(v_ones, 1)
                    pool.memset(PR[:, RING - 1, 0:C], 0.0).then_inc(v_ones, 1)
                    pool.wait_ge(b_loaded, 144)
                    with pool.Fori(0, B) as b:
                        for i in range(HN, NT):
                            n = HN * b + (i - HN + 1)
                            pool.wait_ge(n1_ready, n)
                            pool.tensor_tensor(XN[:, i, :], XN[:, i, :], lng[:, 0, :], ALU.mult).then_inc(g1_ready, 1)
                            pool.wait_ge(g1_ready, n)
                            pool.tensor_tensor(HB[:, i, :], XN[:, i, :], lng[:, 1, :], ALU.add).then_inc(h_ready, 1)
                        pool.wait_ge(stored_x, 16 * b + 16)
                        for i in range(NT):
                            pool.wait_ge(x2_ready, NT * b + (i + 1))
                            pool.tensor_tensor(RS[:, i, :], X2[:, i, :],
                                               X[:, bass.ds(NT * b + i, 1), :].rearrange("p a c -> p (a c)"), ALU.add).then_inc(rs_ready, 1)
                        for i in range(HN, NT):
                            n = HN * b + (i - HN + 1)
                            pool.wait_ge(n2_ready, n)
                            pool.tensor_tensor(XN[:, i, :], XN[:, i, :], lng[:, 2, :], ALU.mult).then_inc(g2_ready, 1)
                            pool.wait_ge(g2_ready, n)
                            pool.tensor_tensor(HB[:, i, :], XN[:, i, :], lng[:, 3, :], ALU.add).then_inc(m_ready, 1)

                @block.scalar
                def _(act):
                    with act.Fori(0, B) as b:
                        act.wait_ge(var1, NT * b + NT)
                        act.activation(sd[:, 0, :], mv[:, :, 1], ACT.Sqrt, bias=epsc[:, :]).then_inc(sd1, 1)

                        def turned(dst, h, full, ready):
                            act.wait_ge(full, 2 * b + (h + 1))
                            act.activation(dst[:, :, 2 * h * P:2 * (h + 1) * P],
                                           PTP[h][:, :].rearrange("p (k t) -> p k t", k=CH), ACT.Copy).then_inc(ready, 1)

                        for h in range(2):
                            turned(hT, h, bht_full, bht_ready)
                        for u in range(2 * CH):
                            act.wait_ge(pr_full, 6 * b + (u + 1))
                            act.activation(HI[:, u, :], sP[u % 4][:, :], ACT.Copy,
                                           scale=float(D) ** -0.5 if u < CH else 1.0).then_inc(bhi, 1)

                        for v in range(NT // 2):
                            act.wait_ge(pr_full, 6 * b + (2 * CH + v + 1))
                            for i in range(2):
                                ins = act.activation(VH[:, 2 * v + i, :, 0:D],
                                                     sP[v][:, i * C:(i + 1) * C].rearrange("p (h d) -> p h d", d=D), ACT.Copy)
                            ins.then_inc(bvh_ready, 1)

                        def exp(tc):
                            act.wait_ge(nm_ready, b * TC + (tc + 1))
                            act.wait_ge(bpt_full, b * TC + (tc + 1))
                            act.activation(PR[:, tc % RING, :], sP[tc % 4][:, :], ACT.Exp,
                                           bias=nm[:, tc % RING:tc % RING + 1]).then_inc(bp_ready, 1)

                        def copy(tc):
                            act.wait_ge(bpt_full, b * TC + (tc + 1 + RING))
                            act.wait_ge(bav, b * TC + (tc + 1))
                            act.activation(PH[:, tc % RING, :], PTP[tc % 3][:, :], ACT.Copy).then_inc(bph_ready, 1)

                        for tc in range(-AHEAD, TC):
                            if tc >= 0:
                                copy(tc)
                            if tc + AHEAD < TC:
                                exp(tc + AHEAD)
                        for h in range(2):
                            turned(YT, h, byt_full, byt_ready)
                        act.wait_ge(var2, NT * b + NT)
                        act.activation(sd[:, 0, :], mv[:, :, 1], ACT.Sqrt, bias=epsc[:, :]).then_inc(sd2, 1)
                        turned(YT, 0, bmt_full, bmt_ready)
                        act.wait_ge(rs_ready, NT * b + NT)
                        act.wait_ge(m_ready, HN * b + HN)
                        act.wait_ge(md_ready, HN * b + HN)
                        act.activation(X[:, bass.ds(NT * b, NT), :].rearrange("p a c -> p (a c)"),
                                       HB[:, :, :].rearrange("p i c -> p (i c)"), ACT.Copy).then_inc(kept, 1)
                        turned(YT, 1, bmt_full, bmt_ready)

                @block.tensor
                def _(pe):
                    pe.wait_ge(b_loaded, 144)
                    with pe.Fori(0, B) as b:
                        def turn_rows(src, h, full):
                            for k in range(CH):
                                for i in (2 * h, 2 * h + 1):
                                    at = k * 2 * P + (i % 2) * P
                                    mm = pe.transpose(PTP[h][:, at:at + P], src[:, i, k * P:(k + 1) * P], ident[:, :])
                            mm.then_inc(full, 1)

                        pe.wait_ge(hd_ready, HN * b + HN)
                        turn_rows(HB, 0, bht_full)
                        pe.wait_ge(h_ready, HN * b + HN)
                        turn_rows(HB, 1, bht_full)
                        pe.wait_ge(bht_ready, 2 * b + 2)
                        for u in range(2 * CH):
                            for k in range(CH):
                                mm = pe.matmul(sP[u % 4][:, :], WQ[:, k, u * P:(u + 1) * P], hT[:, k, :],
                                               start=(k == 0), stop=(k == CH - 1))
                            mm.then_inc(pr_full, 1)
                        for v in range(NT // 2):
                            pe.wait_ge(blo, 4 * b + (v + 1))
                            for i in (2 * v, 2 * v + 1):
                                for k in range(CH):
                                    mm = pe.matmul(sP[v][:, (i % 2) * C:(i % 2 + 1) * C], hT[:, k, i * P:(i + 1) * P],
                                                   WQ[:, k, 2 * C:3 * C], start=(k == 0), stop=(k == CH - 1))
                            mm.then_inc(pr_full, 1)
                        pe.wait_ge(v_ready, 2 * b + 2)
                        pe.wait_ge(blo, 4 * b + 4)

                        def score(tc):
                            g, j, i = tc // (G * NT), tc // NT % G, tc % NT
                            if i == 0:
                                pe.wait_ge(bstage[g % 2][j], b * (BD * NG // 2) + BD * (g // 2 + 1))
                            pe.wait_ge(bp_ready, b * TC + (tc + 1))
                            base = 64 * (j % 2)
                            pe.matmul(sP[tc % 4][:, :], STG[base:base + R3, g % 2, 0, j // 2, i * P:(i + 1) * P],
                                      STG[base:base + R3, g % 2, 1, j // 2, :], start=True, stop=True).then_inc(s_full, 1)

                        def turn(tc):
                            pe.wait_ge(bp_ready, b * TC + (tc + 1 + 4))
                            pe.wait_ge(bpl_ready, b * TC + (tc + 1))
                            for k in range(NT):
                                mm = pe.transpose(PTP[tc % 3][:, k * P:(k + 1) * P], PR[:, tc % RING, k * P:(k + 1) * P], ident[:, :])
                            mm.then_inc(bpt_full, 1)

                        def product(tc):
                            g, j, i = tc // (G * NT), tc // NT % G, tc % NT
                            pe.wait_ge(bpl_ready, b * TC + (tc + 4))
                            if j == 0 and i == 0:
                                pe.wait_ge(by_ready, NG * b + (g + 1))
                            for k in range(NT):
                                ph, pl = PH[:, tc % RING, k * P:(k + 1) * P], PL[:, tc % RING, k * P:(k + 1) * P]
                                vh, vl = VH[:, k, G * g + j, :], VL[:, k, G * g + j, :]
                                pe.matmul(avP[:, i, j, :], ph, vh, start=(k == 0), stop=False)
                                pe.matmul(avP[:, i, j, :], ph, vl, start=False, stop=False)
                                mm = pe.matmul(avP[:, i, j, :], pl, vh, start=False, stop=(k == NT - 1))
                            mm.then_inc(bav, 1)

                        for tc in range(-AHEAD, TC + BEHIND):
                            if tc + AHEAD < TC:
                                score(tc + AHEAD)
                            if 0 <= tc < TC:
                                turn(tc)
                            if tc >= BEHIND:
                                product(tc - BEHIND)

                        pe.wait_ge(by_ready, NG * b + (NG + 1))
                        for h in range(2):
                            turn_rows(Y, h, byt_full)
                        for i in range(NT):
                            pe.wait_ge(byt_ready, 2 * b + (i // 2 + 1))
                            for k in range(CH):
                                mm = pe.matmul(sP[i][:, 0:C], YT[:, k, i * P:(i + 1) * P], WO[:, k, :], start=(k == 0), stop=(k == CH - 1))
                            mm.then_inc(bo_full, 1)
                        pe.wait_ge(md_ready, HN * b + HN)
                        turn_rows(HB, 0, bmt_full)
                        pe.wait_ge(m_ready, HN * b + HN)
                        turn_rows(HB, 1, bmt_full)
                        pe.wait_ge(bmt_ready, 2 * b + 2)
                        for i in range(NT):
                            for k in range(CH):
                                mm = pe.matmul(mis[:, i * E:(i + 1) * E], YT[:, k, i * P:(i + 1) * P], WG[:, k, :],
                                               start=(k == 0), stop=(k == CH - 1))
                        mm.then_inc(blg_full, 1)

                @block.vector
                def _(dve):
                    dve.sem_inc(s_full, 2 * G * NT)
                    dve.sem_inc(bp_ready, 4)
                    dve.sem_inc(bpt_full, RING)
                    dve.sem_inc(bav, RING)
                    dve.sem_inc(bpl_ready, 3)
                    dve.sem_inc(by_ready, 1)
                    dve.sem_inc(stored_x, 16)
                    dve.wait_ge(v_ones, 3)
                    steps = 2 * (NT + 1 + 2 * HN) + NG
                    dve.wait_ge(b_loaded, 144)
                    with dve.Fori(0, B) as b:
                        step = [0]

                        def chain(ins):
                            step[0] += 1
                            ins.then_inc(dve_b, 1)
                            dve.wait_ge(dve_b, steps * b + step[0])

                        def stats(i, src, var):
                            chain(dve.bn_stats(bst[:, i, :], src))
                            dve.sem_inc(passed, 1)
                            dve.bn_aggr(mv[:, i, :], bst[:, i, :]).then_inc(var, 1)

                        def norm(rows, gain, var, root, done, own):
                            dve.wait_ge(var, NT * b + NT)
                            dve.wait_ge(root, b + 1)
                            chain(dve.reciprocal(sd[:, 1, :], sd[:, 0, :]))
                            for i in range(HN, NT):
                                dve.tensor_scalar(XN[:, i, :], rows(i), mv[:, i, 0:1], sd[:, 1, i:i + 1],
                                                  ALU.subtract, ALU.mult).then_inc(done, 1)
                            for i in range(HN):
                                chain(dve.tensor_scalar(XN[:, i, :], rows(i), mv[:, i, 0:1], sd[:, 1, i:i + 1],
                                                        ALU.subtract, ALU.mult))
                                chain(dve.tensor_tensor(XN[:, i, :], XN[:, i, :], lng[:, gain, :], ALU.mult))
                                dve.tensor_tensor(HB[:, i, :], XN[:, i, :], lng[:, gain + 1, :], ALU.add).then_inc(own, 1)

                        def x_row(i):
                            return X[:, bass.ds(NT * b + i, 1), :].rearrange("p a c -> p (a c)")

                        for i in range(NT):
                            stats(i, x_row(i), var1)
                        norm(x_row, 0, var1, sd1, n1_ready, hd_ready)
                        for u in range(2 * CH):
                            dve.wait_ge(bhi, 4 * b + (u + 1))
                            dve.scalar_tensor_tensor(LO[:, u, :], sP[u % 4][:, :], float(D) ** -0.5 if u < CH else 1.0,
                                                     HI[:, u, :], ALU.mult, ALU.subtract).then_inc(blo, 1)
                        for v in range(NT // 2):
                            dve.wait_ge(bvh_ready, 2 * b + (v + 1))
                            for i in range(2):
                                ins = dve.tensor_tensor(VL[:, 2 * v + i, :, 0:D],
                                                        sP[v][:, i * C:(i + 1) * C].rearrange("p (h d) -> p h d", d=D),
                                                        VH[:, 2 * v + i, :, 0:D], ALU.subtract)
                            ins.then_inc(v_ready, 1)

                        def maximum(tc):
                            dve.wait_ge(s_full, b * TC + (2 * G * NT + tc + 1))
                            dve.tensor_reduce(nm[:, tc % RING:tc % RING + 1], sP[tc % 4][:, :], AX.X, ALU.max,
                                              negate=True).then_inc(nm_ready, 1)

                        def low(tc):
                            dve.wait_ge(bph_ready, b * TC + (tc + 1))
                            dve.tensor_tensor(PL[:, tc % RING, :], PTP[tc % 3][:, :], PH[:, tc % RING, :],
                                              ALU.subtract).then_inc(bpl_ready, 1)

                        def normalise(g):
                            dve.wait_ge(bav, b * TC + (NT * G * (g + 1) + RING))
                            chain(dve.reciprocal(rin[:, :, :], avP[:, :, :, D]))
                            dve.tensor_tensor(Y[:, :, G * g * D:G * (g + 1) * D].rearrange("p i (j d) -> p i j d", d=D),
                                              avP[:, :, :, 0:D], rin[:, :, :].unsqueeze(3).broadcast_to([P, NT, G, D]),
                                              ALU.mult).then_inc(by_ready, 1)

                        for tc in range(-AHEAD, TC):
                            if tc + AHEAD < TC:
                                maximum(tc + AHEAD)
                            if tc >= 0:
                                low(tc)
                            if tc > BEHIND and (tc - BEHIND + 1) % (G * NT) == 0:
                                normalise((tc - BEHIND + 1) // (G * NT) - 1)
                        normalise(NG - 1)

                        for i in range(NT):
                            dve.wait_ge(bo_full, NT * b + (i + 1))
                            dve.tensor_tensor(X2[:, i, :], sP[i][:, 0:C], x_row(i), ALU.add).then_inc(x2_ready, 1)
                            dve.wait_ge(x2_ready, NT * b + (i + 1))
                            stats(i, X2[:, i, :], var2)
                        norm(lambda i: X2[:, i, :], 2, var2, sd2, n2_ready, md_ready)
                        dve.wait_ge(blg_full, b + 1)
                        dve.tensor_copy(LG[:, bass.ds(NT * b, NT), :].rearrange("p a e -> p (a e)"), mis[:, 0:NT * E]).then_inc(lg_ready, 1)
                        dve.wait_ge(lg_ready, b + 1)
                        assert step[0] == steps, step[0]
                    dve.wait_ge(stored_x, 16 + 16 * B)


        with ExitStack() as ctx:
            W2S = sb(ctx, "W2S", [P, E, FC, C])
            HS = sb(ctx, "HS", [P, 2, F])
            HT = sb(ctx, "HT", [P, 2, F])
            B1S = sb(ctx, "B1S", [3, E * F], BF16)
            B2S = sb(ctx, "B2S", [3, E * C], BF16)
            tri = sb(ctx, "tri", [P, P], BF16)
            ones = sb(ctx, "ones", [P, P], BF16)
            selb = sb(ctx, "selb", [P, N * E], BF16)
            keys = sb(ctx, "keys", [P, N])
            tilen = sb(ctx, "tilen", [P, SLOTS])
            intsc = sb(ctx, "intsc", [P, N + SLOTS], mybir.dt.int32)
            idx = sb(ctx, "idx", [P, 2, N], mybir.dt.uint32)
            expert = sb(ctx, "expert", [P, SLOTS], mybir.dt.int32)
            gate = sb(ctx, "gate", [P, 2, N])
            bst = sb(ctx, "bstc", [P, 6])
            mv = sb(ctx, "mvc", [P, 2, 2])
            sd = sb(ctx, "sdc", [P, 2, 2])
            hP = [ctx.enter_context(nc.psum_tensor(f"hP{i}", [P, F], F32)) for i in range(2)]
            hTP = ctx.enter_context(nc.psum_tensor("hTP", [P, F], F32))
            yP = ctx.enter_context(nc.psum_tensor("yP", [P, 512], F32))
            tmp = [HS[:, n // 4, (n % 4) * 256:(n % 4) * 256 + N * E].rearrange("p (n e) -> p n e", e=E) for n in range(8)]
            cmp_e = HT[:, 0, 0:E * N].rearrange("p (e n) -> p e n", e=E)
            cmp_s = HT[:, 1, 0:SLOTS * E].rearrange("p (s e) -> p s e", e=E)
            vec = [HT[:, 0, 512 + N * n:512 + N * n + N] for n in range(6)]
            ev = [HT[:, 0, 768 + E * n:768 + E * n + E] for n in range(6)]
            b32 = HT[:, 0, 832:832 + 80]
            bp = sb(ctx, "bp", [P, 3, 80], BF16)
            if N * C >= 20 * C:
                XR = X
            else:
                XR = sb(ctx, "XR", [P, 20, C])
            XS = XR[:, 0:2, :]
            XT = XR[:, 2:4, :].rearrange("p s (k t) -> p s k t", k=CH)
            YS = XR[:, 4:6, :]
            RG = 4
            Y1 = XR[:, 6:6 + RG, :]
            Y2 = XR[:, 10:10 + RG, :]
            XB = XR[:, 14:14 + RG, :]
            ZO = XR[:, 18:20, :]

            w2_loaded = sem("w2_loaded")
            cb_loaded = sem("cb_loaded")
            cb_moved = sem("cb_moved")
            cst = sem("cst")
            lg_off = sem("lg_off")
            lg_exp = sem("lg_exp")
            sel_ready = sem("sel_ready")
            rank_full = sem("rank_full")
            parts_ready = sem("parts_ready")
            idx_ready = sem("idx_ready")
            scattered = sem("scattered")
            xs_loaded = [sem(f"xs_loaded{i}") for i in range(2)]
            xt_full = sem("xt_full")
            xt_ready = sem("xt_ready")
            h_full = sem("h_full")
            h_ready2 = sem("h_ready2")
            ht_full = sem("ht_full")
            ht_ready = sem("ht_ready")
            y_full = sem("y_full")
            ys_ready = sem("ys_ready")
            ys_stored = [sem(f"ys_stored{i}") for i in range(2)]
            gathered = [sem(f"gathered{i}") for i in range(RG)]
            xb_loaded = [sem(f"xb_loaded{i}") for i in range(RG)]
            z_ready = sem("z_ready")
            var3 = sem("var3")
            sd3 = sem("sd3")
            o_ready = sem("o_ready")
            o_stored = [sem(f"o_stored{i}") for i in range(2)]
            dve_c = sem("dve_c")
            HALF = SLOTS // 2

            with nc.Block() as block:
                @block.sync
                def _(sp):
                    sp.dma_start(b32[:, 0:64], a["L0_ffn_b1"].rearrange("e f -> (e f)").rearrange("(p j) -> p j", p=P)).then_inc(cb_loaded, 16)
                    sp.dma_start(b32[:, 64:80], a["L0_ffn_b2"].rearrange("e f -> (e f)").rearrange("(p j) -> p j", p=P)).then_inc(cb_loaded, 16)
                    for e in range(E):
                        sp.dma_start(W2S[:, e, :, :], a["L0_ffn_W2"][e].rearrange("(k p) c -> p k c", p=P)).then_inc(w2_loaded, 16)
                    sp.wait_ge(parts_ready, 3)
                    for r in range(3):
                        sp.dma_start(B1S[r:r + 1, :], bp[:, r, 0:64]).then_inc(cb_moved, 16)
                        sp.dma_start(B2S[r:r + 1, :], bp[:, r, 64:80]).then_inc(cb_moved, 16)
                    sp.wait_ge(scattered, 16 * 2 * N)

                    def load(q, s):
                        sp.wait_ge(xt_full, 2 * q + (s + 1))
                        sp.dma_start(XS[:, s, :], xs_d[bass.ds(2 * q + s, 1)].rearrange("a p c -> (a p) c")).then_inc(xs_loaded[s], 16)

                    def store(q, s):
                        sp.wait_ge(ys_ready, 2 * q + (s + 2))
                        sp.dma_start(ys_d[bass.ds(2 * q + s, 1)].rearrange("a p c -> (a p) c"), YS[:, s, :]).then_inc(ys_stored[s], 16)

                    load(0, 0)
                    load(0, 1)
                    with sp.Fori(0, HALF - 1) as q:
                        for s in range(2):
                            load(q + 1, s)
                            store(q, s)
                    store(HALF - 1, 0)
                    store(HALF - 1, 1)
                    for n in range(N):
                        if n >= RG:
                            sp.wait_ge(z_ready, n - RG + 1)
                        sp.dma_start(XB[:, n % RG, :], x2_d[n // NT, :, n % NT, :]).then_inc(xb_loaded[n % RG], 16)
                        if n >= 2:
                            sp.wait_ge(o_ready, n - 1)
                            sp.dma_start(out_t[(n - 2) // NT, :, (n - 2) % NT, :], ZO[:, n % 2, :]).then_inc(o_stored[n % 2], 16)
                    for n in range(N - 2, N):
                        sp.wait_ge(o_ready, n + 1)
                        sp.dma_start(out_t[n // NT, :, n % NT, :], ZO[:, n % 2, :]).then_inc(o_stored[n % 2], 16)
                    for s in range(2):
                        sp.wait_ge(o_stored[s], 16 * N // 2)

                @block.gpsimd
                def _(pool):
                    pool.memset(tri[:, :], 1.0).then_inc(cst, 1)
                    pool.memset(ones[:, :], 1.0).then_inc(cst, 1)
                    pool.iota(intsc[:, 0:N], pattern=[[P, N]], base=0, channel_multiplier=0).then_inc(cst, 1)
                    pool.iota(intsc[:, N:N + SLOTS], pattern=[[1, SLOTS]], base=0, channel_multiplier=0).then_inc(cst, 1)
                    pool.wait_ge(cst, 4)
                    pool.affine_select(out=tri[:, :], in_=tri[:, :], compare_op=ALU.is_gt, fill=0.0,
                                       base=0, pattern=[[1, P]], channel_multiplier=-1).then_inc(cst, 1)
                    pool.tensor_copy(keys[:, :], intsc[:, 0:N]).then_inc(cst, 1)
                    pool.tensor_copy(tilen[:, :], intsc[:, N:N + SLOTS]).then_inc(cst, 1)
                    pool.wait_ge(idx_ready, 1)
                    for n in range(N):
                        for k in range(2):
                            pool.indirect_dma_start(out=xs_d.rearrange("s p c -> (s p) c"),
                                                    out_offset=bass.IndirectOffsetOnAxis(ap=idx[:, k, n:n + 1], axis=0),
                                                    in_=X[:, n, :], in_offset=None).then_inc(scattered, 16)
                    for s in range(2):
                        pool.wait_ge(ys_stored[s], 16 + 16 * HALF)
                    for n in range(N):
                        if n >= RG:
                            pool.wait_ge(z_ready, n - RG + 1)
                        for k, dst in enumerate((Y1, Y2)):
                            pool.indirect_dma_start(out=dst[:, n % RG, :], out_offset=None,
                                                    in_=ys_d.rearrange("s p c -> (s p) c"),
                                                    in_offset=bass.IndirectOffsetOnAxis(ap=idx[:, k, n:n + 1], axis=0)).then_inc(gathered[n % RG], 16)

                @block.scalar
                def _(act):
                    act.wait_ge(lg_off, 1)
                    act.activation(tmp[1], tmp[0], ACT.Exp).then_inc(lg_exp, 1)

                    def body(q, s):
                        j1 = 2 * q + (s + 1)
                        act.wait_ge(xt_full, j1 + 2)
                        act.activation(XT[:, s, :, :].rearrange("p k t -> p (k t)"), mis[:, 0:C], ACT.Copy).then_inc(xt_ready, 1)

                    def gelu(q, s):
                        j1 = 2 * q + (s + 1)
                        act.wait_ge(h_full, j1)
                        act.wait_ge(ht_full, 2 * j1)
                        act.activation(HS[:, s, :], hP[s][:, :], ACT.Gelu_apprx_tanh).then_inc(h_ready2, 1)

                    body(0, 0)
                    with act.Fori(0, HALF - 1) as q:
                        body(q, 1)
                        gelu(q, 0)
                        body(q + 1, 0)
                        gelu(q, 1)
                    body(HALF - 1, 1)
                    gelu(HALF - 1, 0)
                    gelu(HALF - 1, 1)
                    for n in range(N):
                        act.wait_ge(var3, n + 1)
                        act.activation(sd[:, n % 2, 0:1], mv[:, n % 2, 1:2], ACT.Sqrt, bias=epsc[:, :]).then_inc(sd3, 1)

                @block.tensor
                def _(pe):
                    pe.wait_ge(cst, 7)
                    pe.wait_ge(sel_ready, 1)
                    pe.matmul(hP[0][:, 0:N * E], tri[:, :], selb[:, :], start=True, stop=True)
                    pe.matmul(hP[1][:, 0:N * E], ones[:, :], selb[:, :], start=True, stop=True).then_inc(rank_full, 1)
                    pe.wait_ge(idx_ready, 1)
                    pe.wait_ge(cb_moved, 96)
                    pe.wait_ge(w1_loaded, 16 * E)
                    pe.wait_ge(w2_loaded, 16 * E)
                    w1f = W1S[:, :, :, :].rearrange("p e k f -> p (e k f)")
                    w2f = W2S[:, :, :, :].rearrange("p e k c -> p (e k c)")

                    def turn_x(q, s):
                        j1 = 2 * q + (s + 1)
                        pe.wait_ge(xs_loaded[s], 16 * q + 16)
                        pe.wait_ge(xt_ready, j1)
                        for k in range(CH):
                            mm = pe.transpose(mis[:, k * P:(k + 1) * P], XS[:, s, k * P:(k + 1) * P], ident[:, :])
                        mm.then_inc(xt_full, 1)

                    def hidden(q, s, half, e):
                        j1 = 2 * q + (s + 1)
                        if half == 0:
                            pe.wait_ge(xt_ready, j1 + 1)
                            pe.wait_ge(h_ready2, j1)
                        dst = hP[s][:, half * 512:(half + 1) * 512]
                        for k in range(CH):
                            pe.matmul(dst, XT[:, s, k, :], w1f[:, bass.ds(e * (CH * F) + (k * F + half * 512), 512)],
                                      start=(k == 0), stop=False)
                        mm = pe.matmul(dst, ones[0:3, :], B1S[:, bass.ds(e * F + half * 512, 512)], start=False, stop=True)
                        if half == 1:
                            mm.then_inc(h_full, 1)

                    def turn_h(q, s):
                        j1 = 2 * q + (s + 1)
                        pe.wait_ge(h_ready2, j1 + 2)
                        for half in range(2):
                            pe.wait_ge(ht_ready, 2 * j1 + (half - 1))
                            for k in range(FC // 2 * half, FC // 2 * (half + 1)):
                                mm = pe.transpose(hTP[:, k * P:(k + 1) * P], HS[:, s, k * P:(k + 1) * P], ident[:, :])
                            mm.then_inc(ht_full, 1)

                    def outputs(q, s, e):
                        j1 = 2 * q + (s + 1)
                        pe.wait_ge(ys_ready, j1)
                        for k in range(FC):
                            if k % (FC // 2) == 0:
                                pe.wait_ge(ht_ready, 2 * j1 + (1 + k // (FC // 2)))
                            pe.matmul(yP[:, 0:C], HT[:, s, k * P:(k + 1) * P], w2f[:, bass.ds(e * (FC * C) + k * C, C)],
                                      start=(k == 0), stop=False)
                        pe.matmul(yP[:, 0:C], ones[0:3, :], B2S[:, bass.ds(e * C, C)], start=False, stop=True).then_inc(y_full, 1)

                    def expert_of(j):
                        return pe.value_load(expert[0:1, bass.ds(j, 1)], min_val=0, max_val=E - 1)

                    def step(q, s, pq, ps):
                        e = expert_of(2 * q + s)
                        hidden(q, s, 0, e)
                        if pq is not None:
                            turn_h(pq, ps)
                        hidden(q, s, 1, e)
                        return e

                    turn_x(0, 0)
                    step(0, 0, None, None)
                    turn_x(0, 1)
                    with pe.Fori(0, HALF - 1) as q:
                        step(q, 1, q, 0)
                        turn_x(q + 1, 0)
                        outputs(q, 0, expert_of(2 * q))
                        step(q + 1, 0, q, 1)
                        turn_x(q + 1, 1)
                        outputs(q, 1, expert_of(2 * q + 1))
                    last = HALF - 1
                    step(last, 1, last, 0)
                    outputs(last, 0, expert_of(2 * last))
                    turn_h(last, 1)
                    outputs(last, 1, expert_of(2 * last + 1))

                @block.vector
                def _(dve):
                    step = [0]

                    def chain(ins):
                        step[0] += 1
                        ins.then_inc(dve_c, 1)
                        dve.wait_ge(dve_c, step[0])

                    dve.sem_inc(xt_full, 2)
                    dve.sem_inc(xt_ready, 1)
                    dve.sem_inc(h_ready2, 2)
                    dve.sem_inc(ht_full, 4)
                    dve.sem_inc(ht_ready, 2)
                    dve.sem_inc(ys_ready, 1)
                    dve.sem_inc(ys_stored[0], 16)
                    dve.sem_inc(ys_stored[1], 16)

                    def over_e(v):
                        return v.unsqueeze(2).broadcast_to([P, N, E])

                    dve.wait_ge(cb_loaded, 32)
                    rest = HT[:, 0, 912:992]
                    chain(dve.tensor_copy(bp[:, 0, :], b32))
                    dve.sem_inc(parts_ready, 1)
                    chain(dve.tensor_tensor(rest, b32, bp[:, 0, :], ALU.subtract))
                    chain(dve.tensor_copy(bp[:, 1, :], rest))
                    dve.sem_inc(parts_ready, 1)
                    chain(dve.tensor_tensor(rest, rest, bp[:, 1, :], ALU.subtract))
                    chain(dve.tensor_copy(bp[:, 2, :], rest))
                    dve.sem_inc(parts_ready, 1)

                    chain(dve.tensor_reduce(vec[0], LG[:, :, :], AX.X, ALU.max))
                    dve.tensor_tensor(tmp[0], LG[:, :, :], over_e(vec[0]), ALU.subtract).then_inc(lg_off, 1)
                    dve.wait_ge(lg_exp, 1)
                    chain(dve.tensor_reduce(vec[1], tmp[1], AX.X, ALU.add))
                    chain(dve.reciprocal(vec[2], vec[1]))
                    chain(dve.tensor_tensor(tmp[2], tmp[1], over_e(vec[2]), ALU.mult))

                    def prefix(src, bufs, n, at):
                        d, turn = 1, 0
                        while d < n:
                            dst = bufs[turn]
                            chain(dve.tensor_copy(at(dst, 0, d), at(src, 0, d)))
                            chain(dve.tensor_tensor(at(dst, d, n), at(src, d, n), at(src, 0, n - d), ALU.add))
                            src, turn, d = dst, 1 - turn, 2 * d
                        return src

                    probs, top_p = tmp[2], [vec[3], vec[4]]
                    first = [tmp[5], tmp[6]]
                    for k in range(2):
                        chain(dve.tensor_reduce(top_p[k], probs, AX.X, ALU.max))
                        chain(dve.tensor_tensor(tmp[0], probs, over_e(top_p[k]), ALU.is_equal))
                        count = prefix(tmp[0], [tmp[3], tmp[4]], E, lambda v, lo, hi: v[:, :, lo:hi])
                        chain(dve.scalar_tensor_tensor(first[k], count, 1.0, tmp[0], ALU.is_equal, ALU.mult))
                        if k == 0:
                            chain(dve.scalar_tensor_tensor(tmp[1], first[0], -2.0, probs, ALU.mult, ALU.add))
                            probs = tmp[1]
                    chain(dve.tensor_tensor(selb[:, :].rearrange("p (n e) -> p n e", e=E), first[0], first[1], ALU.add))
                    dve.sem_inc(sel_ready, 1)
                    chain(dve.tensor_tensor(vec[0], vec[3], vec[4], ALU.add))
                    chain(dve.reciprocal(vec[1], vec[0]))
                    for k in range(2):
                        chain(dve.tensor_tensor(gate[:, k, :], top_p[k], vec[1], ALU.mult))

                    dve.wait_ge(rank_full, 1)
                    dve.wait_ge(cst, 7)
                    tot = tmp[0]
                    chain(dve.tensor_copy(tot, hP[1][:, 0:N * E].rearrange("p (n e) -> p n e", e=E)))
                    inc = prefix(tot, [tmp[1], tmp[2]], N, lambda v, lo, hi: v[:, lo:hi, :])
                    chain(dve.tensor_copy(ev[0], inc[:, N - 1, :]))
                    chain(dve.tensor_tensor(cmp_e, ev[0].unsqueeze(2).broadcast_to([P, E, N]),
                                            keys[:, :].unsqueeze(1).broadcast_to([P, E, N]), ALU.is_gt))
                    chain(dve.tensor_reduce(ev[1], cmp_e, AX.X, ALU.add))
                    tinc = prefix(ev[1], [ev[2], ev[3]], E, lambda v, lo, hi: v[:, lo:hi])
                    chain(dve.tensor_tensor(ev[4], tinc, ev[1], ALU.subtract))
                    chain(dve.tensor_tensor(tmp[3], inc, tot, ALU.subtract))
                    chain(dve.tensor_tensor(tmp[4], hP[0][:, 0:N * E].rearrange("p (n e) -> p n e", e=E), tmp[3], ALU.add))
                    chain(dve.scalar_tensor_tensor(tmp[7], ev[4].unsqueeze(1).broadcast_to([P, N, E]), float(P), tmp[4],
                                                   ALU.mult, ALU.add))
                    for k in range(2):
                        chain(dve.tensor_tensor(tmp[3], first[k], tmp[7], ALU.mult))
                        chain(dve.tensor_reduce(vec[5], tmp[3], AX.X, ALU.add))
                        chain(dve.tensor_copy(idx[:, k, :], vec[5]))
                    chain(dve.tensor_tensor(cmp_s, tilen[:, :].unsqueeze(2).broadcast_to([P, SLOTS, E]),
                                            ev[4].unsqueeze(1).broadcast_to([P, SLOTS, E]), ALU.is_ge))
                    count = HT[:, 1, E * SLOTS:E * SLOTS + SLOTS]
                    chain(dve.tensor_reduce(count, cmp_s, AX.X, ALU.add))
                    chain(dve.tensor_scalar(expert[:, :], count, -1.0, None, ALU.add))
                    dve.sem_inc(idx_ready, 1)

                    def copies(q, s):
                        j1 = 2 * q + (s + 1)
                        for half in range(2):
                            dve.wait_ge(ht_full, 2 * j1 + (3 + half))
                            dve.tensor_copy(HT[:, s, half * 512:(half + 1) * 512], hTP[:, half * 512:(half + 1) * 512]).then_inc(ht_ready, 1)

                    def result(q, s):
                        j1 = 2 * q + (s + 1)
                        dve.wait_ge(y_full, j1)
                        dve.wait_ge(ys_stored[s], 16 * q + 16)
                        dve.tensor_copy(YS[:, s, :], yP[:, 0:C]).then_inc(ys_ready, 1)

                    with dve.Fori(0, HALF) as q:
                        for s in range(2):
                            copies(q, s)
                            result(q, s)

                    for n in range(N):
                        z = Y1[:, n % RG, :]
                        dve.wait_ge(gathered[n % RG], 32 * (n // RG + 1))
                        dve.wait_ge(xb_loaded[n % RG], 16 * (n // RG + 1))
                        chain(dve.scalar_tensor_tensor(XB[:, n % RG, :], z, gate[:, 0, n:n + 1], XB[:, n % RG, :], ALU.mult, ALU.add))
                        if n >= 2:
                            dve.wait_ge(o_stored[n % 2], 16 * (n // 2))
                        chain(dve.scalar_tensor_tensor(ZO[:, n % 2, :], Y2[:, n % RG, :], gate[:, 1, n:n + 1], XB[:, n % RG, :],
                                                       ALU.mult, ALU.add))
                        dve.sem_inc(z_ready, 1)
                        chain(dve.bn_stats(bst[:, :], ZO[:, n % 2, :]))
                        dve.bn_aggr(mv[:, n % 2, :], bst[:, :]).then_inc(var3, 1)
                        dve.wait_ge(var3, n + 1)
                        dve.wait_ge(sd3, n + 1)
                        chain(dve.reciprocal(sd[:, n % 2, 1:2], sd[:, n % 2, 0:1]))
                        dve.tensor_scalar(ZO[:, n % 2, :], ZO[:, n % 2, :], mv[:, n % 2, 0:1], sd[:, n % 2, 1:2],
                                          ALU.subtract, ALU.mult).then_inc(o_ready, 1)


def kernel(**inputs):
    import numpy as np
    import concourse.bacc as bacc
    from concourse.bass_utils import run_bass_kernel_spmd

    nc = bacc.Bacc("TRN2", target_bir_lowering=False, num_devices=1)
    arrays, args = {}, {}
    for name, value in inputs.items():
        v = np.ascontiguousarray(value)
        if v.ndim == 0:
            v = v.reshape(1)
        arrays[f"in_{name}"] = v
        args[name] = nc.dram_tensor(f"in_{name}", v.shape, mybir.dt.from_np(v.dtype), kind="ExternalInput").ap()
    shape = inputs["L0_attn_x"].shape
    out = nc.dram_tensor("out_x", shape, F32, kind="ExternalOutput").ap()
    build(nc, args, out)
    return run_bass_kernel_spmd(nc, [arrays], core_ids=[0]).results[0]["out_x"]
```
